# Optimizing a Trainium2 kernel written in Bass

```python
import numpy as np
import jax
import jax.numpy as jnp

def _softmax(x, axis=-1):
    return jax.nn.softmax(x, axis=axis)

def _gelu(x):
    return jax.nn.gelu(x, approximate=True)

def _silu(x):
    return jax.nn.silu(x)

def _sigmoid(x):
    return jax.nn.sigmoid(x)

def _layernorm(x, axis=-1, eps=1e-05):
    m = jnp.mean(x, axis=axis, keepdims=True)
    v = jnp.var(x, axis=axis, keepdims=True)
    return (x - m) / jnp.sqrt(v + eps)

def _scatter_add(tgt, idx, src, axis=0):
    return tgt.at[idx].add(src)

def _segment_sum(src, seg, n):
    return jax.ops.segment_sum(src, seg, n)
kernel_name = 'mk_sandwich_d1_jaxref_r8_baf5f8'

def setup_inputs(seed: int=0):
    np.random.seed(seed)
    _w = jnp.asarray

    def _L0_attn_setup():
        import math
        import jax, jax.numpy as jnp
        import numpy as np
        EPS = 1e-06
        NB_FEATURES = 32
        NUM_HEADS = 16

        def fwht(x):
            shape = x.shape
            P = shape[-1]
            h = 1
            while h < P:
                x = x.reshape(shape[:-1] + (-1, 2 * h))
                a, b = (x[..., :h], x[..., h:])
                x = jnp.concatenate([a + b, a - b], axis=-1).reshape(shape)
                h *= 2
            return x

        def apply_rope(q, k):
            C, H, L, D = q.shape
            dtype = q.dtype
            freqs = 10000.0 ** (-jnp.arange(0, D, 2, dtype=dtype) / D)
            pos = jnp.arange(L - 1, dtype=dtype)[:, None]
            ang = pos * freqs
            cos, sin = (jnp.cos(ang), jnp.sin(ang))

            def rot(t):
                ts = t[..., 1:, :]
                t1, t2 = (ts[..., 0::2], ts[..., 1::2])
                re = t1 * cos - t2 * sin
                im = t1 * sin + t2 * cos
                rs = jnp.stack([re, im], axis=-1).reshape(ts.shape)
                return jnp.concatenate([t[..., :1, :], rs], axis=-2)
            return (rot(q), rot(k))

        def sorf_phi(x, signs, scales, m):
            C, H, L, D = x.shape
            R, P = (signs.shape[1], signs.shape[-1])
            x_p = x if D == P else jnp.pad(x, ((0, 0), (0, 0), (0, 0), (0, P - D)))
            inv = 1.0 / math.sqrt(P)
            s1 = signs[None, :, :, 0, None, :]
            s2 = signs[None, :, :, 1, None, :]
            s3 = signs[None, :, :, 2, None, :]
            g = (scales * inv)[None, :, :, None, :]
            t = fwht(x_p[:, :, None, :, :] * s1) * inv
            t = fwht(t * s2) * inv
            t = fwht(t * s3) * inv
            block = t * g
            phi = block.transpose(0, 1, 3, 2, 4).reshape(C, H, L, R * P)[..., :m]
            x_norm_sq = jnp.sum(x * x, axis=-1, keepdims=True) / 2.0
            return jnp.exp(phi - x_norm_sq) / math.sqrt(m)
        key = jax.random.key(seed)
        ks = jax.random.split(key, 5)
        C, L, E = (4, 512, 128)
        H, D = (NUM_HEADS, 128 // NUM_HEADS)
        P = 64
        R = 4
        x = jax.random.normal(ks[0], (C, L, E), dtype=jnp.float32)
        w_qkv = jax.random.normal(ks[1], (3 * E, E), dtype=jnp.float32) / math.sqrt(E)
        w_out = jax.random.normal(ks[2], (E, E), dtype=jnp.float32) / math.sqrt(E)
        sorf_signs = (2.0 * jax.random.randint(ks[3], (H, R, 3, P), 0, 2) - 1.0).astype(jnp.float32)
        sorf_scales = jax.random.normal(ks[4], (H, R, P), dtype=jnp.float32)
        return {'x': x, 'w_qkv': w_qkv, 'w_out': w_out, 'sorf_signs': sorf_signs, 'sorf_scales': sorf_scales}
    _L0_attn_in = _L0_attn_setup()

    def _L0_ffn_setup():
        import jax, jax.numpy as jnp
        import numpy as np
        D, H, O, E, TOPK = (128, 512, 128, 8, 2)
        B, L = (2, 256)
        ROUTE_SCALE = 1.0
        key = jax.random.key(seed)
        ks = jax.random.split(key, 7)
        gb = float(np.sqrt(6.0 / (E + D)))
        return {'x': jax.random.normal(ks[0], (B, L, D), dtype=jnp.float32), 'gate_w': jax.random.uniform(ks[1], (E, D), jnp.float32, -gb, gb), 'gate_b': jnp.zeros((E,), jnp.float32), 'w1': jax.random.normal(ks[2], (E, D, H), jnp.float32) * 0.02, 'b1': jnp.zeros((E, H), jnp.float32), 'w2': jax.random.normal(ks[3], (E, H, O), jnp.float32) * 0.02, 'b2': jnp.zeros((E, O), jnp.float32)}
    _L0_ffn_in = _L0_ffn_setup()
    _d = {'L0_attn_x': _L0_attn_in['x'], 'L0_attn_w_qkv': _L0_attn_in['w_qkv'], 'L0_attn_w_out': _L0_attn_in['w_out'], 'L0_attn_sorf_signs': _L0_attn_in['sorf_signs'], 'L0_attn_sorf_scales': _L0_attn_in['sorf_scales'], 'L0_ffn_gate_w': _L0_ffn_in['gate_w'], 'L0_ffn_gate_b': _L0_ffn_in['gate_b'], 'L0_ffn_w1': _L0_ffn_in['w1'], 'L0_ffn_b1': _L0_ffn_in['b1'], 'L0_ffn_w2': _L0_ffn_in['w2'], 'L0_ffn_b2': _L0_ffn_in['b2']}
    _x0 = _d['L0_attn_x']
    _d['L0_attn_x'] = jax.random.normal(jax.random.fold_in(jax.random.key(seed), 1), (4, 1024, 128), dtype=_x0.dtype)
    del _x0
    return _d

def reference(L0_attn_x, L0_attn_w_qkv, L0_attn_w_out, L0_attn_sorf_signs, L0_attn_sorf_scales, L0_ffn_gate_w, L0_ffn_gate_b, L0_ffn_w1, L0_ffn_b1, L0_ffn_w2, L0_ffn_b2):

    def _L0_attn_ref(x, w_qkv, w_out, sorf_signs, sorf_scales):
        import math
        import jax, jax.numpy as jnp
        import numpy as np
        EPS = 1e-06
        NB_FEATURES = 32
        NUM_HEADS = 16

        def fwht(x):
            shape = x.shape
            P = shape[-1]
            h = 1
            while h < P:
                x = x.reshape(shape[:-1] + (-1, 2 * h))
                a, b = (x[..., :h], x[..., h:])
                x = jnp.concatenate([a + b, a - b], axis=-1).reshape(shape)
                h *= 2
            return x

        def apply_rope(q, k):
            C, H, L, D = q.shape
            dtype = q.dtype
            freqs = 10000.0 ** (-jnp.arange(0, D, 2, dtype=dtype) / D)
            pos = jnp.arange(L - 1, dtype=dtype)[:, None]
            ang = pos * freqs
            cos, sin = (jnp.cos(ang), jnp.sin(ang))

            def rot(t):
                ts = t[..., 1:, :]
                t1, t2 = (ts[..., 0::2], ts[..., 1::2])
                re = t1 * cos - t2 * sin
                im = t1 * sin + t2 * cos
                rs = jnp.stack([re, im], axis=-1).reshape(ts.shape)
                return jnp.concatenate([t[..., :1, :], rs], axis=-2)
            return (rot(q), rot(k))

        def sorf_phi(x, signs, scales, m):
            C, H, L, D = x.shape
            R, P = (signs.shape[1], signs.shape[-1])
            x_p = x if D == P else jnp.pad(x, ((0, 0), (0, 0), (0, 0), (0, P - D)))
            inv = 1.0 / math.sqrt(P)
            s1 = signs[None, :, :, 0, None, :]
            s2 = signs[None, :, :, 1, None, :]
            s3 = signs[None, :, :, 2, None, :]
            g = (scales * inv)[None, :, :, None, :]
            t = fwht(x_p[:, :, None, :, :] * s1) * inv
            t = fwht(t * s2) * inv
            t = fwht(t * s3) * inv
            block = t * g
            phi = block.transpose(0, 1, 3, 2, 4).reshape(C, H, L, R * P)[..., :m]
            x_norm_sq = jnp.sum(x * x, axis=-1, keepdims=True) / 2.0
            return jnp.exp(phi - x_norm_sq) / math.sqrt(m)
        C, L, E = x.shape
        H = NUM_HEADS
        D = E // H
        qkv = x @ w_qkv.T
        q, k, v = jnp.split(qkv, 3, axis=-1)
        to_heads = lambda t: t.reshape(C, L, H, D).transpose(0, 2, 1, 3)
        q, k, v = (to_heads(q), to_heads(k), to_heads(v))
        q, k = apply_rope(q, k)
        q_phi = sorf_phi(q, sorf_signs, sorf_scales, NB_FEATURES)
        k_phi = sorf_phi(k, sorf_signs, sorf_scales, NB_FEATURES)
        S = jnp.einsum('chlm,chld->chmd', k_phi, v)
        sum_k = jnp.sum(k_phi, axis=2)
        numer = jnp.einsum('chlm,chmd->chld', q_phi, S)
        denom = jnp.maximum(jnp.einsum('chlm,chm->chl', q_phi, sum_k), EPS)
        out_heads = numer / denom[..., None]
        out = out_heads.transpose(0, 2, 1, 3).reshape(C, L, E)
        return out @ w_out.T

    def _L0_ffn_ref(x, gate_w, gate_b, w1, b1, w2, b2):
        import jax, jax.numpy as jnp
        import numpy as np
        D, H, O, E, TOPK = (128, 512, 128, 8, 2)
        B, L = (2, 256)
        ROUTE_SCALE = 1.0
        Bb, Ll, Dd = x.shape
        N = Bb * Ll
        x_flat = x.reshape(N, Dd)
        logits = x_flat @ gate_w.T + gate_b
        probs = jax.nn.softmax(logits * ROUTE_SCALE, axis=-1)
        topk_vals, topk_idx = jax.lax.top_k(probs, TOPK)
        dense_gate = jnp.zeros((N, E), probs.dtype).at[jnp.arange(N)[:, None], topk_idx].set(topk_vals)
        h = jax.nn.relu(jnp.einsum('nd,edh->neh', x_flat, w1) + b1)
        y = jnp.einsum('neh,eho->neo', h, w2) + b2
        out_flat = jnp.einsum('ne,neo->no', dense_gate, y)
        return out_flat.reshape(Bb, Ll, O)
    x = L0_attn_x
    x = x + _layernorm(_L0_attn_ref(_layernorm(x, axis=-1), L0_attn_w_qkv, L0_attn_w_out, L0_attn_sorf_signs, L0_attn_sorf_scales), axis=-1)
    x = x + _layernorm(_L0_ffn_ref(_layernorm(x, axis=-1), L0_ffn_gate_w, L0_ffn_gate_b, L0_ffn_w1, L0_ffn_b1, L0_ffn_w2, L0_ffn_b2), axis=-1)
    return x

_drawn_inputs = setup_inputs


def setup_inputs(seed=0):
    import zlib

    import numpy as np

    out = dict(_drawn_inputs(seed))
    spreads = {'L0_ffn_gate_b': (0.0, 0.1), 'L0_ffn_b1': (0.0, 0.1), 'L0_ffn_b2': (0.0, 0.1)}
    factors = {}
    for name, (base, spread) in spreads.items():
        noise = np.random.default_rng([zlib.crc32(name.encode()), seed]).standard_normal(out[name].shape)
        drawn = base * np.exp(spread * noise) if base else spread * noise
        out[name] = jnp.asarray(drawn.astype(out[name].dtype))
    for name, factor in factors.items():
        out[name] = (out[name] * factor).astype(out[name].dtype)
    return out
```

```python
from contextlib import ExitStack

import numpy as np

import concourse.bass as bass
from concourse import mybir

F32 = mybir.dt.float32
F16 = mybir.dt.float16
I32 = mybir.dt.int32
U32 = mybir.dt.uint32
ALU = mybir.AluOpType
ACT = mybir.ActivationFunctionType
AX = mybir.AxisListType

P = 128
NC, L, E = 4, 1024, 128
NT = L // P
CH = 4
NH, D, M = 16, 8, 32
HG = P // M
NG = NH // HG
W = HG * (D + 1)
SP_ = 64
HALF = D // 2
NX, HID = 8, 512
HC = HID // P
N = NC * L
TT = N // P
NB = (2 * N + NX * (P - 1)) // P
LN_EPS = 1e-5
DEN_EPS = 1e-6
UN = 4


def bc(ap, axis, n):
    shape = list(ap.shape)
    shape.insert(axis, n)
    return ap.unsqueeze(axis).to_broadcast(shape)


def sandwich_kernel(nc, x, wqk, wv, wo, sgn1, sgn2, sgn3, scl, gate_w, gate_b, w1, b1, w2, b2,
                    had, hadp, hmask, smask, cost, sint, out):
    x_d = x.rearrange("(t p) e -> p t e", p=P)
    out_d = out.rearrange("(t p) e -> p t e", p=P)
    xn_d = nc.dram_tensor("xn_rows", (N, 2 * E), F16, kind="Internal").ap()
    y_d = nc.dram_tensor("y_rows", (2 * N + UN * P, E), F32, kind="Internal").ap()
    xn_v = xn_d.rearrange("(t p) e -> p t e", p=P)
    y_v = y_d[0:2 * N, :].rearrange("(t p) e -> p t e", p=P)

    with ExitStack() as ctx:
        def sb(name, shape, dt=F32):
            return ctx.enter_context(nc.sbuf_tensor(name, shape, dt))

        def sem(name):
            return ctx.enter_context(nc.semaphore(name))

        bank = [ctx.enter_context(nc.psum_tensor(f"bank{i}", [P, 512], F32)) for i in range(8)]
        T_BANK, V_BANK, Z_BANK, S_BANK = bank[0], bank[1], bank[2], bank[3]
        QK_BANK, PHI_BANK = bank[4:6], bank[6:8]

        x_sb = sb("x_sb", [P, TT, E])
        x2_sb = x_sb
        logit = sb("logit", [P, TT, NX])
        eq_all = sb("eq_all", [P, TT, NH])
        ident = sb("ident", [P, P])
        ident16 = sb("ident16", [P, P], F16)
        wqk_sb, wv_sb, wo_sb = sb("wqk_sb", [P, 2 * E]), sb("wv_sb", [P, E]), sb("wo_sb", [P, E])
        gw_sb, gb_sb = sb("gw_sb", [P, NX]), sb("gb_sb", [P, NX])
        cos_sb, sin_sb = sb("cos_sb", [P, NT, E]), sb("sin_sb", [P, NT, 2 * E])
        sorf = sb("sorf", [P, NH, M])
        mhalf = sb("mhalf", [P, CH])
        carrier = sb("carrier", [P, 3])
        sm_sb = sb("sm_sb", [P, W])
        had_sb, hadp_sb = sb("had_sb", [SP_, SP_]), sb("hadp_sb", [SP_, P])
        s1_sb, s2_sb, s3_sb = sb("s1_sb", [SP_, P]), sb("s2_sb", [SP_, NH]), sb("s3_sb", [SP_, NH])
        scl_sb, hm_sb = sb("scl_sb", [P, NH * M]), sb("hm_sb", [P, NH])
        u1, u2, u3 = sb("u1", [SP_, P]), sb("u2", [SP_, P]), sb("u3", [SP_, P])
        t3 = sb("t3", [P, M])
        stage = sb("stage", [P, 2, HID])
        bst, mv = sb("bst", [P, 2, CH, 6]), sb("mv", [P, 2, CH, 2])
        vpe, rstd = sb("vpe", [P, 2, CH]), sb("rstd", [P, 2, CH])
        xn = sb("xn", [P, NT, E])
        xT = sb("xT", [P, L])
        rc, rs_ = sb("rc", [P, 2, 512]), sb("rs_", [P, 2, 512])
        rot = sb("rot", [P, NT, 2 * E])
        sq = sb("sq", [P, 2, 512])
        nrm = sb("nrm", [P, NT, 2, NH])
        ek = sb("ek", [P, NT, NH])
        v_sb = sb("v_sb", [P, NT, E])
        vext = sb("vext", [P, NT, NG * W])
        qT, kT = sb("qT", [P, L]), sb("kT", [P, L])
        kphi = sb("kphi", [P, NT, NH * M])
        qphi = sb("qphi", [P, NG, L])
        s_sb = sb("s_sb", [P, NG * W])
        den = sb("den", [P, 2, 4, 2, NH])
        att = sb("att", [P, NT, E])
        attT = sb("attT", [P, 2, 512])
        zst, zmv = sb("zst", [P, 2, CH, 6]), sb("zmv", [P, 2, CH, 2])
        zvp, zr = sb("zvp", [P, 2, CH]), sb("zr", [P, 2, CH])
        z_sb = sb("z_sb", [P, 2, CH, E])
        yst, ymv = sb("yst", [P, 2, CH, 6]), sb("ymv", [P, 2, CH, 2])
        yvp, yr = sb("yvp", [P, 2, CH]), sb("yr", [P, 2, CH])
        xn2 = sb("xn2", [P, 2, CH, E])
        hl = sb("hl", [P, 2, CH, 2 * E], F16)
        x2T = sb("x2T", [P, 2, 512])
        w1h, w1l = sb("w1h", [P, NX, HID], F16), sb("w1l", [P, NX, HID], F16)
        w2s = sb("w2s", [P, NX, HC, 2, E], F16)
        b1_sb, b1_all = sb("b1_sb", [64, P]), sb("b1_all", [P, P], F16)
        b1_h = sb("b1_h", [64, P], F16)
        b2_sb, b2_all = sb("b2_sb", [64, P]), sb("b2_all", [P, P], F16)
        b2_h = sb("b2_h", [64, P], F16)
        sel1 = sb("sel1", [P, NX, HC, P], F16)
        sel2 = sb("sel2", [P, NX, P], F16)

        rows = kphi[:, :, :].rearrange("p t f -> p (t f)")
        prob, expo, hit, cand, one1, one2, slot3, cum = (
            rows[:, TT * NX * i:TT * NX * (i + 1)] for i in range(8))
        prob2, tot, excl, cmp8 = (rows[:, TT * NX * i:TT * NX * (i + 1)] for i in range(8, 12))
        tokens = lambda a: a.rearrange("p (t e) -> p t e", e=NX)
        experts = lambda a: a.rearrange("p (e t) -> p e t", e=NX)
        red = sb("red", [P, 6, TT])
        gates = sb("gates", [P, 2, TT])
        mask16 = sb("mask16", [P, TT * NX], F16)
        tri16, ones16 = sb("tri16", [P, P], F16), sb("ones16", [P, P], F16)
        tie, steps128, fresh = sb("tie", [P, NX]), sb("steps128", [P, TT]), sb("fresh", [P, NX * TT])
        count, nblk, bend, ones8 = (sb(n, [P, NX]) for n in ("count", "nblk", "bend", "ones8"))
        slots, slot_i = sb("slots", [P, 2, TT]), sb("slot_i", [P, 2, TT], I32)
        blk_i, row_i = sb("blk_i", [P, 2, TT], I32), sb("row_i", [P, 2, TT], I32)
        blk, row = sb("blk", [P, 2 * TT]), sb("row", [P, 2 * TT])
        iota_r, iota_b = sb("iota_r", [P, P], F16), sb("iota_b", [P, NB], F16)
        iota_bf = sb("iota_bf", [1, NB])
        part1, jtab = sb("part1", [P, 1]), sb("jtab", [P, 2 * TT])
        spare = sb("spare", [P, -(-NB // UN) * UN])
        hot_r, hot_b = sb("hot_r", [P, UN, P], F16), sb("hot_b", [P, UN, 2 * NB], F16)
        eb3, ebf, ebi = sb("eb3", [1, NB, NX]), sb("ebf", [1, NB]), sb("ebi", [1, NB + 2], I32)
        ix = sb("ix", [P, 6, NB])
        idx = sb("idx", [P, 2, NB], U32)
        gat_i, sca_i = sb("gat_i", [P, UN], U32), sb("sca_i", [P, UN], U32)
        taken = [0]

        def carve(a, b, dt=F32):
            words = a * b * (1 if dt == F32 else 2) // (1 if dt == F32 else 4)
            flat = qphi[:, :, :].rearrange("p g l -> p (g l)")[:, taken[0]:taken[0] + words]
            taken[0] += words
            return (flat if dt == F32 else flat.bitcast(dt)).rearrange("p (a b) -> p a b", a=a)

        xg, xgT = carve(UN, 2 * E, F16), carve(2, 2 * E, F16)
        hid_h, hid_l = carve(2, HID, F16), carve(2, HID, F16)
        y_part, y_sb = carve(2, E), carve(UN, E)
        XG_BANK, H_BANK, Y_BANK = bank[0:2], bank[4:6], bank[6:8]
        IDX_BANK, RANK_BANK, TOTAL_BANK = bank[2], bank[4], bank[5]
        y1 = xn[:, :, :].rearrange("p (q t) e -> p q t e", q=2)
        y2 = xT[:, :].rearrange("p (q t e) -> p q t e", q=2, e=E)
        o_sb = rot[:, 0:CH, :].rearrange("p t f -> p (t f)").rearrange("p (q t e) -> p q t e", q=2, e=E)

        s = {k: sem(k) for k in (
            "route_const", "sm_sub", "sm_exp", "masks", "ranked", "hot_ready", "hot_used", "idx_done",
            "idx_ready", "eb_ready", "gi_ready", "si_ready", "xg_done", "xg_copied", "h_done", "hi_ready",
            "lo_ready", "y_done", "yp_ready", "y_ready", "w_ready", "u_done", "f_var", "f_rstd", "f_norm",
            "o_ready", "g_land0", "g_land1", "g_land2", "g_land3", "s_land0", "s_land1", "s_land2", "s_land3",
            "y_ld0", "g_carried", "s_carried", "y_ld1", "o_st0", "o_st1",
            "x_first", "x_rest", "ld_set", "ld_proj", "ld_cos", "ld_sin", "ld_gate", "ld_w0", "ld_w1",
            "ld_b", "pool_const", "dve_done", "act_own", "pool_own", "h_split", "l_split",
            "b_zero", "b_ready", "t2_done", "t3_done", "u_ready", "sorf_ready",
            "ln1_var", "ln1_rstd", "xn_ready", "xt_done", "xt_copied", "qk_done", "v_done", "rope_read",
            "rot_ready", "sq_done", "nrm_ready", "e_ready", "v_copied", "vext_ready",
            "rt_done", "rt_copied", "pk_done", "ek_done", "s_done", "s_ready", "pq_done", "eq_done",
            "nu_done", "nu_read", "at_done", "at_copied", "z_done", "z_read", "z_var",
            "z_rstd", "x2_ready", "y_var", "y_rstd", "xn2_ready", "hl_ready",
            "x2t_done", "x2t_copied", "lg_done", "lg_read", "hl_st0", "hl_st1")}
        S = type("Sems", (), s)

        block = ctx.enter_context(nc.Block())

        def drive(step):
            step(-1, False, False, True)
            step(0, False, True, True)
            return step

        @block.sync
        def _(sp):
            sp.dma_start(x_sb[:, 0:NT, :], x_d[:, 0:NT, :]).then_inc(S.x_first, 16)
            sp.dma_start(wqk_sb[:, :], wqk).then_inc(S.ld_proj, 16)
            sp.dma_start(wv_sb[:, :], wv).then_inc(S.ld_proj, 16)
            for dst, src in ((had_sb[:, :], had), (hadp_sb[:, :], hadp), (s2_sb[:, :], sgn2),
                             (s3_sb[:, :], sgn3), (s1_sb[:, :], sgn1.to_broadcast([SP_, P])),
                             (hm_sb[:, :], hmask), (scl_sb[:, :], scl.to_broadcast([P, NH * M]))):
                sp.dma_start(dst, src).then_inc(S.ld_set, 16)
            for q in range(2):
                sp.dma_start(cos_sb[:, CH * q:CH * q + CH, :], cost[:, CH * q:CH * q + CH, :])\
                    .then_inc(S.ld_cos, 16)
                sp.dma_start(sin_sb[:, :, q * E:(q + 1) * E], sint).then_inc(S.ld_sin, 16)
            sp.dma_start(x_sb[:, NT:, :], x_d[:, NT:, :]).then_inc(S.x_rest, 16)
            for dst, src in ((wo_sb[:, :], wo), (sm_sb[:, :], smask), (gw_sb[:, :], gate_w),
                             (gb_sb[:, :], gate_b.to_broadcast([P, NX]))):
                sp.dma_start(dst, src).then_inc(S.ld_gate, 16)
            for half in range(2):
                sp.dma_start(b1_sb[32 * half:32 * half + NX * HC, :],
                             b1.rearrange("e (c m) -> (e c) m", m=P)).then_inc(S.ld_b, 16)
            sp.wait_ge(S.b_zero, 1)
            for half in range(2):
                sp.dma_start(b2_sb[32 * half:32 * half + NX, :], b2).then_inc(S.ld_b, 16)
            for k in range(2 * NX):
                e, second = k // 2, k % 2
                if k >= 2:
                    sp.wait_ge(S.l_split, k - 1)
                src = w2[e].rearrange("(c p) o -> p c o", p=P) if second else w1[e]
                dst = stage[:, k % 2, :]
                dst = dst.rearrange("p (c o) -> p c o", c=HC) if second else dst
                sp.dma_start(dst, src).then_inc(S.ld_w1 if second else S.ld_w0, 16)

            def store(c, h):
                sp.wait_ge(S.hl_ready, 2 * c + h + 1)
                sp.dma_start(xn_v[:, bass.ds(NT * c + CH * h, CH), :], hl[:, h, :, :])\
                    .then_inc(S.hl_st1 if h else S.hl_st0, 16)

            def step(c, prev, cur, nxt):
                if prev:
                    store(c - 1, 1)
                if cur:
                    store(c, 0)

            step(0, False, True, True)
            with sp.Fori(1, NC - 1) as c:
                step(c, True, True, True)
            step(NC - 1, True, True, False)
            step(NC, True, False, False)
            for i in range(UN):
                sp.wait_ge(s[f"s_land{i}"], 16 * ((NB - i + UN - 1) // UN))
            chunks = TT // CH

            def load(k, i):
                for half, dst in enumerate((y1, y2)):
                    sp.dma_start(dst[:, i, :, :], y_v[:, bass.ds(TT * half + CH * (k + i), CH), :])\
                        .then_inc(s[f"y_ld{i}"], 16)

            def put(k, i):
                sp.wait_ge(S.o_ready, k + i + 1)
                sp.dma_start(out_d[:, bass.ds(CH * (k + i), CH), :], o_sb[:, i, :, :]).then_inc(s[f"o_st{i}"], 16)

            load(0, 0)
            load(0, 1)
            with sp.Fori(0, chunks // 2 - 1) as pair:
                k = 2 * pair
                for i in range(2):
                    put(k, i)
                    load(k + 2, i)
            put(chunks - 2, 0)
            put(chunks - 2, 1)
            for i in range(2):
                sp.wait_ge(s[f"o_st{i}"], 16 * chunks // 2)

        @block.gpsimd
        def _(pool):
            own = [0]

            def settle(ins):
                ins.then_inc(S.pool_own, 1)
                own[0] += 1
                pool.wait_ge(S.pool_own, own[0])

            settle(pool.memset(ident[:, :], 0.0))
            settle(pool.affine_select(out=ident[:, :], in_=ident[:, :], compare_op=ALU.not_equal, fill=1.0,
                                      base=0, pattern=[[-1, P]], channel_multiplier=1))
            settle(pool.memset(mhalf[:, :], -0.5))
            pool.tensor_copy(ident16[:, :], ident[:, :]).then_inc(S.pool_const, 1)

            def route_constants():
                for t in (b1_all, b2_all, ones16, tri16, ones8, fresh):
                    pool.memset(t[:, :], 1.0 if t in (ones16, tri16, ones8, fresh) else 0.0)
                pool.memset(sel2[:, :, :], 0.0)
                pool.memset(ebi[:, :], 0)
                settle(pool.memset(sel1[:, :, :, :], 0.0))
                pool.affine_select(out=tri16[:, :], in_=tri16[:, :], compare_op=ALU.is_gt, fill=0.0,
                                   base=0, pattern=[[1, P]], channel_multiplier=-1)
                pool.affine_select(out=fresh[:, :], in_=fresh[:, :], compare_op=ALU.not_equal, fill=0.0,
                                   base=0, pattern=[[0, NX], [1, TT]], channel_multiplier=0)
                for half in range(2):
                    settle(pool.affine_select(out=sel1[:, :, :, :], in_=sel1[:, :, :, :], compare_op=ALU.not_equal,
                                              fill=1.0, base=-32 * half, channel_multiplier=1,
                                              pattern=[[-HC, NX], [-1, HC], [0, P]]))
                    settle(pool.affine_select(out=sel2[:, :, :], in_=sel2[:, :, :], compare_op=ALU.not_equal,
                                              fill=1.0, base=-32 * half, channel_multiplier=1,
                                              pattern=[[-1, NX], [0, P]]))
                for t, pattern, b, m in (
                        (tie, [[-1, NX]], NX, 0), (steps128, [[P, TT]], 0, 0), (iota_r, [[1, P]], 0, 0),
                        (iota_b, [[1, NB]], 0, 0), (iota_bf, [[1, NB]], 0, 0), (part1, [[0, 1]], 1, 1),
                        (jtab, [[1, 2 * TT]], 0, 0), (spare, [[0, -(-NB // UN)], [P, UN]], 2 * N + 1, 1)):
                    ins = pool.iota(t[:, :], pattern, base=b, channel_multiplier=m,
                                    allow_small_or_imprecise_dtypes=True)
                ins.then_inc(S.route_const, 1)

            def power(src, dst, h, have, value, done):
                pool.wait_ge(have, value)
                pool.tensor_tensor(dst[:, h, :], src[:, h, :], mhalf[:, :], ALU.pow).then_inc(done, 1)

            def add_rotated(c, p):
                pool.wait_ge(S.rope_read, 4 * c + p + 1)
                pool.tensor_tensor(
                    rot[:, 2 * p:2 * p + 2, :].rearrange("p t f -> p (t f)"),
                    rc[:, p % 2, :], rs_[:, p % 2, :], ALU.add).then_inc(S.rot_ready, 1)

            def add_x(c, h):
                pool.wait_ge(S.z_read, 2 * c + h + 1)
                pool.tensor_tensor(x2_sb[:, bass.ds(NT * c + CH * h, CH), :],
                                   x_sb[:, bass.ds(NT * c + CH * h, CH), :], z_sb[:, h, :, :],
                                   ALU.add).then_inc(S.x2_ready, 1)

            def scale_v(c, h):
                pool.wait_ge(S.e_ready, 2 * c + h + 1)
                pool.wait_ge(S.v_copied, 2 * c + h + 1)
                ts = slice(CH * h, CH * h + CH)
                pool.tensor_tensor(
                    vext[:, ts, :].rearrange("p t (h d) -> p (t h) d", d=D + 1)[:, :, 0:D],
                    v_sb[:, ts, :].rearrange("p t (h d) -> p (t h) d", d=D),
                    bc(ek[:, ts, :].rearrange("p t h -> p (t h)"), 2, D),
                    ALU.mult).then_inc(S.vext_ready, 1)

            def finish_add(k):
                pool.wait_ge(S.f_norm, k + 1)
                if k >= 2:
                    pool.wait_ge(s[f"o_st{k % 2}"], 16 * (k // 2))
                pool.tensor_tensor(o_sb[:, k % 2, :, :], x2_sb[:, CH * k:CH * k + CH, :],
                                   z_sb[:, k % 2, :, :], ALU.add).then_inc(S.o_ready, 1)

            def step(c, prev, cur, nxt):
                if prev:
                    power(zvp, zr, 1, S.z_var, 2 * c, S.z_rstd)
                if nxt:
                    for h in range(2):
                        power(vpe, rstd, h, S.ln1_var, 2 * c + 3 + h, S.ln1_rstd)
                if prev:
                    add_x(c - 1, 1)
                    power(yvp, yr, 1, S.y_var, 2 * c, S.y_rstd)
                if nxt:
                    add_rotated(c + 1, 0)
                    add_rotated(c + 1, 1)
                if cur:
                    power(zvp, zr, 0, S.z_var, 2 * c + 1, S.z_rstd)
                if nxt:
                    add_rotated(c + 1, 2)
                    add_rotated(c + 1, 3)
                if cur:
                    add_x(c, 0)
                    power(yvp, yr, 0, S.y_var, 2 * c + 1, S.y_rstd)
                if nxt:
                    scale_v(c + 1, 0)
                    scale_v(c + 1, 1)

            step(-1, False, False, True)
            for k in range(2 * NX):
                e, second = k // 2, k % 2
                pool.wait_ge(S.h_split, k + 1)
                src = stage[:, k % 2, :]
                if second:
                    src = src.rearrange("p (c o) -> p c o", c=HC)
                    pool.tensor_tensor(w2s[:, e, :, 1, :], src, w2s[:, e, :, 0, :],
                                       ALU.subtract).then_inc(S.l_split, 1)
                else:
                    pool.tensor_tensor(w1l[:, e, :], src, w1h[:, e, :], ALU.subtract).then_inc(S.l_split, 1)
            route_constants()
            step(0, False, True, True)
            with pool.Fori(1, NC - 1) as c:
                step(c, True, True, True)
            step(NC - 1, True, True, False)
            step(NC, True, False, False)
            for q in (S.hl_st0, S.hl_st1):
                pool.wait_ge(q, 16 * NC)

            def carry(b, col, carried):
                if not (isinstance(b, int) and b == 0):
                    pool.wait_ge(carried, b)
                pool.tensor_tensor(carrier[0:1, col:col + 1], mhalf[0:1, 0:1], mhalf[0:1, 0:1], ALU.add)\
                    .then_inc(carried, 1)

            def gather(b, i):
                if not (isinstance(b, int) and b < UN):
                    pool.wait_ge(S.xg_done, b - UN + 1)
                pool.wait_ge(S.gi_ready, b + 1)
                carry(b, 1, S.g_carried)
                pool.indirect_dma_start(
                    out=xg[:, i, :], out_offset=None, in_=xn_d,
                    in_offset=bass.IndirectOffsetOnAxis(ap=gat_i[:, i:i + 1], axis=0))\
                    .then_inc(s[f"g_land{i}"], 16)

            def scatter(b, i):
                pool.wait_ge(S.y_ready, b + 1)
                carry(b, 2, S.s_carried)
                pool.indirect_dma_start(
                    out=y_d, out_offset=bass.IndirectOffsetOnAxis(ap=sca_i[:, i:i + 1], axis=0),
                    in_=y_sb[:, i, :], in_offset=None).then_inc(s[f"s_land{i}"], 16)

            def block_step(n, i):
                if not (isinstance(n, int) and n >= NB):
                    gather(n, i)
                if not (isinstance(n, int) and n < 3):
                    scatter(n - 3, (i - 3) % UN)

            rounds(pool, block_step, 0, NB + 3, 3)
            for k in range(TT // CH):
                pool.wait_ge(S.f_var, k + 1)
                pool.tensor_tensor(zr[:, k % 2, :], zvp[:, k % 2, :], mhalf[:, :], ALU.pow).then_inc(S.f_rstd, 1)
                if k:
                    finish_add(k - 1)
            finish_add(TT // CH - 1)

        @block.scalar
        def _(act):
            def split(k):
                e, second = k // 2, k % 2
                act.wait_ge(S.ld_w1 if second else S.ld_w0, 16 * (e + 1))
                src = stage[:, k % 2, :]
                if second:
                    act.activation(w2s[:, e, :, 0, :], src.rearrange("p (c o) -> p c o", c=HC),
                                   ACT.Copy).then_inc(S.h_split, 1)
                else:
                    act.activation(w1h[:, e, :], src, ACT.Copy).then_inc(S.h_split, 1)

            def copy(src, dst, have, value, done):
                act.wait_ge(have, value)
                act.activation(dst, src, ACT.Copy).then_inc(done, 1)

            def features_k(c, t):
                act.wait_ge(S.pk_done, NT * c + t + 1)
                act.activation(kphi[:, t, :], PHI_BANK[t % 2][:, :], ACT.Exp).then_inc(S.ek_done, 1)

            def features_q(c, j):
                act.wait_ge(S.pq_done, 2 * NG * c + j + 1)
                h, g = j // NG, j % NG
                act.activation(qphi[:, g, 512 * h:512 * h + 512], PHI_BANK[j % 2][:, :],
                               ACT.Exp).then_inc(S.eq_done, 1)

            def square(c, p):
                act.wait_ge(S.rot_ready, 4 * c + p + 1)
                if p >= 2:
                    act.wait_ge(S.nrm_ready, 4 * c + p - 1)
                else:
                    if not (isinstance(c, int) and c == 0):
                        act.wait_ge(S.nrm_ready, 4 * c + p - 1)
                act.activation(sq[:, p % 2, :], rot[:, 2 * p:2 * p + 2, :].rearrange("p t f -> p (t f)"),
                               ACT.Square).then_inc(S.sq_done, 1)

            def factors(c, h):
                act.wait_ge(S.nrm_ready, 4 * c + 2 * h + 2)
                ts = slice(CH * h, CH * h + CH)
                act.activation(eq_all[:, bass.ds(NT * c + CH * h, CH), :], nrm[:, ts, 0, :], ACT.Exp, scale=-0.5)
                act.activation(vext[:, ts, :].rearrange("p t (h d) -> p t h d", d=D + 1)[:, :, :, D],
                               nrm[:, ts, 1, :], ACT.Exp, scale=-0.5)
                act.activation(ek[:, ts, :], nrm[:, ts, 1, :], ACT.Exp, scale=-0.5).then_inc(S.e_ready, 1)

            def copy_rot(c, h):
                copy(V_BANK[:, :], qT[:, 512 * h:512 * h + 512], S.rt_done, 4 * c + 2 * h + 1, S.rt_copied)
                copy(T_BANK[:, :], kT[:, 512 * h:512 * h + 512], S.rt_done, 4 * c + 2 * h + 2, S.rt_copied)

            def step(c, prev, cur, nxt):
                if cur:
                    for t in range(6):
                        features_k(c, t)
                if prev:
                    copy(T_BANK[:, :], x2T[:, 0, :], S.x2t_done, 2 * c - 1, S.x2t_copied)
                if cur:
                    features_k(c, 6)
                    features_k(c, 7)
                    features_q(c, 0)
                    features_q(c, 1)
                if prev:
                    copy(T_BANK[:, :], x2T[:, 1, :], S.x2t_done, 2 * c, S.x2t_copied)
                if cur:
                    for j in range(2, 2 * NG):
                        features_q(c, j)
                if nxt:
                    copy(T_BANK[:, :], xT[:, 0:512], S.xt_done, 2 * c + 3, S.xt_copied)
                    copy(V_BANK[:, :], xT[:, 512:1024], S.xt_done, 2 * c + 4, S.xt_copied)
                    copy(V_BANK[:, :], v_sb[:, 0:CH, :].rearrange("p t f -> p (t f)"),
                         S.v_done, 2 * c + 3, S.v_copied)
                    square(c + 1, 0)
                    square(c + 1, 1)
                if cur:
                    copy(T_BANK[:, :], attT[:, 0, :], S.at_done, 2 * c + 1, S.at_copied)
                if nxt:
                    copy(V_BANK[:, :], v_sb[:, CH:, :].rearrange("p t f -> p (t f)"),
                         S.v_done, 2 * c + 4, S.v_copied)
                if cur:
                    copy(T_BANK[:, :], attT[:, 1, :], S.at_done, 2 * c + 2, S.at_copied)
                if nxt:
                    square(c + 1, 2)
                    square(c + 1, 3)
                    copy_rot(c + 1, 0)
                    factors(c + 1, 0)
                    copy_rot(c + 1, 1)
                    factors(c + 1, 1)

            step(-1, False, False, True)
            for k in range(2 * NX):
                split(k)
            step(0, False, True, True)
            with act.Fori(1, NC - 1) as c:
                step(c, True, True, True)
            step(NC - 1, True, True, False)
            step(NC, True, False, False)

            act.wait_ge(S.sm_sub, 1)
            act.activation(expo, prob, ACT.Exp).then_inc(S.sm_exp, 1)

            def block_step(n, i):
                if not (isinstance(n, int) and (n < 1 or n > NB)):
                    act.wait_ge(S.h_done, n)
                    act.activation(hid_h[:, (i - 1) % 2, :], H_BANK[(i - 1) % 2][:, :], ACT.Relu)\
                        .then_inc(S.hi_ready, 1)
                if not (isinstance(n, int) and n < 2):
                    act.wait_ge(S.y_done, n - 1)
                    act.activation(y_part[:, i % 2, :], Y_BANK[i % 2][:, E:2 * E], ACT.Copy)\
                        .then_inc(S.yp_ready, 1)

            rounds(act, block_step, 0, NB + 2, 2)
            for k in range(TT // CH):
                act.wait_ge(s[f"y_ld{k % 2}"], 32 * (k // 2 + 1))
                for t in range(CH):
                    ins = act.activation(y1[:, k % 2, t, :], y1[:, k % 2, t, :], ACT.Copy,
                                         scale=gates[:, 0, CH * k + t:CH * k + t + 1])
                ins.then_inc(S.u_done, 1)

        @block.tensor
        def _(pe):
            pe.wait_ge(S.pool_const, 1)

            def transposes(dst, tiles, done):
                for i, src in enumerate(tiles):
                    ins = pe.transpose(dst[:, P * i:P * i + P], src, ident[:, :])
                ins.then_inc(done, 1)

            def x_transposes(c, h):
                pe.wait_ge(S.xn_ready, 2 * c + h + 1)
                transposes(V_BANK if h else T_BANK, [xn[:, CH * h + t, :] for t in range(CH)], S.xt_done)

            def project(c, h):
                for p in range(2 * h, 2 * h + 2):
                    if p >= 2:
                        pe.wait_ge(S.rope_read, 4 * c + p - 1)
                    elif not (isinstance(c, int) and c == 0):
                        pe.wait_ge(S.rope_read, 4 * c + p - 1)
                    for t in (2 * p, 2 * p + 1):
                        ins = pe.matmul(QK_BANK[p % 2][:, 2 * E * (t % 2):2 * E * (t % 2 + 1)],
                                        xT[:, P * t:P * t + P], wqk_sb[:, :], start=True, stop=True)
                    ins.then_inc(S.qk_done, 1)
                if h:
                    pe.wait_ge(S.v_copied, 2 * c + 1)
                for t in range(CH):
                    ins = pe.matmul(V_BANK[:, E * t:E * t + E], xT[:, P * (CH * h + t):P * (CH * h + t) + P],
                                    wv_sb[:, :], start=True, stop=True)
                ins.then_inc(S.v_done, 1)

            def rot_transposes(c, h, k):
                transposes(T_BANK if k else V_BANK,
                           [rot[:, CH * h + t, E * k:E * k + E] for t in range(CH)], S.rt_done)

            def phi_k(c, t):
                pe.matmul(PHI_BANK[t % 2][:, :], kT[:, P * t:P * t + P],
                          sorf[:, :, :].rearrange("p h m -> p (h m)"), start=True, stop=True).then_inc(S.pk_done, 1)

            def sums(c, t):
                pe.wait_ge(S.ek_done, NT * c + t + 1)
                if t % CH == 0:
                    pe.wait_ge(S.vext_ready, 2 * c + t // CH + 1)
                if t == 0 and not (isinstance(c, int) and c == 0):
                    pe.wait_ge(S.s_ready, c)
                for g in range(NG):
                    ins = pe.matmul(S_BANK[:, W * g:W * g + W], kphi[:, t, P * g:P * g + P],
                                    vext[:, t, W * g:W * g + W], start=(t == 0 and g == 0), stop=(t == NT - 1),
                                    skip_group_check=True)
                if t == NT - 1:
                    ins.then_inc(S.s_done, 1)

            def phi_q(c, j):
                if j < 2:
                    pe.wait_ge(S.ek_done, NT * c + NT - 1 + j)
                else:
                    pe.wait_ge(S.eq_done, 2 * NG * c + j - 1)
                h, g = j // NG, j % NG
                pe.matmul(PHI_BANK[j % 2][:, :], sorf[:, HG * g:HG * g + HG, :].rearrange("p h m -> p (h m)"),
                          qT[:, 512 * h:512 * h + 512], start=True, stop=True).then_inc(S.pq_done, 1)

            def outputs(c, n):
                if n < 2:
                    pe.wait_ge(S.eq_done, 2 * NG * c + 2 * NG - 1 + n)
                else:
                    pe.wait_ge(S.nu_read, 4 * c + n - 1)
                if n == 0:
                    pe.wait_ge(S.s_ready, c + 1)
                for i in range(2):
                    t = 2 * n + i
                    for g in range(NG):
                        ins = pe.matmul(PHI_BANK[n % 2][:, NG * W * i + W * g:NG * W * i + W * g + W],
                                        qphi[:, g, P * t:P * t + P], s_sb[:, W * g:W * g + W],
                                        start=True, stop=True, skip_group_check=True)
                ins.then_inc(S.nu_done, 1)

            def att_transposes(c, h):
                pe.wait_ge(S.nu_read, 4 * c + 2 * h + 2)
                transposes(T_BANK, [att[:, CH * h + t, :] for t in range(CH)], S.at_done)

            def out_project(c, h):
                pe.wait_ge(S.at_copied, 2 * c + h + 1)
                for t in range(CH):
                    ins = pe.matmul(Z_BANK[:, E * t:E * t + E], attT[:, h, P * t:P * t + P], wo_sb[:, :],
                                    start=True, stop=True)
                ins.then_inc(S.z_done, 1)

            def x2_transposes(c, h):
                pe.wait_ge(S.xn2_ready, 2 * c + h + 1)
                transposes(T_BANK, [xn2[:, h, t, :] for t in range(CH)], S.x2t_done)

            def logits(c, h):
                pe.wait_ge(S.x2t_copied, 2 * c + h + 1)
                for t in range(CH):
                    ins = pe.matmul(Z_BANK[:, NX * t:NX * t + NX], x2T[:, h, P * t:P * t + P], gw_sb[:, :],
                                    start=True, stop=True)
                ins.then_inc(S.lg_done, 1)

            def step(c, prev, cur, nxt):
                if cur:
                    pe.wait_ge(S.rt_copied, 4 * c + 2)
                    for t in range(NT):
                        if t == CH:
                            pe.wait_ge(S.rt_copied, 4 * c + 4)
                        if t >= 2:
                            pe.wait_ge(S.ek_done, NT * c + t - 1)
                        elif prev:
                            pe.wait_ge(S.nu_read, 4 * c - 1 + t)
                        phi_k(c, t)
                        if t >= 2:
                            sums(c, t - 2)
                        if prev and t == 4:
                            x2_transposes(c - 1, 0)
                        if prev and t == 6:
                            pe.wait_ge(S.z_read, 2 * c)
                            logits(c - 1, 0)
                    phi_q(c, 0)
                    sums(c, NT - 2)
                    phi_q(c, 1)
                    sums(c, NT - 1)
                elif prev:
                    pe.wait_ge(S.at_copied, 2 * c)
                    x2_transposes(c - 1, 0)
                    pe.wait_ge(S.z_read, 2 * c)
                    logits(c - 1, 0)
                if prev:
                    x2_transposes(c - 1, 1)
                if cur:
                    phi_q(c, 2)
                    phi_q(c, 3)
                if prev:
                    pe.wait_ge(S.lg_read, 2 * c - 1)
                    logits(c - 1, 1)
                if cur:
                    for j in range(NG, 2 * NG):
                        phi_q(c, j)
                if nxt:
                    x_transposes(c + 1, 0)
                    x_transposes(c + 1, 1)
                if cur:
                    outputs(c, 0)
                    outputs(c, 1)
                if nxt:
                    if not cur:
                        pe.wait_ge(S.ld_proj, 32)
                    pe.wait_ge(S.xt_copied, 2 * c + 4)
                    project(c + 1, 0)
                if cur:
                    att_transposes(c, 0)
                    outputs(c, 2)
                    if prev:
                        pe.wait_ge(S.lg_read, 2 * c)
                    elif isinstance(c, int) and c == 0:
                        pe.wait_ge(S.ld_gate, 64)
                    out_project(c, 0)
                    outputs(c, 3)
                if nxt:
                    project(c + 1, 1)
                if cur:
                    att_transposes(c, 1)
                if nxt:
                    pe.wait_ge(S.rot_ready, 4 * c + 6)
                    pe.wait_ge(S.v_copied, 2 * c + 4)
                    rot_transposes(c + 1, 0, 0)
                if cur:
                    pe.wait_ge(S.at_copied, 2 * c + 2)
                if nxt:
                    rot_transposes(c + 1, 0, 1)
                if cur:
                    pe.wait_ge(S.z_read, 2 * c + 1)
                    out_project(c, 1)
                if nxt:
                    pe.wait_ge(S.rot_ready, 4 * c + 8)
                    pe.wait_ge(S.rt_copied, 4 * c + 5)
                    rot_transposes(c + 1, 1, 0)
                    pe.wait_ge(S.rt_copied, 4 * c + 6)
                    rot_transposes(c + 1, 1, 1)

            step(-1, False, False, True)
            pe.wait_ge(S.u_ready, 1)
            pe.matmul(PHI_BANK[0][0:SP_, 0:P], had_sb[:, :], u2[:, :], start=True, stop=True).then_inc(S.t2_done, 1)
            pe.wait_ge(S.u_ready, 2)
            pe.matmul(PHI_BANK[1][:, 0:M], u3[:, :], had_sb[:, 0:M], start=True, stop=True).then_inc(S.t3_done, 1)
            pe.wait_ge(S.sorf_ready, 1)
            step(0, False, True, True)
            with pe.Fori(1, NC - 1) as c:
                step(c, True, True, True)
            step(NC - 1, True, True, False)
            step(NC, True, False, False)

            pe.wait_ge(S.masks, 1)
            pe.wait_ge(S.route_const, 1)
            pe.matmul(RANK_BANK[:, 0:TT * NX], tri16[:, :], mask16[:, :], start=True, stop=True)
            pe.matmul(TOTAL_BANK[:, 0:TT * NX], ones16[:, :], mask16[:, :], start=True, stop=True).then_inc(S.ranked, 1)

            def place(j, i, first):
                pe.wait_ge(S.hot_ready, j + i + 1)
                pe.matmul(IDX_BANK[:, 0:2 * NB], hot_r[:, i, :], hot_b[:, i, :], start=first, stop=False,
                          skip_group_check=True).then_inc(S.hot_used, 1)

            for i in range(UN):
                place(0, i, i == 0)
            with pe.Fori(1, 2 * TT // UN) as k:
                j = UN * k
                for i in range(UN):
                    place(j, i, False)

            def gather_transposes(b, i):
                q = i % 2
                pe.wait_ge(s[f"g_land{i}"], landed(b, i))
                if not (isinstance(b, int) and b < 2):
                    pe.wait_ge(S.xg_copied, b - 1)
                dst = XG_BANK[q][:, 0:E].bitcast(F16)
                for k in range(2):
                    ins = pe.transpose(dst[:, E * k:E * k + E], xg[:, i, E * k:E * k + E], ident16[:, :])
                ins.then_inc(S.xg_done, 1)

            def hidden(b, q, e):
                pe.wait_ge(S.xg_copied, b + 1)
                if not (isinstance(b, int) and b < 2):
                    pe.wait_ge(S.lo_ready, b - 1)
                pe.matmul(H_BANK[q][:, :], b1_all[:, :],
                          sel1[:, bass.ds(e, 1), :, :].rearrange("p o c t -> p (o c t)"),
                          start=True, stop=False, skip_group_check=True)
                for c in range(HC):
                    dst = H_BANK[q][:, P * c:P * c + P]
                    high = w1h[:, bass.ds(e, 1), P * c:P * c + P].rearrange("p o f -> p (o f)")
                    low = w1l[:, bass.ds(e, 1), P * c:P * c + P].rearrange("p o f -> p (o f)")
                    pe.matmul(dst, high, xgT[:, q, 0:E], start=False, stop=False, skip_group_check=True)
                    pe.matmul(dst, high, xgT[:, q, E:2 * E], start=False, stop=False, skip_group_check=True)
                    ins = pe.matmul(dst, low, xgT[:, q, 0:E], start=False, stop=True, skip_group_check=True)
                ins.then_inc(S.h_done, 1)

            def output(b, q, e):
                pe.wait_ge(S.lo_ready, b + 1)
                if not (isinstance(b, int) and b < 2):
                    pe.wait_ge(S.y_ready, b - 1)
                dst = Y_BANK[q]
                for c in range(HC):
                    both = w2s[:, bass.ds(e, 1), c, :, :].rearrange("p o h f -> p (o h f)")
                    high = w2s[:, bass.ds(e, 1), c, 0, :].rearrange("p o f -> p (o f)")
                    pe.matmul(dst[:, 0:2 * E], hid_h[:, q, P * c:P * c + P], both,
                              start=(c == 0), stop=False, skip_group_check=True)
                    pe.matmul(dst[:, 0:E], hid_l[:, q, P * c:P * c + P], high, start=False, stop=False,
                              skip_group_check=True)
                pe.matmul(dst[:, 0:E], sel2[:, bass.ds(e, 1), :].rearrange("p o t -> p (o t)"), b2_all[:, :],
                          start=False, stop=True, skip_group_check=True).then_inc(S.y_done, 1)

            pe.wait_ge(S.eb_ready, 1)
            expert_of = {}

            def block_step(n, i):
                if not (isinstance(n, int) and n >= NB):
                    gather_transposes(n, i)
                if not (isinstance(n, int) and (n < 1 or n > NB)):
                    hidden(n - 1, (i - 1) % 2, expert_of[i - 1])
                if not (isinstance(n, int) and n < 2):
                    output(n - 2, i % 2, expert_of[i - 2])

            def experts_from(n, count):
                _, values = nc.values_load_multi_w_load_instructions(
                    ebi[0:1, bass.ds(n, count)], engines=(pe.engine,), min_val=0, max_val=NX - 1)
                return values

            def expert_round(n, count, first):
                for k, v in enumerate(experts_from(n, min(count + 1, NB + 2 - n) if isinstance(n, int) else count + 1)):
                    expert_of[first - 2 + k] = v

            rounds(pe, block_step, 0, NB + 2, 2, expert_round)

        @block.vector
        def _(dve):
            done = [0]
            base = [0]

            def mark(ins):
                ins.then_inc(S.dve_done, 1)
                done[0] += 1

            def settle():
                dve.wait_ge(S.dve_done, base[0] + done[0])

            def statistics(tiles, st, m, v, h, ready):
                for t, src in enumerate(tiles):
                    ins = dve.bn_stats(st[:, h, t, :], src)
                mark(ins)
                settle()
                dve.tensor_copy(carrier[:, 0:1], mhalf[:, 0:1])
                for t in range(CH):
                    ins = dve.bn_aggr(m[:, h, t, :], st[:, h, t, :])
                mark(ins)
                settle()
                dve.tensor_scalar(v[:, h, :], m[:, h, :, 1], LN_EPS, None, ALU.add).then_inc(ready, 1)

            def normalise(dst, src, m, r, h, finished):
                for t in range(CH):
                    ins = dve.tensor_scalar(dst[t], src[t], m[:, h, t, 0:1], r[:, h, t:t + 1],
                                            ALU.subtract, ALU.mult)
                ins.then_inc(finished, 1)

            def x_tiles(c, h):
                return [x_sb[:, bass.ds(NT * c + CH * h + t, 1), :].rearrange("p o e -> p (o e)")
                        for t in range(CH)]

            def rope(c, p):
                dve.wait_ge(S.qk_done, 4 * c + p + 1)
                if p >= 2:
                    dve.wait_ge(S.rot_ready, 4 * c + p - 1)
                elif not (isinstance(c, int) and c == 0):
                    dve.wait_ge(S.rot_ready, 4 * c + p - 1)
                qk = QK_BANK[p % 2]
                ts = slice(2 * p, 2 * p + 2)
                dve.tensor_tensor(rc[:, p % 2, :].rearrange("p (t a f) -> p t a f", t=2, a=2),
                                  qk[:, :].rearrange("p (t a f) -> p t a f", t=2, a=2),
                                  bc(cos_sb[:, ts, :], 2, 2), ALU.mult)
                swapped = qk[:, :].rearrange("p (a h f) -> p a h f", h=2, f=E // 2)
                sn = sin_sb[:, ts, :].rearrange("p t (a h f) -> p (t a) h f", h=2, f=E // 2)
                dst = rs_[:, p % 2, :].rearrange("p (a h f) -> p a h f", h=2, f=E // 2)
                for h in range(2):
                    ins = dve.tensor_tensor(dst[:, :, h, :], swapped[:, :, 1 - h, :], sn[:, :, h, :], ALU.mult)
                ins.then_inc(S.rope_read, 1)

            def squares(c, p):
                dve.wait_ge(S.sq_done, 4 * c + p + 1)
                dve.tensor_reduce(
                    nrm[:, 2 * p:2 * p + 2, :, :].rearrange("p t a h -> p (t a) h"),
                    sq[:, p % 2, :].rearrange("p (a s h i) -> p a h s i", a=4, s=2, i=HALF),
                    AX.XY, ALU.add).then_inc(S.nrm_ready, 1)

            def mask_sums(c):
                dve.wait_ge(S.s_done, c + 1)
                dve.tensor_tensor(s_sb[:, :].rearrange("p (g w) -> p g w", g=NG),
                                  S_BANK[:, 0:NG * W].rearrange("p (g w) -> p g w", g=NG),
                                  bc(sm_sb[:, :], 1, NG), ALU.mult).then_inc(S.s_ready, 1)

            def divide(c, n):
                dve.wait_ge(S.nu_done, 4 * c + n + 1)
                nu = PHI_BANK[n % 2][:, 0:2 * NG * W].rearrange("p (t h d) -> p t h d", t=2, d=D + 1)
                eqs = eq_all[:, bass.ds(NT * c + 2 * n, 2), :]
                d0, d1, d2, d3 = (den[:, n % 2, k, :, :] for k in range(4))
                mark(dve.scalar_tensor_tensor(out=d0, in0=nu[:, :, :, D], scalar=1.0 / M, in1=eqs,
                                              op0=ALU.mult, op1=ALU.mult))
                settle()
                mark(dve.tensor_scalar(d1, d0, DEN_EPS, None, ALU.max))
                settle()
                mark(dve.reciprocal(d2, d1))
                settle()
                mark(dve.scalar_tensor_tensor(out=d3, in0=d2, scalar=1.0 / M, in1=eqs,
                                              op0=ALU.mult, op1=ALU.mult))
                settle()
                dve.tensor_tensor(
                    att[:, 2 * n:2 * n + 2, :].rearrange("p t (h d) -> p (t h) d", d=D),
                    nu.rearrange("p t h d -> p (t h) d")[:, :, 0:D],
                    bc(d3.rearrange("p t h -> p (t h)"), 2, D), ALU.mult).then_inc(S.nu_read, 1)

            def z_tiles():
                return [Z_BANK[:, E * t:E * t + E] for t in range(CH)]

            def z_statistics(c, h):
                dve.wait_ge(S.z_done, 2 * c + h + 1)
                statistics(z_tiles(), zst, zmv, zvp, h, S.z_var)

            def z_normalise(c, h):
                dve.wait_ge(S.z_rstd, 2 * c + h + 1)
                normalise([z_sb[:, h, t, :] for t in range(CH)], z_tiles(), zmv, zr, h, S.z_read)

            def x2_tiles(c, h):
                return [x2_sb[:, bass.ds(NT * c + CH * h + t, 1), :].rearrange("p o e -> p (o e)")
                        for t in range(CH)]

            def y_statistics(c, h):
                dve.wait_ge(S.x2_ready, 2 * c + h + 1)
                statistics(x2_tiles(c, h), yst, ymv, yvp, h, S.y_var)

            def y_normalise(c, h):
                dve.wait_ge(S.y_rstd, 2 * c + h + 1)
                normalise([xn2[:, h, t, :] for t in range(CH)], x2_tiles(c, h), ymv, yr, h, S.xn2_ready)
                dve.wait_ge(S.xn2_ready, 2 * c + h + 1)
                if not (isinstance(c, int) and c == 0):
                    dve.wait_ge(S.hl_st1 if h else S.hl_st0, 16 * c)
                mark(dve.tensor_copy(hl[:, h, :, 0:E], xn2[:, h, :, :]))
                settle()
                dve.tensor_tensor(hl[:, h, :, E:2 * E], xn2[:, h, :, :], hl[:, h, :, 0:E],
                                  ALU.subtract).then_inc(S.hl_ready, 1)

            def read_logits(c, h):
                dve.wait_ge(S.lg_done, 2 * c + h + 1)
                dve.tensor_tensor(logit[:, bass.ds(NT * c + CH * h, CH), :],
                                  Z_BANK[:, 0:NX * CH].rearrange("p (t e) -> p t e", e=NX),
                                  bc(gb_sb[:, :], 1, CH), ALU.add).then_inc(S.lg_read, 1)

            def step(c, prev, cur, nxt):
                if prev:
                    z_statistics(c - 1, 1)
                if nxt:
                    for h in range(2):
                        statistics(x_tiles(c + 1, h), bst, mv, vpe, h, S.ln1_var)
                if prev:
                    z_normalise(c - 1, 1)
                if nxt:
                    for h in range(2):
                        dve.wait_ge(S.ln1_rstd, 2 * c + 3 + h)
                        normalise([xn[:, CH * h + t, :] for t in range(CH)], x_tiles(c + 1, h), mv, rstd, h,
                                  S.xn_ready)
                if prev:
                    y_statistics(c - 1, 1)
                    y_normalise(c - 1, 1)
                    read_logits(c - 1, 0)
                if cur:
                    mask_sums(c)
                if prev:
                    read_logits(c - 1, 1)
                if cur:
                    divide(c, 0)
                    divide(c, 1)
                if nxt:
                    rope(c + 1, 0)
                    rope(c + 1, 1)
                if cur:
                    divide(c, 2)
                    divide(c, 3)
                    z_statistics(c, 0)
                if nxt:
                    squares(c + 1, 0)
                    squares(c + 1, 1)
                    rope(c + 1, 2)
                if cur:
                    z_normalise(c, 0)
                if nxt:
                    rope(c + 1, 3)
                    squares(c + 1, 2)
                    squares(c + 1, 3)
                if cur:
                    y_statistics(c, 0)
                    y_normalise(c, 0)

            dve.memset(b2_sb[:, :], 0.0).then_inc(S.b_zero, 1)
            dve.wait_ge(S.pool_const, 1)
            dve.wait_ge(S.x_first, 16)
            for h in range(2):
                statistics(x_tiles(0, h), bst, mv, vpe, h, S.ln1_var)
            for h in range(2):
                dve.wait_ge(S.ln1_rstd, h + 1)
                normalise([xn[:, CH * h + t, :] for t in range(CH)], x_tiles(0, h), mv, rstd, h, S.xn_ready)
            dve.wait_ge(S.ld_set, 7 * 16)
            mark(dve.tensor_tensor(u1[:, :], hadp_sb[:, :], s1_sb[:, :], ALU.mult))
            settle()

            def by_head(ap):
                return ap.rearrange("k (s h i) -> k s h i", s=2, i=HALF)

            for a in range(2):
                ins = dve.tensor_tensor(by_head(u2[:, :])[:, a], by_head(u1[:, :])[:, a],
                                        bc(s2_sb[:, :], 2, HALF), ALU.mult)
            ins.then_inc(S.u_ready, 1)
            dve.wait_ge(S.ld_cos, 32)
            dve.wait_ge(S.ld_sin, 32)
            rope(0, 0)
            rope(0, 1)
            squares(0, 0)
            squares(0, 1)
            rope(0, 2)
            rope(0, 3)
            squares(0, 2)
            squares(0, 3)
            dve.wait_ge(S.t2_done, 1)
            for a in range(2):
                ins = dve.tensor_tensor(by_head(u3[:, :])[:, a], by_head(PHI_BANK[0][0:SP_, 0:P])[:, a],
                                        bc(s3_sb[:, :], 2, HALF), ALU.mult)
            ins.then_inc(S.u_ready, 1)
            mark(dve.tensor_tensor(sorf[:, :, :], scl_sb[:, :].rearrange("p (h m) -> p h m", m=M),
                                   bc(hm_sb[:, :], 2, M), ALU.mult))
            dve.wait_ge(S.t3_done, 1)
            mark(dve.tensor_scalar(t3[:, :], PHI_BANK[1][:, 0:M], float(SP_) ** -2, None, ALU.mult))
            settle()
            dve.tensor_tensor(sorf[:, :, :], sorf[:, :, :], bc(t3[:, :], 1, NH), ALU.mult).then_inc(S.sorf_ready, 1)
            dve.wait_ge(S.ld_gate, 64)
            dve.wait_ge(S.x_rest, 16)
            step(0, False, True, True)
            base[0], done[0] = done[0], 0
            start = base[0]
            with dve.Fori(1, NC - 1) as c:
                base[0] = start + (c - 1) * MARKS
                step(c, True, True, True)
                assert done[0] == MARKS, done[0]
            base[0], done[0] = start + (NC - 2) * MARKS, 0
            step(NC - 1, True, True, False)
            step(NC, True, False, False)

            def link(ins):
                mark(ins)
                settle()

            dve.wait_ge(S.ld_b, 64)
            dve.wait_ge(S.route_const, 1)
            for src, high, dst in ((b1_sb, b1_h, b1_all), (b2_sb, b2_h, b2_all)):
                link(dve.tensor_copy(high[:, :], src[:, :]))
                dve.tensor_copy(dst[0:32, :], src[0:32, :])
                dve.tensor_tensor(dst[32:64, :], src[32:64, :], high[32:64, :], ALU.subtract)
            lg = logit[:, :, :]
            pr, ex, p2 = tokens(prob), tokens(expo), tokens(prob2)
            link(dve.tensor_reduce(red[:, 0, :], lg, AX.X, ALU.max))
            dve.tensor_tensor(pr, lg, bc(red[:, 0, :], 2, NX), ALU.subtract).then_inc(S.sm_sub, 1)
            dve.wait_ge(S.sm_exp, 1)
            link(dve.tensor_reduce(red[:, 1, :], ex, AX.X, ALU.add))
            link(dve.reciprocal(red[:, 2, :], red[:, 1, :]))
            link(dve.tensor_tensor(pr, ex, bc(red[:, 2, :], 2, NX), ALU.mult))

            def choose(src, gate, one, k):
                link(dve.tensor_reduce(gates[:, gate, :], src, AX.X, ALU.max))
                link(dve.tensor_tensor(tokens(hit), src, bc(gates[:, gate, :], 2, NX), ALU.is_equal))
                link(dve.tensor_tensor(tokens(cand), tokens(hit), bc(tie[:, :], 1, TT), ALU.mult))
                link(dve.tensor_reduce(red[:, 3 + k, :], tokens(cand), AX.X, ALU.max))
                link(dve.tensor_tensor(tokens(one), tokens(cand), bc(red[:, 3 + k, :], 2, NX), ALU.is_equal))

            choose(pr, 0, one1, 0)
            link(dve.scalar_tensor_tensor(out=prob2, in0=one1, scalar=-2.0, in1=prob, op0=ALU.mult, op1=ALU.add))
            choose(p2, 1, one2, 1)
            dve.tensor_tensor(mask16[:, :], one1, one2, ALU.add).then_inc(S.masks, 1)
            dve.wait_ge(S.ranked, 1)
            link(dve.tensor_copy(experts(tot), TOTAL_BANK[:, 0:TT * NX].rearrange("p (t e) -> p e t", e=NX)))
            link(dve.tensor_tensor_scan(cum, fresh[:, :], tot, 0.0, ALU.mult, ALU.add))
            dve.tensor_copy(count[:, :], experts(cum)[:, :, TT - 1])
            link(dve.tensor_tensor(excl, cum, tot, ALU.subtract))
            link(dve.tensor_tensor(experts(cmp8), bc(count[:, :], 2, TT), bc(steps128[:, :], 1, NX), ALU.is_gt))
            link(dve.tensor_reduce(nblk[:, :], experts(cmp8), AX.X, ALU.add))
            link(dve.tensor_tensor_scan(bend[:, :], ones8[:, :], nblk[:, :], 0.0, ALU.mult, ALU.add))
            link(dve.tensor_tensor(eb3[:, :, :], bc(iota_bf[:, :], 2, NX), bc(bend[0:1, :], 1, NB), ALU.is_ge))
            link(dve.tensor_reduce(ebf[:, :], eb3[:, :, :], AX.X, ALU.add))
            dve.tensor_scalar(ebi[:, 2:NB + 2], ebf[:, :], float(NX - 1), None, ALU.min).then_inc(S.eb_ready, 1)
            link(dve.tensor_tensor(nblk[:, :], bend[:, :], nblk[:, :], ALU.subtract))
            link(dve.scalar_tensor_tensor(out=experts(cmp8), in0=bc(nblk[:, :], 2, TT), scalar=float(P),
                                          in1=experts(excl), op0=ALU.mult, op1=ALU.add))
            link(dve.tensor_tensor(tokens(slot3), RANK_BANK[:, 0:TT * NX].rearrange("p (t e) -> p t e", e=NX),
                                   cmp8.rearrange("p (e t) -> p t e", e=NX), ALU.add))
            for k, one in enumerate((one1, one2)):
                link(dve.tensor_tensor(hit, one, slot3, ALU.mult))
                link(dve.tensor_reduce(slots[:, k, :], tokens(hit), AX.X, ALU.add))
            link(dve.tensor_copy(slot_i[:, :, :], slots[:, :, :]))
            dve.tensor_scalar(blk_i[:, :, :], slot_i[:, :, :], 7, None, ALU.arith_shift_right)
            link(dve.tensor_scalar(row_i[:, :, :], slot_i[:, :, :], P - 1, None, ALU.bitwise_and))
            dve.tensor_copy(blk[:, :], blk_i[:, :, :].rearrange("p k t -> p (k t)"))
            link(dve.tensor_copy(row[:, :], row_i[:, :, :].rearrange("p k t -> p (k t)")))

            def hot(j, i, reuse):
                if reuse:
                    dve.wait_ge(S.hot_used, j + i + 1 - UN)
                at = bass.ds(j + i, 1)
                dve.tensor_scalar(hot_r[:, i, :], iota_r[:, :], row[:, at], None, ALU.is_equal)
                dve.tensor_scalar(hot_b[:, i, 0:NB], iota_b[:, :], blk[:, at], part1[:, :],
                                  ALU.is_equal, ALU.mult)
                dve.tensor_scalar(hot_b[:, i, NB:2 * NB], iota_b[:, :], blk[:, at], jtab[:, at],
                                  ALU.is_equal, ALU.mult).then_inc(S.hot_ready, 1)

            for i in range(UN):
                hot(0, i, False)
            with dve.Fori(1, 2 * TT // UN) as m:
                j = UN * m
                for i in range(UN):
                    hot(j, i, True)
            dve.wait_ge(S.hot_used, 2 * TT)
            v, w, a, b_, c_, d_ = (ix[:, i, :] for i in range(6))
            link(dve.tensor_copy(w, IDX_BANK[:, 0:NB]))
            link(dve.scalar_tensor_tensor(out=v, in0=IDX_BANK[:, NB:2 * NB], scalar=float(P), in1=w,
                                          op0=ALU.mult, op1=ALU.add))
            dve.tensor_scalar(a, v, float(N), float(N), ALU.is_gt, ALU.mult)
            link(dve.scalar_tensor_tensor(out=b_, in0=v, scalar=1.0, in1=spare[:, 0:NB],
                                          op0=ALU.is_lt, op1=ALU.mult))
            dve.tensor_tensor(c_, v, a, ALU.subtract)
            link(dve.tensor_tensor(d_, v, b_, ALU.add))
            dve.tensor_scalar(idx[:, 0, :], c_, -1.0, 0.0, ALU.add, ALU.max)
            link(dve.tensor_scalar(idx[:, 1, :], d_, -1.0, None, ALU.add))

            def block_step(n, i):
                q = i % 2
                if not (isinstance(n, int) and n >= NB):
                    dve.wait_ge(S.xg_done, n + 1)
                    dve.tensor_copy(xgT[:, q, :], XG_BANK[q][:, 0:E].bitcast(F16)).then_inc(S.xg_copied, 1)
                    if not (isinstance(n, int) and n >= NB - AHEAD):
                        next_rows(n + AHEAD, (i + AHEAD) % UN)
                if not (isinstance(n, int) and (n < 1 or n > NB)):
                    dve.wait_ge(S.hi_ready, n)
                    dve.scalar_tensor_tensor(out=hid_l[:, 1 - q, :], in0=H_BANK[1 - q][:, :], scalar=0.0,
                                             in1=hid_h[:, 1 - q, :], op0=ALU.max, op1=ALU.subtract)\
                        .then_inc(S.lo_ready, 1)
                if not (isinstance(n, int) and n < 2):
                    dve.wait_ge(S.yp_ready, n - 1)
                    k = (i - 2) % UN
                    if not (isinstance(n, int) and n < UN + 2):
                        dve.wait_ge(s[f"s_land{k}"], scattered(n - 2, k))
                    dve.tensor_copy(sca_i[:, k:k + 1], idx[:, 1, bass.ds(n - 2, 1)])
                    dve.tensor_tensor(y_sb[:, k, :], Y_BANK[q][:, 0:E], y_part[:, q, :], ALU.add)\
                        .then_inc(S.y_ready, 1)

            def next_rows(b, i):
                if not (isinstance(b, int) and b < UN):
                    dve.wait_ge(s[f"g_land{i}"], scattered(b, i))
                dve.tensor_copy(gat_i[:, i:i + 1], idx[:, 0, bass.ds(b, 1)]).then_inc(S.gi_ready, 1)

            for b in range(AHEAD):
                next_rows(b, b)
            rounds(dve, block_step, 0, NB + 2, 2)

            for k in range(TT // CH):
                q = k % 2
                dve.wait_ge(S.u_done, k + 1)
                for t in range(CH):
                    ins = dve.scalar_tensor_tensor(out=y2[:, q, t, :], in0=y2[:, q, t, :],
                                                   scalar=gates[:, 1, CH * k + t:CH * k + t + 1],
                                                   in1=y1[:, q, t, :], op0=ALU.mult, op1=ALU.add)
                link(ins)
                tiles = [y2[:, q, t, :] for t in range(CH)]
                statistics(tiles, zst, zmv, zvp, q, S.f_var)
                dve.wait_ge(S.f_rstd, k + 1)
                if k >= 2:
                    dve.wait_ge(S.o_ready, k - 1)
                normalise([z_sb[:, q, t, :] for t in range(CH)], tiles, zmv, zr, q, S.f_norm)


MARKS = 30
AHEAD = 3


def rounds(engine, step, first, end, straight, before=None):
    n = first
    head = -(-max(straight, AHEAD) // UN) * UN
    loops = (NB - AHEAD - head) // UN
    for start in range(first, head, UN):
        if before:
            before(start, UN, 0)
        for i in range(UN):
            step(start + i, i)
    with engine.Fori(head // UN, head // UN + loops) as k:
        m = UN * k
        if before:
            before(m, UN, 0)
        for i in range(UN):
            step(m + i, i)
    for start in range(head + UN * loops, end, UN):
        count = min(UN, end - start)
        if before:
            before(start, count, 0)
        for i in range(count):
            step(start + i, i)


def landed(b, i):
    return (b - i) * (16 // UN) + 16


def scattered(b, i):
    return (b - i) * (16 // UN)


def _constants():
    had = np.ones((1, 1), np.float32)
    while had.shape[0] < SP_:
        had = np.block([[had, had], [had, -had]]).astype(np.float32)
    rows = np.arange(P)
    half, head, i = rows // (P // 2), rows // HALF % NH, rows % HALF
    hadp = np.ascontiguousarray(had[:, 2 * i + half])
    hmask = (head[:, None] == np.arange(NH)).astype(np.float32)
    smask = (rows[:, None] // M == np.arange(W) // (D + 1)).astype(np.float32)
    freqs = (np.float32(10000.0) ** (-np.arange(0, D, 2, dtype=np.float32) / np.float32(D))).astype(np.float32)
    ang = np.maximum(np.arange(L, dtype=np.float32) - 1, 0)[:, None] * freqs
    cos, sin = np.cos(ang), np.sin(ang)
    cost = np.tile(cos, (1, P // HALF))
    sint = np.concatenate([np.tile(-sin, (1, NH)), np.tile(sin, (1, NH))], axis=1)

    def tiles(a):
        return np.ascontiguousarray(a.reshape(NT, P, P).transpose(1, 0, 2).astype(np.float32))

    return dict(had=had, hadp=hadp, hmask=hmask, smask=smask, cost=tiles(cost), sint=tiles(sint))


def kernel(L0_attn_x, L0_attn_w_qkv, L0_attn_w_out, L0_attn_sorf_signs, L0_attn_sorf_scales,
           L0_ffn_gate_w, L0_ffn_gate_b, L0_ffn_w1, L0_ffn_b1, L0_ffn_w2, L0_ffn_b2):
    import concourse.bacc as bacc
    from concourse.bass_utils import run_bass_kernel_spmd

    a = {k: np.asarray(v) for k, v in dict(
        x=L0_attn_x, qkv=L0_attn_w_qkv, wo=L0_attn_w_out, signs=L0_attn_sorf_signs,
        scales=L0_attn_sorf_scales, gate_w=L0_ffn_gate_w, gate_b=L0_ffn_gate_b, w1=L0_ffn_w1,
        b1=L0_ffn_b1, w2=L0_ffn_w2, b2=L0_ffn_b2).items()}
    qk = a["qkv"][:2 * E].reshape(2, NH, HALF, 2, E).transpose(4, 0, 3, 1, 2).reshape(E, 2 * E)
    signs = a["signs"][:, 0]
    arrays = dict(
        x=a["x"].reshape(N, E), wqk=qk, wv=a["qkv"][2 * E:].T, wo=a["wo"].T,
        sgn1=signs[:, 0, :D].reshape(NH, HALF, 2).transpose(2, 0, 1).reshape(1, P),
        sgn2=signs[:, 1].T, sgn3=signs[:, 2].T, scl=a["scales"][:, 0, :M].reshape(1, NH * M),
        gate_w=a["gate_w"].T, gate_b=a["gate_b"].reshape(1, NX), w1=a["w1"],
        b1=a["b1"], w2=a["w2"], b2=a["b2"], **_constants())
    nc = bacc.Bacc("TRN2", target_bir_lowering=False, num_devices=1)
    named = {f"in_{k}": np.ascontiguousarray(v) for k, v in arrays.items()}
    args = [nc.dram_tensor(k, v.shape, mybir.dt.from_np(v.dtype), kind="ExternalInput").ap()
            for k, v in named.items()]
    out = nc.dram_tensor("out", (N, E), F32, kind="ExternalOutput").ap()
    sandwich_kernel(nc, *args, out)
    got = run_bass_kernel_spmd(nc, [named], core_ids=[0])
    return got.results[0]["out"].reshape(NC, L, E)
```

```python
from contextlib import ExitStack

import numpy as np

import concourse.bass as bass
from concourse import mybir

F32 = mybir.dt.float32
F16 = mybir.dt.float16
I32 = mybir.dt.int32
U32 = mybir.dt.uint32
ALU = mybir.AluOpType
ACT = mybir.ActivationFunctionType
AX = mybir.AxisListType

P = 128
NC, L, E = 4, 1024, 128
NT = L // P
CH = 4
NH, D, M = 16, 8, 32
HG = P // M
NG = NH // HG
W = HG * (D + 1)
SP_ = 64
HALF = D // 2
NX, HID = 8, 512
HC = HID // P
N = NC * L
TT = N // P
NB = (2 * N + NX * (P - 1)) // P
LN_EPS = 1e-5
DEN_EPS = 1e-6
CHUNKS = TT // CH
UN = 4
SPLITS = 2 * NX // NC
ROUNDS = -(-(NB + 2) // UN)


def bc(ap, axis, n):
    shape = list(ap.shape)
    shape.insert(axis, n)
    return ap.unsqueeze(axis).to_broadcast(shape)


def sandwich_kernel(nc, x, wqk, wv, wo, sgn1, sgn2, sgn3, scl, gate_w, gate_b, w1, b1, w2, b2,
                    had, hadp, hmask, smask, cost, sint, out):
    x_d = x.rearrange("(t p) e -> p t e", p=P)
    out_d = out.rearrange("(t p) e -> p t e", p=P)
    xn_d = nc.dram_tensor("xn_rows", (N, 2 * E), F16, kind="Internal").ap()
    y_d = nc.dram_tensor("y_rows", (2 * N + UN * P, E), F32, kind="Internal").ap()
    xn_v = xn_d.rearrange("(t p) e -> p t e", p=P)
    y_v = y_d[0:2 * N, :].rearrange("(t p) e -> p t e", p=P)

    with ExitStack() as ctx:
        def sb(name, shape, dt=F32):
            return ctx.enter_context(nc.sbuf_tensor(name, shape, dt))

        def sem(name):
            return ctx.enter_context(nc.semaphore(name))

        bank = [ctx.enter_context(nc.psum_tensor(f"bank{i}", [P, 512], F32)) for i in range(8)]
        T_BANK, V_BANK, Z_BANK, S_BANK = bank[0], bank[1], bank[2], bank[3]
        QK_BANK, PHI_BANK = bank[4:6], bank[6:8]
        LAST_BANK = PHI_BANK[0]

        x_sb = sb("x_sb", [P, TT, E])
        x2_sb = x_sb
        logit = sb("logit", [P, TT, NX])
        eq_all = sb("eq_all", [P, TT, NH])
        ident = sb("ident", [P, P])
        ident16 = sb("ident16", [P, P], F16)
        wqk_sb, wv_sb, wo_sb = sb("wqk_sb", [P, 2 * E]), sb("wv_sb", [P, E]), sb("wo_sb", [P, E])
        gw_sb, gb_sb = sb("gw_sb", [P, NX]), sb("gb_sb", [P, NX])
        cos_sb, sin_sb = sb("cos_sb", [P, NT, E]), sb("sin_sb", [P, NT, 2 * E])
        sorf = sb("sorf", [P, NH, M])
        mhalf = sb("mhalf", [P, CH])
        carrier = sb("carrier", [P, 2])
        sm_sb = sb("sm_sb", [P, W])
        had_sb, hadp_sb = sb("had_sb", [SP_, SP_]), sb("hadp_sb", [SP_, P])
        s1_sb, s2_sb, s3_sb = sb("s1_sb", [SP_, P]), sb("s2_sb", [SP_, NH]), sb("s3_sb", [SP_, NH])
        scl_sb, hm_sb = sb("scl_sb", [P, NH * M]), sb("hm_sb", [P, NH])
        u1, u2, u3 = sb("u1", [SP_, P]), sb("u2", [SP_, P]), sb("u3", [SP_, P])
        t3 = sb("t3", [P, M])
        stage = sb("stage", [P, 2, HID])
        bst, mv = sb("bst", [P, 2, CH, 6]), sb("mv", [P, 2, CH, 2])
        vpe, rstd = sb("vpe", [P, 2, CH]), sb("rstd", [P, 2, CH])
        xn = sb("xn", [P, NT, E])
        xT = sb("xT", [P, L])
        rc, rs_ = sb("rc", [P, 2, 512]), sb("rs_", [P, 2, 512])
        rot = sb("rot", [P, NT, 2 * E])
        sq = sb("sq", [P, 2, 512])
        nrm = sb("nrm", [P, NT, 2, NH])
        ek = sb("ek", [P, NT, NH])
        v_sb = sb("v_sb", [P, NT, E])
        vext = sb("vext", [P, NT, NG * W])
        qT, kT = sb("qT", [P, L]), sb("kT", [P, L])
        kphi = sb("kphi", [P, NT, NH * M])
        qphi = sb("qphi", [P, NG, L])
        s_sb = sb("s_sb", [P, NG * W])
        den = sb("den", [P, 2, 4, 2, NH])
        att = sb("att", [P, NT, E])
        attT = sb("attT", [P, 2, 512])
        zst, zmv = sb("zst", [P, 2, CH, 6]), sb("zmv", [P, 2, CH, 2])
        zvp, zr = sb("zvp", [P, 2, CH]), sb("zr", [P, 2, CH])
        z_sb = sb("z_sb", [P, 2, CH, E])
        yst, ymv = sb("yst", [P, 2, CH, 6]), sb("ymv", [P, 2, CH, 2])
        yvp, yr = sb("yvp", [P, 2, CH]), sb("yr", [P, 2, CH])
        xn2 = sb("xn2", [P, 2, CH, E])
        hl = sb("hl", [P, 2, CH, 2 * E], F16)
        x2T = sb("x2T", [P, 2, 512])
        w1h, w1l = sb("w1h", [P, NX, HID], F16), sb("w1l", [P, NX, HID], F16)
        w2s = sb("w2s", [P, NX, HC, 2, E], F16)
        b1_sb, b1_all = sb("b1_sb", [64, P]), sb("b1_all", [P, P], F16)
        b1_h = sb("b1_h", [64, P], F16)
        b2_sb, b2_all = sb("b2_sb", [64, P]), sb("b2_all", [P, P], F16)
        b2_h = sb("b2_h", [64, P], F16)
        sel1 = sb("sel1", [P, NX, HC, P], F16)
        sel2 = sb("sel2", [P, NX, P], F16)

        rows = kphi[:, :, :].rearrange("p t f -> p (t f)")
        prob, expo, hit, cand, one1, one2, slot3, cum = (
            rows[:, TT * NX * i:TT * NX * (i + 1)] for i in range(8))
        prob2, tot, excl, cmp8 = (rows[:, TT * NX * i:TT * NX * (i + 1)] for i in range(8, 12))
        tokens = lambda a: a.rearrange("p (t e) -> p t e", e=NX)
        experts = lambda a: a.rearrange("p (e t) -> p e t", e=NX)
        red = sb("red", [P, 6, TT])
        gates = sb("gates", [P, 2, TT])
        mask16 = sb("mask16", [P, TT * NX], F16)
        tri16, ones16 = sb("tri16", [P, P], F16), sb("ones16", [P, P], F16)
        tie, steps128, fresh = sb("tie", [P, NX]), sb("steps128", [P, TT]), sb("fresh", [P, NX * TT])
        count, nblk, bend, ones8 = (sb(n, [P, NX]) for n in ("count", "nblk", "bend", "ones8"))
        slots, slot_i = sb("slots", [P, 2, TT]), sb("slot_i", [P, 2, TT], I32)
        blk_i, row_i = sb("blk_i", [P, 2, TT], I32), sb("row_i", [P, 2, TT], I32)
        blk, row = sb("blk", [P, 2 * TT]), sb("row", [P, 2 * TT])
        iota_r, iota_b = sb("iota_r", [P, P], F16), sb("iota_b", [P, NB], F16)
        iota_bf = sb("iota_bf", [1, NB])
        part1, jtab = sb("part1", [P, 1]), sb("jtab", [P, 2 * TT], F16)
        spare = sb("spare", [P, -(-NB // UN) * UN])
        hot = rot[:, :, :].rearrange("p t f -> p (t f)").bitcast(F16)
        hot_r = hot[:, 0:2 * UN * P].rearrange("p (q i r) -> p q i r", q=2, i=UN)
        hot_a = hot[:, 2 * UN * P:2 * UN * (P + NB)].rearrange("p (q i b) -> p q i b", q=2, i=UN)
        hot_b = hot[:, 2 * UN * (P + NB):2 * UN * (P + 3 * NB)]\
            .rearrange("p (q i c b) -> p q i c b", q=2, i=UN, c=2)
        eb3, ebf, ebp = sb("eb3", [1, NB, NX]), sb("ebf", [1, NB]), sb("ebp", [1, UN * (ROUNDS + 1)])
        words_f, words_i = sb("words_f", [1, 2, ROUNDS]), sb("words_i", [1, ROUNDS], I32)
        ix = sb("ix", [P, 6, NB])
        idx = sb("idx", [P, 2, NB], U32)
        gat_i, sca_i = sb("gat_i", [P, UN], U32), sb("sca_i", [P, UN], U32)
        taken = [0]

        def carve(a, b, dt=F32):
            words = a * b * (1 if dt == F32 else 2) // (1 if dt == F32 else 4)
            flat = qphi[:, :, :].rearrange("p g l -> p (g l)")[:, taken[0]:taken[0] + words]
            taken[0] += words
            return (flat if dt == F32 else flat.bitcast(dt)).rearrange("p (a b) -> p a b", a=a)

        xg, xgT = carve(UN, 2 * E, F16), carve(2, 2 * E, F16)
        hid_h, hid_l = carve(2, HID, F16), carve(2, HID, F16)
        y_part, y_sb = carve(2, E), carve(UN, E)
        XG_BANK, H_BANK, Y_BANK = bank[0:2], bank[4:6], bank[6:8]
        IDX_BANK, RANK_BANK, TOTAL_BANK = bank[2], bank[4], bank[5]
        y1 = rows.rearrange("p (t e) -> p t e", e=E)
        y2 = w2s[:, :, :, :, :].rearrange("p x c h e -> p (x c h e)").bitcast(F32)\
            .rearrange("p (t e) -> p t e", e=E)
        zb = sb("zb", [P, 2, CH])

        s = {k: sem(k) for k in (
            "route_const", "sm_sub", "sm_exp", "masks", "ranked", "hot_ready", "hot_part", "hot_tile", "hot_used", "sel_ready", "bias_ready", "idx_done",
            "idx_ready", "eb_ready", "gi_ready", "si_ready", "xg_done", "xg_copied", "h_done", "hi_ready",
            "lo_ready", "y_done", "yp_ready", "y_ready", "w_ready", "u_done", "f_var", "f_rstd", "f_norm",
            "o_ready", "g_land0", "g_land1", "g_land2", "g_land3", "s_land0", "s_land1", "s_land2", "s_land3",
            "y_ld0", "y_ld1", "carried", "f_bias", "o_st",
            "x_first", "x_rest", "ld_set", "ld_proj", "ld_cos", "ld_sin", "ld_gate", "ld_w0", "ld_w1",
            "ld_b", "pool_const", "dve_done", "act_own", "pool_own", "h_split", "l_split",
            "b_zero", "b_ready", "t2_done", "t3_done", "u_ready", "sorf_ready",
            "ln1_var", "ln1_rstd", "xn_ready", "xt_done", "xt_copied", "qk_done", "v_done", "rope_read",
            "rot_ready", "sq_done", "nrm_ready", "e_ready", "v_copied", "vext_ready",
            "rt_done", "rt_copied", "pk_done", "ek_done", "s_done", "s_ready", "pq_done", "eq_done",
            "nu_done", "nu_read", "at_done", "at_copied", "z_done", "z_read", "z_var",
            "z_rstd", "x2_ready", "y_var", "y_rstd", "xn2_ready", "hl_ready",
            "x2t_done", "x2t_copied", "lg_done", "lg_read", "hl_st0", "hl_st1")}
        S = type("Sems", (), s)

        block = ctx.enter_context(nc.Block())

        def drive(step):
            step(-1, False, False, True)
            step(0, False, True, True)
            return step

        @block.sync
        def _(sp):
            sp.dma_start(x_sb[:, 0:NT, :], x_d[:, 0:NT, :]).then_inc(S.x_first, 16)
            sp.dma_start(wqk_sb[:, :], wqk).then_inc(S.ld_proj, 16)
            sp.dma_start(wv_sb[:, :], wv).then_inc(S.ld_proj, 16)
            for dst, src in ((had_sb[:, :], had), (hadp_sb[:, :], hadp), (s2_sb[:, :], sgn2),
                             (s3_sb[:, :], sgn3), (s1_sb[:, :], sgn1.to_broadcast([SP_, P])),
                             (hm_sb[:, :], hmask), (scl_sb[:, :], scl.to_broadcast([P, NH * M]))):
                sp.dma_start(dst, src).then_inc(S.ld_set, 16)
            for q in range(2):
                sp.dma_start(cos_sb[:, CH * q:CH * q + CH, :], cost[:, CH * q:CH * q + CH, :])\
                    .then_inc(S.ld_cos, 16)
                sp.dma_start(sin_sb[:, :, q * E:(q + 1) * E], sint).then_inc(S.ld_sin, 16)
            sp.dma_start(x_sb[:, NT:, :], x_d[:, NT:, :]).then_inc(S.x_rest, 16)
            for dst, src in ((wo_sb[:, :], wo), (sm_sb[:, :], smask), (gw_sb[:, :], gate_w),
                             (gb_sb[:, :], gate_b.to_broadcast([P, NX]))):
                sp.dma_start(dst, src).then_inc(S.ld_gate, 16)
            for half in range(2):
                sp.dma_start(b1_sb[32 * half:32 * half + NX * HC, :],
                             b1.rearrange("e (c m) -> (e c) m", m=P)).then_inc(S.ld_b, 16)
            sp.wait_ge(S.b_zero, 1)
            for half in range(2):
                sp.dma_start(b2_sb[32 * half:32 * half + NX, :], b2).then_inc(S.ld_b, 16)

            def weights(c, j):
                e, second = SPLITS // 2 * c + j // 2, j % 2
                if j >= 2 or not isinstance(c, int) or c > 0:
                    sp.wait_ge(S.l_split, SPLITS * c + j - 1)
                at = slice(e, e + 1) if isinstance(e, int) else bass.ds(e, 1)
                dst = stage[:, second, :]
                if second:
                    sp.dma_start(dst.rearrange("p (c o) -> p c o", c=HC),
                                 w2[at].rearrange("x (c p) o -> p (x c) o", p=P)).then_inc(S.ld_w1, 16)
                else:
                    sp.dma_start(dst, w1[at].rearrange("x p f -> p (x f)")).then_inc(S.ld_w0, 16)

            def store(c, h):
                sp.wait_ge(S.hl_ready, 2 * c + h + 1)
                sp.dma_start(xn_v[:, bass.ds(NT * c + CH * h, CH), :], hl[:, h, :, :])\
                    .then_inc(S.hl_st1 if h else S.hl_st0, 16)

            def step(c, prev, cur, nxt):
                if cur:
                    for j in range(SPLITS):
                        weights(c, j)
                if prev:
                    store(c - 1, 0)
                    store(c - 1, 1)

            step(0, False, True, True)
            with sp.Fori(1, NC - 1) as c:
                step(c, True, True, True)
            step(NC - 1, True, True, False)
            step(NC, True, False, False)
            for i in range(UN):
                sp.wait_ge(s[f"s_land{i}"], 16 * ((NB - i + UN - 1) // UN))
            def load(k, q):
                for half, dst in enumerate((y1, y2)):
                    sp.dma_start(dst[:, bass.ds(CH * k, CH), :], y_v[:, bass.ds(TT * half + CH * k, CH), :])\
                        .then_inc(S.y_ld1 if q else S.y_ld0, 16)

            load(0, 0)
            load(1, 1)
            with sp.Fori(1, CHUNKS // 2) as pair:
                for q in range(2):
                    sp.wait_ge(S.y_ld1 if q else S.y_ld0, 32 * pair)
                    load(2 * pair + q, q)
            with sp.Fori(0, CHUNKS) as k:
                sp.wait_ge(S.o_ready, k + 1)
                sp.dma_start(out_d[:, bass.ds(CH * k, CH), :], y2[:, bass.ds(CH * k, CH), :]).then_inc(S.o_st, 16)
            sp.wait_ge(S.o_st, 16 * CHUNKS)

        @block.gpsimd
        def _(pool):
            own = [0]

            def settle(ins):
                ins.then_inc(S.pool_own, 1)
                own[0] += 1
                pool.wait_ge(S.pool_own, own[0])

            settle(pool.memset(ident[:, :], 0.0))
            settle(pool.affine_select(out=ident[:, :], in_=ident[:, :], compare_op=ALU.not_equal, fill=1.0,
                                      base=0, pattern=[[-1, P]], channel_multiplier=1))
            settle(pool.memset(mhalf[:, :], -0.5))
            pool.tensor_copy(ident16[:, :], ident[:, :]).then_inc(S.pool_const, 1)

            def route_constants():
                for t in (b1_all, b2_all, ones16, tri16, ones8, fresh):
                    pool.memset(t[:, :], 1.0 if t in (ones16, tri16, ones8, fresh) else 0.0)
                settle(pool.memset(ebp[:, :], 0.0))
                pool.affine_select(out=tri16[:, :], in_=tri16[:, :], compare_op=ALU.is_gt, fill=0.0,
                                   base=0, pattern=[[1, P]], channel_multiplier=-1)
                pool.affine_select(out=fresh[:, :], in_=fresh[:, :], compare_op=ALU.not_equal, fill=0.0,
                                   base=0, pattern=[[0, NX], [1, TT]], channel_multiplier=0)
                for t, pattern, b, m in (
                        (tie, [[-1, NX]], NX, 0), (steps128, [[P, TT]], 0, 0), (iota_r, [[1, P]], 0, 0),
                        (iota_b, [[1, NB]], 0, 0), (iota_bf, [[1, NB]], 0, 0), (part1, [[0, 1]], 1, 1),
                        (jtab, [[1, 2 * TT]], 0, 0), (spare, [[0, -(-NB // UN)], [P, UN]], 2 * N + 1, 1)):
                    ins = pool.iota(t[:, :], pattern, base=b, channel_multiplier=m,
                                    allow_small_or_imprecise_dtypes=True)
                ins.then_inc(S.route_const, 1)

            def selectors():
                pool.memset(sel2[:, :, :], 0.0)
                settle(pool.memset(sel1[:, :, :, :], 0.0))
                for half in range(2):
                    settle(pool.affine_select(out=sel1[:, :, :, :], in_=sel1[:, :, :, :], compare_op=ALU.not_equal,
                                              fill=1.0, base=-32 * half, channel_multiplier=1,
                                              pattern=[[-HC, NX], [-1, HC], [0, P]]))
                    ins = pool.affine_select(out=sel2[:, :, :], in_=sel2[:, :, :], compare_op=ALU.not_equal,
                                             fill=1.0, base=-32 * half, channel_multiplier=1,
                                             pattern=[[-1, NX], [0, P]])
                    settle(ins)
                pool.tensor_copy(carrier[0:1, 1:2], mhalf[0:1, 0:1]).then_inc(S.sel_ready, 1)

            def power(src, dst, h, have, value, done):
                pool.wait_ge(have, value)
                pool.tensor_tensor(dst[:, h, :], src[:, h, :], mhalf[:, :], ALU.pow).then_inc(done, 1)

            def add_rotated(c, p):
                pool.wait_ge(S.rope_read, 4 * c + p + 1)
                pool.tensor_tensor(
                    rot[:, 2 * p:2 * p + 2, :].rearrange("p t f -> p (t f)"),
                    rc[:, p % 2, :], rs_[:, p % 2, :], ALU.add).then_inc(S.rot_ready, 1)

            def add_x(c, h):
                pool.wait_ge(S.z_read, 2 * c + h + 1)
                pool.tensor_tensor(x2_sb[:, bass.ds(NT * c + CH * h, CH), :],
                                   x_sb[:, bass.ds(NT * c + CH * h, CH), :], z_sb[:, h, :, :],
                                   ALU.add).then_inc(S.x2_ready, 1)

            def split_low(c, j):
                e, second = SPLITS // 2 * c + j // 2, j % 2
                at = slice(e, e + 1) if isinstance(e, int) else bass.ds(e, 1)
                pool.wait_ge(S.h_split, SPLITS * c + j + 1)
                src = stage[:, second, :]
                if second:
                    pool.tensor_tensor(w2s[:, at, :, 1, :].rearrange("p x c o -> p (x c) o"),
                                       src.rearrange("p (c o) -> p c o", c=HC),
                                       w2s[:, at, :, 0, :].rearrange("p x c o -> p (x c) o"),
                                       ALU.subtract).then_inc(S.l_split, 1)
                else:
                    pool.tensor_tensor(w1l[:, at, :].rearrange("p x f -> p (x f)"), src,
                                       w1h[:, at, :].rearrange("p x f -> p (x f)"), ALU.subtract)\
                        .then_inc(S.l_split, 1)

            def scale_v(c, h):
                pool.wait_ge(S.e_ready, 2 * c + h + 1)
                pool.wait_ge(S.v_copied, 2 * c + h + 1)
                ts = slice(CH * h, CH * h + CH)
                pool.tensor_tensor(
                    vext[:, ts, :].rearrange("p t (h d) -> p (t h) d", d=D + 1)[:, :, 0:D],
                    v_sb[:, ts, :].rearrange("p t (h d) -> p (t h) d", d=D),
                    bc(ek[:, ts, :].rearrange("p t h -> p (t h)"), 2, D),
                    ALU.mult).then_inc(S.vext_ready, 1)

            def step(c, prev, cur, nxt):
                if prev:
                    power(zvp, zr, 0, S.z_var, 2 * c - 1, S.z_rstd)
                if nxt:
                    for h in range(2):
                        power(vpe, rstd, h, S.ln1_var, 2 * c + 3 + h, S.ln1_rstd)
                if prev:
                    add_x(c - 1, 0)
                    power(yvp, yr, 0, S.y_var, 2 * c - 1, S.y_rstd)
                    power(zvp, zr, 1, S.z_var, 2 * c, S.z_rstd)
                if nxt:
                    add_rotated(c + 1, 0)
                if prev:
                    add_x(c - 1, 1)
                if nxt:
                    add_rotated(c + 1, 1)
                if prev:
                    power(yvp, yr, 1, S.y_var, 2 * c, S.y_rstd)
                if cur:
                    split_low(c, 0)
                    split_low(c, 1)
                if nxt:
                    add_rotated(c + 1, 2)
                if cur:
                    split_low(c, 2)
                if nxt:
                    add_rotated(c + 1, 3)
                if cur:
                    split_low(c, 3)
                if isinstance(c, int) and c == NC - 1:
                    route_constants()
                if nxt:
                    scale_v(c + 1, 0)
                    scale_v(c + 1, 1)
            step(-1, False, False, True)
            step(0, False, True, True)
            with pool.Fori(1, NC - 1) as c:
                step(c, True, True, True)
            step(NC - 1, True, True, False)
            step(NC, True, False, False)
            def hot_tiles(m, q):
                pool.wait_ge(S.hot_ready, m + 1)
                at = slice(UN * m, UN * m + UN) if isinstance(m, int) else bass.ds(UN * m, UN)
                pool.tensor_tensor(hot_b[:, q, :, 1, :], hot_a[:, q, :, :], bc(jtab[:, at], 2, NB), ALU.mult)\
                    .then_inc(S.hot_tile, 1)

            selectors()
            for q in range(2):
                hot_tiles(q, q)
            with pool.Fori(1, TT // UN) as pair:
                for q in range(2):
                    hot_tiles(2 * pair + q, q)

            for q in (S.hl_st0, S.hl_st1):
                pool.wait_ge(q, 16 * NC)

            def block_step(n, i):
                gathers = not (isinstance(n, int) and n >= NB)
                scatters = not (isinstance(n, int) and n < LAG)
                if gathers:
                    pool.wait_ge(S.gi_ready, n + 1)
                if scatters:
                    pool.wait_ge(S.y_ready, n - LAG + 1)
                if not (isinstance(n, int) and n == 0):
                    pool.wait_ge(S.carried, n)
                pool.tensor_tensor(carrier[0:1, 1:2], mhalf[0:1, 0:1], mhalf[0:1, 0:1], ALU.add)\
                    .then_inc(S.carried, 1)
                if gathers:
                    pool.indirect_dma_start(
                        out=xg[:, i, :], out_offset=None, in_=xn_d,
                        in_offset=bass.IndirectOffsetOnAxis(ap=gat_i[:, i:i + 1], axis=0))\
                        .then_inc(s[f"g_land{i}"], 16)
                if scatters:
                    k = (i - LAG) % UN
                    pool.indirect_dma_start(
                        out=y_d, out_offset=bass.IndirectOffsetOnAxis(ap=sca_i[:, k:k + 1], axis=0),
                        in_=y_sb[:, k, :], in_offset=None).then_inc(s[f"s_land{k}"], 16)

            rounds(pool, block_step, NB + LAG, 2 * UN)

            def power_f(k, q):
                pool.wait_ge(S.f_var, k + 1)
                pool.tensor_tensor(zr[:, q, :], zvp[:, q, :], mhalf[:, :], ALU.pow).then_inc(S.f_rstd, 1)

            def add_x2(k):
                pool.wait_ge(S.f_norm, k + 1)
                ts = bass.ds(CH * k, CH)
                pool.tensor_tensor(y2[:, ts, :], x2_sb[:, ts, :], y1[:, ts, :], ALU.add).then_inc(S.o_ready, 1)

            power_f(0, 0)
            power_f(1, 1)
            with pool.Fori(0, CHUNKS // 2 - 1) as pair:
                for q in range(2):
                    add_x2(2 * pair + q)
                    power_f(2 * pair + 2 + q, q)
            for q in range(2):
                add_x2(CHUNKS - 2 + q)

        @block.scalar
        def _(act):
            def split_high(c, j):
                e, second = SPLITS // 2 * c + j // 2, j % 2
                at = slice(e, e + 1) if isinstance(e, int) else bass.ds(e, 1)
                act.wait_ge(S.ld_w1 if second else S.ld_w0, 8 * (SPLITS * c + j - second) + 16)
                src = stage[:, second, :]
                if second:
                    act.activation(w2s[:, at, :, 0, :].rearrange("p x c o -> p (x c) o"),
                                   src.rearrange("p (c o) -> p c o", c=HC), ACT.Copy).then_inc(S.h_split, 1)
                else:
                    act.activation(w1h[:, at, :].rearrange("p x f -> p (x f)"), src, ACT.Copy)\
                        .then_inc(S.h_split, 1)

            def copy(src, dst, have, value, done):
                act.wait_ge(have, value)
                act.activation(dst, src, ACT.Copy).then_inc(done, 1)

            def features_k(c, t):
                act.wait_ge(S.pk_done, NT * c + t + 1)
                act.activation(kphi[:, t, :], PHI_BANK[t % 2][:, :], ACT.Exp).then_inc(S.ek_done, 1)

            def features_q(c, j):
                act.wait_ge(S.pq_done, 2 * NG * c + j + 1)
                h, g = j // NG, j % NG
                act.activation(qphi[:, g, 512 * h:512 * h + 512], PHI_BANK[j % 2][:, :],
                               ACT.Exp).then_inc(S.eq_done, 1)

            def square(c, p):
                act.wait_ge(S.rot_ready, 4 * c + p + 1)
                if p >= 2:
                    act.wait_ge(S.nrm_ready, 4 * c + p - 1)
                else:
                    if not (isinstance(c, int) and c == 0):
                        act.wait_ge(S.nrm_ready, 4 * c + p - 1)
                act.activation(sq[:, p % 2, :], rot[:, 2 * p:2 * p + 2, :].rearrange("p t f -> p (t f)"),
                               ACT.Square).then_inc(S.sq_done, 1)

            def factors(c, h):
                act.wait_ge(S.nrm_ready, 4 * c + 2 * h + 2)
                ts = slice(CH * h, CH * h + CH)
                act.activation(eq_all[:, bass.ds(NT * c + CH * h, CH), :], nrm[:, ts, 0, :], ACT.Exp, scale=-0.5)
                act.activation(vext[:, ts, :].rearrange("p t (h d) -> p t h d", d=D + 1)[:, :, :, D],
                               nrm[:, ts, 1, :], ACT.Exp, scale=-0.5)
                act.activation(ek[:, ts, :], nrm[:, ts, 1, :], ACT.Exp, scale=-0.5).then_inc(S.e_ready, 1)

            def copy_rot(c, h, k):
                copy((T_BANK if k else V_BANK)[:, :], (kT if k else qT)[:, 512 * h:512 * h + 512],
                     S.rt_done, 4 * c + 2 * h + k + 1, S.rt_copied)

            def copy_v(c, h):
                copy(V_BANK[:, :], v_sb[:, CH * h:CH * h + CH, :].rearrange("p t f -> p (t f)"),
                     S.v_done, 2 * c + h + 1, S.v_copied)

            def step(c, prev, cur, nxt):
                if cur:
                    features_k(c, 0)
                    features_k(c, 1)
                if prev:
                    copy(T_BANK[:, :], attT[:, 1, :], S.at_done, 2 * c, S.at_copied)
                if cur:
                    for t in range(2, 6):
                        features_k(c, t)
                if nxt:
                    copy(V_BANK[:, :], xT[:, 0:512], S.xt_done, 2 * c + 3, S.xt_copied)
                    copy(T_BANK[:, :], xT[:, 512:1024], S.xt_done, 2 * c + 4, S.xt_copied)
                if cur:
                    features_k(c, 6)
                    features_k(c, 7)
                    features_q(c, 0)
                if nxt:
                    copy_v(c + 1, 0)
                if prev:
                    copy(T_BANK[:, :], x2T[:, 0, :], S.x2t_done, 2 * c - 1, S.x2t_copied)
                if cur:
                    features_q(c, 1)
                    split_high(c, 0)
                    features_q(c, 2)
                if nxt:
                    square(c + 1, 0)
                if cur:
                    features_q(c, 3)
                    split_high(c, 1)
                if nxt:
                    square(c + 1, 1)
                if cur:
                    features_q(c, 4)
                if nxt:
                    copy_v(c + 1, 1)
                if cur:
                    features_q(c, 5)
                    split_high(c, 2)
                if prev:
                    copy(T_BANK[:, :], x2T[:, 1, :], S.x2t_done, 2 * c, S.x2t_copied)
                if cur:
                    features_q(c, 6)
                    split_high(c, 3)
                if nxt:
                    factors(c + 1, 0)
                if cur:
                    features_q(c, 7)
                if nxt:
                    copy_rot(c + 1, 0, 0)
                    copy_rot(c + 1, 0, 1)
                    square(c + 1, 2)
                    square(c + 1, 3)
                if cur:
                    copy(T_BANK[:, :], attT[:, 0, :], S.at_done, 2 * c + 1, S.at_copied)
                if nxt:
                    copy_rot(c + 1, 1, 0)
                    factors(c + 1, 1)
                    copy_rot(c + 1, 1, 1)

            step(-1, False, False, True)
            step(0, False, True, True)
            with act.Fori(1, NC - 1) as c:
                step(c, True, True, True)
            step(NC - 1, True, True, False)
            step(NC, True, False, False)

            def hot_parts(m, q):
                act.wait_ge(S.hot_ready, m + 1)
                act.activation(hot_b[:, q, :, 0, :], hot_a[:, q, :, :], ACT.Copy, scale=part1[:, 0:1])\
                    .then_inc(S.hot_part, 1)

            act.wait_ge(S.route_const, 1)
            for q in range(2):
                hot_parts(q, q)
            with act.Fori(1, TT // UN) as pair:
                for q in range(2):
                    hot_parts(2 * pair + q, q)
            act.wait_ge(S.sm_sub, 1)
            act.activation(expo, prob, ACT.Exp).then_inc(S.sm_exp, 1)

            def block_step(n, i):
                if not (isinstance(n, int) and (n < 1 or n > NB)):
                    act.wait_ge(S.h_done, n)
                    act.activation(hid_h[:, (i - 1) % 2, :], H_BANK[(i - 1) % 2][:, :], ACT.Relu)\
                        .then_inc(S.hi_ready, 1)
                if not (isinstance(n, int) and n < 2):
                    act.wait_ge(S.y_done, n - 1)
                    act.activation(y_part[:, i % 2, :], Y_BANK[i % 2][:, E:2 * E], ACT.Copy)\
                        .then_inc(S.yp_ready, 1)

            rounds(act, block_step, NB + 2, UN)

            def weigh(k, q):
                act.wait_ge(S.y_ld1 if q else S.y_ld0, 16 * (k - q) + 32)
                for t in range(CH):
                    at = bass.ds(CH * k + t, 1)
                    ins = act.activation(tile(y1, at), tile(y1, at), ACT.Copy, scale=gates[:, 0, at])
                ins.then_inc(S.u_done, 1)

            def normalise(k, q):
                act.wait_ge(S.f_bias, k + 1)
                for t in range(CH):
                    at = bass.ds(CH * k + t, 1)
                    ins = act.activation(tile(y1, at), tile(y2, at), ACT.Identity, scale=zr[:, q, t:t + 1],
                                         bias=zb[:, q, t:t + 1])
                ins.then_inc(S.f_norm, 1)

            weigh(0, 0)
            weigh(1, 1)
            with act.Fori(0, CHUNKS // 2 - 1) as pair:
                for q in range(2):
                    weigh(2 * pair + 2 + q, q)
                    normalise(2 * pair + q, q)
            for q in range(2):
                normalise(CHUNKS - 2 + q, q)

        @block.tensor
        def _(pe):
            pe.wait_ge(S.pool_const, 1)

            def transposes(dst, tiles, done):
                for i, src in enumerate(tiles):
                    ins = pe.transpose(dst[:, P * i:P * i + P], src, ident[:, :])
                ins.then_inc(done, 1)

            def x_transposes(c, h):
                pe.wait_ge(S.xn_ready, 2 * c + h + 1)
                transposes(T_BANK if h else V_BANK, [xn[:, CH * h + t, :] for t in range(CH)], S.xt_done)

            def project(c, p):
                pe.wait_ge(S.xt_copied, 2 * c + p // 2 + 1)
                if p >= 2 or not (isinstance(c, int) and c == 0):
                    pe.wait_ge(S.rope_read, 4 * c + p - 1)
                for t in (2 * p, 2 * p + 1):
                    ins = pe.matmul(QK_BANK[p % 2][:, 2 * E * (t % 2):2 * E * (t % 2 + 1)],
                                    xT[:, P * t:P * t + P], wqk_sb[:, :], start=True, stop=True)
                ins.then_inc(S.qk_done, 1)

            def project_v(c, h):
                if h:
                    pe.wait_ge(S.v_copied, 2 * c + 1)
                for t in range(CH):
                    ins = pe.matmul(V_BANK[:, E * t:E * t + E], xT[:, P * (CH * h + t):P * (CH * h + t) + P],
                                    wv_sb[:, :], start=True, stop=True)
                ins.then_inc(S.v_done, 1)

            def rot_transposes(c, h, k):
                transposes(T_BANK if k else V_BANK,
                           [rot[:, CH * h + t, E * k:E * k + E] for t in range(CH)], S.rt_done)

            def phi_k(c, t):
                pe.matmul(PHI_BANK[t % 2][:, :], kT[:, P * t:P * t + P],
                          sorf[:, :, :].rearrange("p h m -> p (h m)"), start=True, stop=True).then_inc(S.pk_done, 1)

            def sums(c, t):
                pe.wait_ge(S.ek_done, NT * c + t + 1)
                if t % CH == 0:
                    pe.wait_ge(S.vext_ready, 2 * c + t // CH + 1)
                if t == 0 and not (isinstance(c, int) and c == 0):
                    pe.wait_ge(S.s_ready, c)
                for g in range(NG):
                    ins = pe.matmul(S_BANK[:, W * g:W * g + W], kphi[:, t, P * g:P * g + P],
                                    vext[:, t, W * g:W * g + W], start=(t == 0 and g == 0), stop=(t == NT - 1),
                                    skip_group_check=True)
                if t == NT - 1:
                    ins.then_inc(S.s_done, 1)

            def phi_q(c, j):
                if j < 2:
                    pe.wait_ge(S.ek_done, NT * c + NT - 1 + j)
                else:
                    pe.wait_ge(S.eq_done, 2 * NG * c + j - 1)
                h, g = j // NG, j % NG
                pe.matmul(PHI_BANK[j % 2][:, :], sorf[:, HG * g:HG * g + HG, :].rearrange("p h m -> p (h m)"),
                          qT[:, 512 * h:512 * h + 512], start=True, stop=True).then_inc(S.pq_done, 1)

            def outputs(c, n):
                if n < 2:
                    pe.wait_ge(S.eq_done, 2 * NG * c + 2 * NG - 1 + n)
                else:
                    pe.wait_ge(S.nu_read, 4 * c + n - 1)
                if n == 0:
                    pe.wait_ge(S.s_ready, c + 1)
                for i in range(2):
                    t = 2 * n + i
                    for g in range(NG):
                        ins = pe.matmul(PHI_BANK[n % 2][:, NG * W * i + W * g:NG * W * i + W * g + W],
                                        qphi[:, g, P * t:P * t + P], s_sb[:, W * g:W * g + W],
                                        start=True, stop=True, skip_group_check=True)
                ins.then_inc(S.nu_done, 1)

            def att_transposes(c, h):
                pe.wait_ge(S.nu_read, 4 * c + 2 * h + 2)
                transposes(T_BANK, [att[:, CH * h + t, :] for t in range(CH)], S.at_done)

            def out_project(c, h, dst=Z_BANK):
                pe.wait_ge(S.at_copied, 2 * c + h + 1)
                for t in range(CH):
                    ins = pe.matmul(dst[:, E * t:E * t + E], attT[:, h, P * t:P * t + P], wo_sb[:, :],
                                    start=True, stop=True)
                ins.then_inc(S.z_done, 1)

            def x2_transposes(c, h):
                pe.wait_ge(S.xn2_ready, 2 * c + h + 1)
                transposes(T_BANK, [xn2[:, h, t, :] for t in range(CH)], S.x2t_done)

            def logits(c, h):
                pe.wait_ge(S.x2t_copied, 2 * c + h + 1)
                for t in range(CH):
                    ins = pe.matmul(Z_BANK[:, NX * t:NX * t + NX], x2T[:, h, P * t:P * t + P], gw_sb[:, :],
                                    start=True, stop=True)
                ins.then_inc(S.lg_done, 1)

            def step(c, prev, cur, nxt):
                for t in range(NT):
                    if cur:
                        if t == 0:
                            pe.wait_ge(S.rt_copied, 4 * c + 2)
                        if t == CH:
                            pe.wait_ge(S.rt_copied, 4 * c + 4)
                        if t >= 2:
                            pe.wait_ge(S.ek_done, NT * c + t - 1)
                        elif prev:
                            pe.wait_ge(S.nu_read, 4 * c - 1 + t)
                        phi_k(c, t)
                        if t >= 2:
                            sums(c, t - 2)
                    if prev and t == 1:
                        if cur:
                            pe.wait_ge(S.rt_copied, 4 * c + 4)
                        else:
                            pe.wait_ge(S.at_copied, 2 * c - 1)
                        att_transposes(c - 1, 1)
                    if prev and t == 4:
                        if cur:
                            pe.wait_ge(S.z_read, 2 * c - 1)
                        out_project(c - 1, 1, Z_BANK if cur else LAST_BANK)
                    if nxt and t == 5:
                        x_transposes(c + 1, 0)
                        x_transposes(c + 1, 1)
                        if not cur:
                            pe.wait_ge(S.ld_proj, 32)
                    if nxt and t >= 6:
                        project(c + 1, t - 6)
                for j in range(2 * NG):
                    if cur:
                        phi_q(c, j)
                        if j < 2:
                            sums(c, NT - 2 + j)
                    if nxt and j == 0:
                        project_v(c + 1, 0)
                    if prev and j == 0:
                        if nxt:
                            pe.wait_ge(S.xt_copied, 2 * c + 4)
                        x2_transposes(c - 1, 0)
                    if nxt and j == 2:
                        project(c + 1, 2)
                    if prev and j == 3:
                        pe.wait_ge(S.z_read, 2 * c if cur else 2 * c - 1)
                        logits(c - 1, 0)
                    if nxt and j == 4:
                        project(c + 1, 3)
                        project_v(c + 1, 1)
                    if prev and j == 5:
                        x2_transposes(c - 1, 1)
                    if prev and j == 7:
                        pe.wait_ge(S.lg_read, 2 * c - 1)
                        logits(c - 1, 1)
                if cur:
                    outputs(c, 0)
                    outputs(c, 1)
                if nxt:
                    pe.wait_ge(S.rot_ready, 4 * c + 6)
                    pe.wait_ge(S.v_copied, 2 * c + 4)
                    rot_transposes(c + 1, 0, 0)
                    rot_transposes(c + 1, 0, 1)
                if cur:
                    outputs(c, 2)
                    if nxt:
                        pe.wait_ge(S.rt_copied, 4 * c + 6)
                    att_transposes(c, 0)
                    outputs(c, 3)
                if nxt:
                    pe.wait_ge(S.rt_copied, 4 * c + 5)
                    pe.wait_ge(S.rot_ready, 4 * c + 8)
                    rot_transposes(c + 1, 1, 0)
                if cur:
                    if prev:
                        pe.wait_ge(S.lg_read, 2 * c)
                    else:
                        pe.wait_ge(S.ld_gate, 64)
                    out_project(c, 0)
                if nxt:
                    if not cur:
                        pe.wait_ge(S.rt_copied, 4 * c + 6)
                    rot_transposes(c + 1, 1, 1)

            step(-1, False, False, True)
            pe.wait_ge(S.u_ready, 1)
            pe.matmul(PHI_BANK[0][0:SP_, 0:P], had_sb[:, :], u2[:, :], start=True, stop=True).then_inc(S.t2_done, 1)
            pe.wait_ge(S.u_ready, 2)
            pe.matmul(PHI_BANK[1][:, 0:M], u3[:, :], had_sb[:, 0:M], start=True, stop=True).then_inc(S.t3_done, 1)
            pe.wait_ge(S.sorf_ready, 1)
            step(0, False, True, True)
            with pe.Fori(1, NC - 1) as c:
                step(c, True, True, True)
            step(NC - 1, True, True, False)
            step(NC, True, False, False)

            pe.wait_ge(S.masks, 1)
            pe.wait_ge(S.route_const, 1)
            pe.matmul(RANK_BANK[:, 0:TT * NX], tri16[:, :], mask16[:, :], start=True, stop=True)
            pe.matmul(TOTAL_BANK[:, 0:TT * NX], ones16[:, :], mask16[:, :], start=True, stop=True).then_inc(S.ranked, 1)

            def place(m, q, first):
                pe.wait_ge(S.hot_part, m + 1)
                pe.wait_ge(S.hot_tile, m + 1)
                for i in range(UN):
                    ins = pe.matmul(IDX_BANK[:, 0:2 * NB], hot_r[:, q, i, :],
                                    hot_b[:, q, i, :, :].rearrange("p c b -> p (c b)"),
                                    start=(first and i == 0), stop=False, skip_group_check=True)
                ins.then_inc(S.hot_used, 1)

            for q in range(2):
                place(q, q, q == 0)
            with pe.Fori(1, TT // UN) as pair:
                for q in range(2):
                    place(2 * pair + q, q, False)

            def gather_transposes(b, i):
                q = i % 2
                pe.wait_ge(s[f"g_land{i}"], landed(b, i))
                dst = XG_BANK[q][:, 0:E].bitcast(F16)
                for k in range(2):
                    ins = pe.transpose(dst[:, E * k:E * k + E], xg[:, i, E * k:E * k + E], ident16[:, :])
                ins.then_inc(S.xg_done, 1)

            def hidden(b, q, e):
                pe.wait_ge(S.xg_copied, b + 1)
                pe.matmul(H_BANK[q][:, :], b1_all[:, :],
                          sel1[:, bass.ds(e, 1), :, :].rearrange("p o c t -> p (o c t)"),
                          start=True, stop=False, skip_group_check=True)
                for c in range(HC):
                    dst = H_BANK[q][:, P * c:P * c + P]
                    high = w1h[:, bass.ds(e, 1), P * c:P * c + P].rearrange("p o f -> p (o f)")
                    low = w1l[:, bass.ds(e, 1), P * c:P * c + P].rearrange("p o f -> p (o f)")
                    pe.matmul(dst, high, xgT[:, q, 0:E], start=False, stop=False, skip_group_check=True)
                    pe.matmul(dst, high, xgT[:, q, E:2 * E], start=False, stop=False, skip_group_check=True)
                    ins = pe.matmul(dst, low, xgT[:, q, 0:E], start=False, stop=True, skip_group_check=True)
                ins.then_inc(S.h_done, 1)

            def output(b, q, e):
                pe.wait_ge(S.lo_ready, b + 1)
                dst = Y_BANK[q]
                for c in range(HC):
                    both = w2s[:, bass.ds(e, 1), c, :, :].rearrange("p o h f -> p (o h f)")
                    high = w2s[:, bass.ds(e, 1), c, 0, :].rearrange("p o f -> p (o f)")
                    pe.matmul(dst[:, 0:2 * E], hid_h[:, q, P * c:P * c + P], both,
                              start=(c == 0), stop=False, skip_group_check=True)
                    pe.matmul(dst[:, 0:E], hid_l[:, q, P * c:P * c + P], high, start=False, stop=False,
                              skip_group_check=True)
                pe.matmul(dst[:, 0:E], sel2[:, bass.ds(e, 1), :].rearrange("p o t -> p (o t)"), b2_all[:, :],
                          start=False, stop=True, skip_group_check=True).then_inc(S.y_done, 1)

            pe.wait_ge(S.eb_ready, 1)
            pe.wait_ge(S.sel_ready, 1)
            pe.wait_ge(S.bias_ready, 1)
            expert_of = {}

            def block_step(n, i):
                if not (isinstance(n, int) and n >= NB):
                    gather_transposes(n, i)
                if not (isinstance(n, int) and (n < 1 or n > NB)):
                    hidden(n - 1, (i - 1) % 2, expert_of[i - 1])
                if not (isinstance(n, int) and n < 2):
                    output(n - 2, i % 2, expert_of[i - 2])

            def expert_round(n, count):
                at = slice(n // UN, n // UN + 1) if isinstance(n, int) else bass.ds(n // UN, 1)
                _, (word,) = nc.values_load_multi_w_load_instructions(
                    words_i[0:1, at], engines=(pe.engine,), min_val=0, max_val=NX ** (UN + 1) - 1)
                for k in range(UN + 1):
                    expert_of[k - 2] = pe.snap((word >> (3 * k)) & (NX - 1))

            rounds(pe, block_step, NB + 2, UN, expert_round)

        @block.vector
        def _(dve):
            done = [0]
            base = [0]

            def mark(ins):
                ins.then_inc(S.dve_done, 1)
                done[0] += 1

            def settle():
                dve.wait_ge(S.dve_done, base[0] + done[0])

            def statistics(tiles, st, m, v, h, ready):
                for t, src in enumerate(tiles):
                    ins = dve.bn_stats(st[:, h, t, :], src)
                mark(ins)
                settle()
                dve.tensor_copy(carrier[:, 0:1], mhalf[:, 0:1])
                for t in range(CH):
                    ins = dve.bn_aggr(m[:, h, t, :], st[:, h, t, :])
                mark(ins)
                settle()
                dve.tensor_scalar(v[:, h, :], m[:, h, :, 1], LN_EPS, None, ALU.add).then_inc(ready, 1)

            def normalise(dst, src, m, r, h, finished):
                for t in range(CH):
                    ins = dve.tensor_scalar(dst[t], src[t], m[:, h, t, 0:1], r[:, h, t:t + 1],
                                            ALU.subtract, ALU.mult)
                ins.then_inc(finished, 1)

            def x_tiles(c, h):
                return [x_sb[:, bass.ds(NT * c + CH * h + t, 1), :].rearrange("p o e -> p (o e)")
                        for t in range(CH)]

            def rope(c, p):
                dve.wait_ge(S.qk_done, 4 * c + p + 1)
                if p >= 2:
                    dve.wait_ge(S.rot_ready, 4 * c + p - 1)
                elif not (isinstance(c, int) and c == 0):
                    dve.wait_ge(S.rot_ready, 4 * c + p - 1)
                qk = QK_BANK[p % 2]
                ts = slice(2 * p, 2 * p + 2)
                dve.tensor_tensor(rc[:, p % 2, :].rearrange("p (t a f) -> p t a f", t=2, a=2),
                                  qk[:, :].rearrange("p (t a f) -> p t a f", t=2, a=2),
                                  bc(cos_sb[:, ts, :], 2, 2), ALU.mult)
                swapped = qk[:, :].rearrange("p (a h f) -> p a h f", h=2, f=E // 2)
                sn = sin_sb[:, ts, :].rearrange("p t (a h f) -> p (t a) h f", h=2, f=E // 2)
                dst = rs_[:, p % 2, :].rearrange("p (a h f) -> p a h f", h=2, f=E // 2)
                for h in range(2):
                    ins = dve.tensor_tensor(dst[:, :, h, :], swapped[:, :, 1 - h, :], sn[:, :, h, :], ALU.mult)
                ins.then_inc(S.rope_read, 1)

            def squares(c, p):
                dve.wait_ge(S.sq_done, 4 * c + p + 1)
                dve.tensor_reduce(
                    nrm[:, 2 * p:2 * p + 2, :, :].rearrange("p t a h -> p (t a) h"),
                    sq[:, p % 2, :].rearrange("p (a s h i) -> p a h s i", a=4, s=2, i=HALF),
                    AX.XY, ALU.add).then_inc(S.nrm_ready, 1)

            def mask_sums(c):
                dve.wait_ge(S.s_done, c + 1)
                dve.tensor_tensor(s_sb[:, :].rearrange("p (g w) -> p g w", g=NG),
                                  S_BANK[:, 0:NG * W].rearrange("p (g w) -> p g w", g=NG),
                                  bc(sm_sb[:, :], 1, NG), ALU.mult).then_inc(S.s_ready, 1)

            def divide(c, n):
                dve.wait_ge(S.nu_done, 4 * c + n + 1)
                nu = PHI_BANK[n % 2][:, 0:2 * NG * W].rearrange("p (t h d) -> p t h d", t=2, d=D + 1)
                eqs = eq_all[:, bass.ds(NT * c + 2 * n, 2), :]
                d0, d1, d2, d3 = (den[:, n % 2, k, :, :] for k in range(4))
                mark(dve.scalar_tensor_tensor(out=d0, in0=nu[:, :, :, D], scalar=1.0 / M, in1=eqs,
                                              op0=ALU.mult, op1=ALU.mult))
                settle()
                mark(dve.tensor_scalar(d1, d0, DEN_EPS, None, ALU.max))
                settle()
                mark(dve.reciprocal(d2, d1))
                settle()
                mark(dve.scalar_tensor_tensor(out=d3, in0=d2, scalar=1.0 / M, in1=eqs,
                                              op0=ALU.mult, op1=ALU.mult))
                settle()
                dve.tensor_tensor(
                    att[:, 2 * n:2 * n + 2, :].rearrange("p t (h d) -> p (t h) d", d=D),
                    nu.rearrange("p t h d -> p (t h) d")[:, :, 0:D],
                    bc(d3.rearrange("p t h -> p (t h)"), 2, D), ALU.mult).then_inc(S.nu_read, 1)

            def z_statistics(c, h, src=Z_BANK):
                dve.wait_ge(S.z_done, 2 * c + h + 1)
                statistics([src[:, E * t:E * t + E] for t in range(CH)], zst, zmv, zvp, h, S.z_var)

            def z_normalise(c, h, src=Z_BANK):
                dve.wait_ge(S.z_rstd, 2 * c + h + 1)
                normalise([z_sb[:, h, t, :] for t in range(CH)], [src[:, E * t:E * t + E] for t in range(CH)],
                          zmv, zr, h, S.z_read)

            def x2_tiles(c, h):
                return [x2_sb[:, bass.ds(NT * c + CH * h + t, 1), :].rearrange("p o e -> p (o e)")
                        for t in range(CH)]

            def y_statistics(c, h):
                dve.wait_ge(S.x2_ready, 2 * c + h + 1)
                statistics(x2_tiles(c, h), yst, ymv, yvp, h, S.y_var)

            def y_normalise(c, h):
                dve.wait_ge(S.y_rstd, 2 * c + h + 1)
                normalise([xn2[:, h, t, :] for t in range(CH)], x2_tiles(c, h), ymv, yr, h, S.xn2_ready)
                dve.wait_ge(S.xn2_ready, 2 * c + h + 1)
                if not (isinstance(c, int) and c == 0):
                    dve.wait_ge(S.hl_st1 if h else S.hl_st0, 16 * c)
                mark(dve.tensor_copy(hl[:, h, :, 0:E], xn2[:, h, :, :]))
                settle()
                dve.tensor_tensor(hl[:, h, :, E:2 * E], xn2[:, h, :, :], hl[:, h, :, 0:E],
                                  ALU.subtract).then_inc(S.hl_ready, 1)

            def read_logits(c, h):
                dve.wait_ge(S.lg_done, 2 * c + h + 1)
                dve.tensor_tensor(logit[:, bass.ds(NT * c + CH * h, CH), :],
                                  Z_BANK[:, 0:NX * CH].rearrange("p (t e) -> p t e", e=NX),
                                  bc(gb_sb[:, :], 1, CH), ALU.add).then_inc(S.lg_read, 1)

            def step(c, prev, cur, nxt):
                if prev:
                    z_statistics(c - 1, 0)
                if nxt:
                    for h in range(2):
                        statistics(x_tiles(c + 1, h), bst, mv, vpe, h, S.ln1_var)
                if prev:
                    z_normalise(c - 1, 0)
                if nxt:
                    for h in range(2):
                        dve.wait_ge(S.ln1_rstd, 2 * c + 3 + h)
                        normalise([xn[:, CH * h + t, :] for t in range(CH)], x_tiles(c + 1, h), mv, rstd, h,
                                  S.xn_ready)
                if prev:
                    y_statistics(c - 1, 0)
                    z_statistics(c - 1, 1, Z_BANK if cur else LAST_BANK)
                if nxt:
                    rope(c + 1, 0)
                if prev:
                    y_normalise(c - 1, 0)
                if nxt:
                    rope(c + 1, 1)
                if prev:
                    z_normalise(c - 1, 1, Z_BANK if cur else LAST_BANK)
                if nxt:
                    squares(c + 1, 0)
                if prev:
                    y_statistics(c - 1, 1)
                if cur:
                    mask_sums(c)
                if nxt:
                    rope(c + 1, 2)
                if prev:
                    read_logits(c - 1, 0)
                    y_normalise(c - 1, 1)
                if nxt:
                    squares(c + 1, 1)
                    rope(c + 1, 3)
                if prev:
                    read_logits(c - 1, 1)
                if cur:
                    divide(c, 0)
                    divide(c, 1)
                if nxt:
                    squares(c + 1, 2)
                    squares(c + 1, 3)
                if cur:
                    divide(c, 2)
                    divide(c, 3)

            dve.memset(b2_sb[:, :], 0.0).then_inc(S.b_zero, 1)
            dve.wait_ge(S.pool_const, 1)
            dve.wait_ge(S.x_first, 16)
            for h in range(2):
                statistics(x_tiles(0, h), bst, mv, vpe, h, S.ln1_var)
            for h in range(2):
                dve.wait_ge(S.ln1_rstd, h + 1)
                normalise([xn[:, CH * h + t, :] for t in range(CH)], x_tiles(0, h), mv, rstd, h, S.xn_ready)
            dve.wait_ge(S.ld_set, 7 * 16)
            mark(dve.tensor_tensor(u1[:, :], hadp_sb[:, :], s1_sb[:, :], ALU.mult))
            settle()

            def by_head(ap):
                return ap.rearrange("k (s h i) -> k s h i", s=2, i=HALF)

            for a in range(2):
                ins = dve.tensor_tensor(by_head(u2[:, :])[:, a], by_head(u1[:, :])[:, a],
                                        bc(s2_sb[:, :], 2, HALF), ALU.mult)
            ins.then_inc(S.u_ready, 1)
            dve.wait_ge(S.ld_cos, 32)
            dve.wait_ge(S.ld_sin, 32)
            rope(0, 0)
            rope(0, 1)
            squares(0, 0)
            squares(0, 1)
            rope(0, 2)
            rope(0, 3)
            squares(0, 2)
            squares(0, 3)
            dve.wait_ge(S.t2_done, 1)
            for a in range(2):
                ins = dve.tensor_tensor(by_head(u3[:, :])[:, a], by_head(PHI_BANK[0][0:SP_, 0:P])[:, a],
                                        bc(s3_sb[:, :], 2, HALF), ALU.mult)
            ins.then_inc(S.u_ready, 1)
            mark(dve.tensor_tensor(sorf[:, :, :], scl_sb[:, :].rearrange("p (h m) -> p h m", m=M),
                                   bc(hm_sb[:, :], 2, M), ALU.mult))
            dve.wait_ge(S.t3_done, 1)
            mark(dve.tensor_scalar(t3[:, :], PHI_BANK[1][:, 0:M], float(SP_) ** -2, None, ALU.mult))
            settle()
            dve.tensor_tensor(sorf[:, :, :], sorf[:, :, :], bc(t3[:, :], 1, NH), ALU.mult).then_inc(S.sorf_ready, 1)
            dve.wait_ge(S.ld_gate, 64)
            dve.wait_ge(S.x_rest, 16)
            step(0, False, True, True)
            base[0], done[0] = done[0], 0
            start = base[0]
            with dve.Fori(1, NC - 1) as c:
                base[0] = start + (c - 1) * MARKS
                step(c, True, True, True)
                assert done[0] == MARKS, done[0]
            base[0], done[0] = start + (NC - 2) * MARKS, 0
            step(NC - 1, True, True, False)
            step(NC, True, False, False)

            def link(ins):
                mark(ins)
                settle()

            def choose(src, one, k):
                link(dve.tensor_reduce(red[:, k, :], src, AX.X, ALU.max))
                link(dve.tensor_tensor(tokens(hit), src, bc(red[:, k, :], 2, NX), ALU.is_equal))
                link(dve.tensor_tensor(tokens(cand), tokens(hit), bc(tie[:, :], 1, TT), ALU.mult))
                link(dve.tensor_reduce(red[:, 2 + k, :], tokens(cand), AX.X, ALU.max))
                link(dve.tensor_tensor(tokens(one), tokens(cand), bc(red[:, 2 + k, :], 2, NX), ALU.is_equal))

            dve.wait_ge(S.route_const, 1)
            dve.wait_ge(S.lg_read, 2 * NC)
            lg = logit[:, :, :]
            pr, ex = tokens(prob), tokens(expo)
            choose(lg, one1, 0)
            link(dve.scalar_tensor_tensor(out=prob2, in0=one1, scalar=-FAR,
                                          in1=lg.rearrange("p t e -> p (t e)"), op0=ALU.mult, op1=ALU.add))
            choose(tokens(prob2), one2, 1)
            dve.tensor_tensor(mask16[:, :], one1, one2, ALU.add).then_inc(S.masks, 1)
            dve.wait_ge(S.ranked, 1)
            link(dve.tensor_copy(experts(tot), TOTAL_BANK[:, 0:TT * NX].rearrange("p (t e) -> p e t", e=NX)))
            link(dve.tensor_tensor_scan(cum, fresh[:, :], tot, 0.0, ALU.mult, ALU.add))
            dve.tensor_copy(count[:, :], experts(cum)[:, :, TT - 1])
            link(dve.tensor_tensor(excl, cum, tot, ALU.subtract))
            link(dve.tensor_tensor(experts(cmp8), bc(count[:, :], 2, TT), bc(steps128[:, :], 1, NX), ALU.is_gt))
            link(dve.tensor_reduce(nblk[:, :], experts(cmp8), AX.X, ALU.add))
            link(dve.tensor_tensor_scan(bend[:, :], ones8[:, :], nblk[:, :], 0.0, ALU.mult, ALU.add))
            link(dve.tensor_tensor(eb3[:, :, :], bc(iota_bf[:, :], 2, NX), bc(bend[0:1, :], 1, NB), ALU.is_ge))
            link(dve.tensor_reduce(ebf[:, :], eb3[:, :, :], AX.X, ALU.add))
            link(dve.tensor_scalar(ebp[:, 2:NB + 2], ebf[:, :], float(NX - 1), None, ALU.min))
            of_round = [ebp[:, k:k + UN * (ROUNDS - 1) + 1:UN] for k in range(UN + 1)]
            words = of_round[UN]
            for k in range(UN - 1, -1, -1):
                part = words_f[:, k % 2, :]
                link(dve.scalar_tensor_tensor(out=part, in0=words, scalar=float(NX), in1=of_round[k],
                                              op0=ALU.mult, op1=ALU.add))
                words = part
            dve.tensor_copy(words_i[:, :], words).then_inc(S.eb_ready, 1)
            link(dve.tensor_tensor(nblk[:, :], bend[:, :], nblk[:, :], ALU.subtract))
            link(dve.scalar_tensor_tensor(out=experts(cmp8), in0=bc(nblk[:, :], 2, TT), scalar=float(P),
                                          in1=experts(excl), op0=ALU.mult, op1=ALU.add))
            link(dve.tensor_tensor(tokens(slot3), RANK_BANK[:, 0:TT * NX].rearrange("p (t e) -> p t e", e=NX),
                                   cmp8.rearrange("p (e t) -> p t e", e=NX), ALU.add))
            for k, one in enumerate((one1, one2)):
                link(dve.tensor_tensor(hit, one, slot3, ALU.mult))
                link(dve.tensor_reduce(slots[:, k, :], tokens(hit), AX.X, ALU.add))
            link(dve.tensor_copy(slot_i[:, :, :], slots[:, :, :]))
            dve.tensor_scalar(blk_i[:, :, :], slot_i[:, :, :], 7, None, ALU.arith_shift_right)
            link(dve.tensor_scalar(row_i[:, :, :], slot_i[:, :, :], P - 1, None, ALU.bitwise_and))
            dve.tensor_copy(blk[:, :], blk_i[:, :, :].rearrange("p k t -> p (k t)"))
            link(dve.tensor_copy(row[:, :], row_i[:, :, :].rearrange("p k t -> p (k t)")))

            def make_hot(m, q):
                if not (isinstance(m, int) and m < 2):
                    dve.wait_ge(S.hot_used, m - 1)
                for i in range(UN):
                    at = slice(UN * m + i, UN * m + i + 1) if isinstance(m, int) else bass.ds(UN * m + i, 1)
                    dve.tensor_scalar(hot_a[:, q, i, :], iota_b[:, :], blk[:, at], None, ALU.is_equal)
                    ins = dve.tensor_scalar(hot_r[:, q, i, :], iota_r[:, :], row[:, at], None, ALU.is_equal)
                ins.then_inc(S.hot_ready, 1)

            for q in range(2):
                make_hot(q, q)
            with dve.Fori(1, TT // UN) as pair:
                for q in range(2):
                    make_hot(2 * pair + q, q)
            dve.wait_ge(S.hot_used, 2 * TT // UN)
            v, w, a, b_, c_, d_ = (ix[:, i, :] for i in range(6))
            link(dve.tensor_copy(w, IDX_BANK[:, 0:NB]))
            link(dve.scalar_tensor_tensor(out=v, in0=IDX_BANK[:, NB:2 * NB], scalar=float(P), in1=w,
                                          op0=ALU.mult, op1=ALU.add))
            dve.tensor_scalar(a, v, float(N), float(N), ALU.is_gt, ALU.mult)
            link(dve.scalar_tensor_tensor(out=b_, in0=v, scalar=1.0, in1=spare[:, 0:NB],
                                          op0=ALU.is_lt, op1=ALU.mult))
            dve.tensor_tensor(c_, v, a, ALU.subtract)
            link(dve.tensor_tensor(d_, v, b_, ALU.add))
            dve.tensor_scalar(idx[:, 0, :], c_, -1.0, 0.0, ALU.add, ALU.max)
            link(dve.tensor_scalar(idx[:, 1, :], d_, -1.0, None, ALU.add))

            def block_step(n, i):
                q = i % 2
                if not (isinstance(n, int) and n >= NB):
                    dve.wait_ge(S.xg_done, n + 1)
                    dve.tensor_copy(xgT[:, q, :], XG_BANK[q][:, 0:E].bitcast(F16)).then_inc(S.xg_copied, 1)
                    if not (isinstance(n, int) and n >= NB - UN):
                        next_rows(bass.ds(n + UN, 1), i)
                if not (isinstance(n, int) and (n < 1 or n > NB)):
                    dve.wait_ge(S.hi_ready, n)
                    dve.scalar_tensor_tensor(out=hid_l[:, 1 - q, :], in0=H_BANK[1 - q][:, :], scalar=0.0,
                                             in1=hid_h[:, 1 - q, :], op0=ALU.max, op1=ALU.subtract)\
                        .then_inc(S.lo_ready, 1)
                if not (isinstance(n, int) and n < 2):
                    dve.wait_ge(S.yp_ready, n - 1)
                    k = (i - 2) % UN
                    if not (isinstance(n, int) and n < UN + 2):
                        dve.wait_ge(s[f"s_land{k}"], scattered(n - 2, k))
                    dve.tensor_copy(sca_i[:, k:k + 1], idx[:, 1, bass.ds(n - 2, 1)])
                    dve.tensor_tensor(y_sb[:, k, :], Y_BANK[q][:, 0:E], y_part[:, q, :], ALU.add)\
                        .then_inc(S.y_ready, 1)

            def next_rows(at, i):
                dve.tensor_copy(gat_i[:, i:i + 1], idx[:, 0, at]).then_inc(S.gi_ready, 1)

            for b in range(UN):
                next_rows(slice(b, b + 1), b)
            dve.wait_ge(S.ld_b, 64)
            for src, high, dst in ((b1_sb, b1_h, b1_all), (b2_sb, b2_h, b2_all)):
                link(dve.tensor_copy(high[:, :], src[:, :]))
                dve.tensor_copy(dst[0:32, :], src[0:32, :])
                ins = dve.tensor_tensor(dst[32:64, :], src[32:64, :], high[32:64, :], ALU.subtract)
            ins.then_inc(S.bias_ready, 1)
            dve.tensor_tensor(pr, lg, bc(red[:, 0, :], 2, NX), ALU.subtract).then_inc(S.sm_sub, 1)
            dve.wait_ge(S.sm_exp, 1)
            link(dve.tensor_reduce(red[:, 4, :], ex, AX.X, ALU.add))
            link(dve.reciprocal(red[:, 5, :], red[:, 4, :]))
            link(dve.tensor_tensor(pr, ex, bc(red[:, 5, :], 2, NX), ALU.mult))
            for k, one in enumerate((one1, one2)):
                link(dve.tensor_tensor(hit, one, prob, ALU.mult))
                link(dve.tensor_reduce(gates[:, k, :], tokens(hit), AX.X, ALU.add))
            rounds(dve, block_step, NB + 2, 2 * UN)

            def combine(k, q):
                dve.wait_ge(S.u_done, k + 1)
                for t in range(CH):
                    at = bass.ds(CH * k + t, 1)
                    ins = dve.scalar_tensor_tensor(out=tile(y2, at), in0=tile(y2, at), scalar=gates[:, 1, at],
                                                   in1=tile(y1, at), op0=ALU.mult, op1=ALU.add)
                mark(ins)
                settle()
                dve.tensor_copy(carrier[:, 0:1], mhalf[:, 0:1])
                statistics([tile(y2, bass.ds(CH * k + t, 1)) for t in range(CH)], zst, zmv, zvp, q, S.f_var)

            def shift(k, q):
                if not (isinstance(k, int) and k < 2):
                    dve.wait_ge(S.f_norm, k - 1)
                dve.wait_ge(S.f_rstd, k + 1)
                dve.scalar_tensor_tensor(out=zb[:, q, :], in0=zmv[:, q, :, 0], scalar=-1.0, in1=zr[:, q, :],
                                         op0=ALU.mult, op1=ALU.mult).then_inc(S.f_bias, 1)

            for k in range(2):
                combine(k, k)
            shift(0, 0)
            combine(2, 0)
            shift(1, 1)
            combine(3, 1)
            base[0] += done[0]
            done[0] = 0
            start = base[0]
            with dve.Fori(1, CHUNKS // 2 - 1) as pair:
                base[0] = start + (pair - 1) * FINISH_MARKS
                for q in range(2):
                    shift(2 * pair + q, q)
                    combine(2 * pair + 2 + q, q)
                assert done[0] == FINISH_MARKS, done[0]
            for q in range(2):
                shift(CHUNKS - 2 + q, q)


MARKS = 30
FINISH_MARKS = 6
FAR = 1e30
LAG = 6


def tile(t, at):
    return t[:, at, :].rearrange("p o e -> p (o e)")


def rounds(engine, step, end, head, before=None):
    loops = (NB - UN) // UN
    for start in range(0, head, UN):
        if before:
            before(start, UN)
        for i in range(UN):
            step(start + i, i)
    with engine.Fori(head // UN, loops) as k:
        m = UN * k
        if before:
            before(m, UN)
        for i in range(UN):
            step(m + i, i)
    for start in range(UN * loops, end, UN):
        count = min(UN, end - start)
        if before:
            before(start, count)
        for i in range(count):
            step(start + i, i)


def landed(b, i):
    return (b - i) * (16 // UN) + 16


def scattered(b, i):
    return (b - i) * (16 // UN)


def _constants():
    had = np.ones((1, 1), np.float32)
    while had.shape[0] < SP_:
        had = np.block([[had, had], [had, -had]]).astype(np.float32)
    rows = np.arange(P)
    half, head, i = rows // (P // 2), rows // HALF % NH, rows % HALF
    hadp = np.ascontiguousarray(had[:, 2 * i + half])
    hmask = (head[:, None] == np.arange(NH)).astype(np.float32)
    smask = (rows[:, None] // M == np.arange(W) // (D + 1)).astype(np.float32)
    freqs = (np.float32(10000.0) ** (-np.arange(0, D, 2, dtype=np.float32) / np.float32(D))).astype(np.float32)
    ang = np.maximum(np.arange(L, dtype=np.float32) - 1, 0)[:, None] * freqs
    cos, sin = np.cos(ang), np.sin(ang)
    cost = np.tile(cos, (1, P // HALF))
    sint = np.concatenate([np.tile(-sin, (1, NH)), np.tile(sin, (1, NH))], axis=1)

    def tiles(a):
        return np.ascontiguousarray(a.reshape(NT, P, P).transpose(1, 0, 2).astype(np.float32))

    return dict(had=had, hadp=hadp, hmask=hmask, smask=smask, cost=tiles(cost), sint=tiles(sint))


def kernel(L0_attn_x, L0_attn_w_qkv, L0_attn_w_out, L0_attn_sorf_signs, L0_attn_sorf_scales,
           L0_ffn_gate_w, L0_ffn_gate_b, L0_ffn_w1, L0_ffn_b1, L0_ffn_w2, L0_ffn_b2):
    import concourse.bacc as bacc
    from concourse.bass_utils import run_bass_kernel_spmd

    a = {k: np.asarray(v) for k, v in dict(
        x=L0_attn_x, qkv=L0_attn_w_qkv, wo=L0_attn_w_out, signs=L0_attn_sorf_signs,
        scales=L0_attn_sorf_scales, gate_w=L0_ffn_gate_w, gate_b=L0_ffn_gate_b, w1=L0_ffn_w1,
        b1=L0_ffn_b1, w2=L0_ffn_w2, b2=L0_ffn_b2).items()}
    qk = a["qkv"][:2 * E].reshape(2, NH, HALF, 2, E).transpose(4, 0, 3, 1, 2).reshape(E, 2 * E)
    signs = a["signs"][:, 0]
    arrays = dict(
        x=a["x"].reshape(N, E), wqk=qk, wv=a["qkv"][2 * E:].T, wo=a["wo"].T,
        sgn1=signs[:, 0, :D].reshape(NH, HALF, 2).transpose(2, 0, 1).reshape(1, P),
        sgn2=signs[:, 1].T, sgn3=signs[:, 2].T, scl=a["scales"][:, 0, :M].reshape(1, NH * M),
        gate_w=a["gate_w"].T, gate_b=a["gate_b"].reshape(1, NX), w1=a["w1"],
        b1=a["b1"], w2=a["w2"], b2=a["b2"], **_constants())
    nc = bacc.Bacc("TRN2", target_bir_lowering=False, num_devices=1)
    named = {f"in_{k}": np.ascontiguousarray(v) for k, v in arrays.items()}
    args = [nc.dram_tensor(k, v.shape, mybir.dt.from_np(v.dtype), kind="ExternalInput").ap()
            for k, v in named.items()]
    out = nc.dram_tensor("out", (N, E), F32, kind="ExternalOutput").ap()
    sandwich_kernel(nc, *args, out)
    got = run_bass_kernel_spmd(nc, [named], core_ids=[0])
    return got.results[0]["out"].reshape(NC, L, E)
```

```python
from contextlib import ExitStack

import numpy as np

import concourse.bass as bass
from concourse import mybir

F32 = mybir.dt.float32
F16 = mybir.dt.float16
I32 = mybir.dt.int32
U32 = mybir.dt.uint32
ALU = mybir.AluOpType
ACT = mybir.ActivationFunctionType
AX = mybir.AxisListType

P = 128
NC, L, E = 4, 1024, 128
NT = L // P
CH = 4
NH, D, M = 16, 8, 32
HG = P // M
NG = NH // HG
W = HG * (D + 1)
HD = 64
HALF = D // 2
GH = HG * HALF
SLOTS = 4
NX, HID = 8, 512
HC = HID // P
N = NC * L
TT = N // P
NB = (2 * N + NX * (P - 1)) // P
LN_EPS = 1e-5
DEN_EPS = 1e-6
CHUNKS = TT // CH
UN = 8
HB = 4
HOT = 4
SPLITS = 2 * NX // NC
ROUNDS = -(-(NB + 2) // UN)


def bc(ap, axis, n):
    shape = list(ap.shape)
    shape.insert(axis, n)
    return ap.unsqueeze(axis).to_broadcast(shape)


def sandwich_kernel(nc, x, wqk, wv, wo, sgn1, sgn2, sgn3, scl, gate_w, gate_b, w1, b1, w2, b2,
                    had, hadp, hmask, smask, cost, sint, out):
    x_d = x.rearrange("(t p) e -> p t e", p=P)
    out_d = out.rearrange("(t p) e -> p t e", p=P)
    xn_d = nc.dram_tensor("xn_rows", (N, 2 * E), F16, kind="Internal").ap()
    y_d = nc.dram_tensor("y_rows", (2 * N + UN * P, E), F32, kind="Internal").ap()
    xn_v = xn_d.rearrange("(t p) e -> p t e", p=P)
    y_v = y_d[0:2 * N, :].rearrange("(t p) e -> p t e", p=P)

    with ExitStack() as ctx:
        def sb(name, shape, dt=F32):
            return ctx.enter_context(nc.sbuf_tensor(name, shape, dt))

        def sem(name):
            return ctx.enter_context(nc.semaphore(name))

        bank = [ctx.enter_context(nc.psum_tensor(f"bank{i}", [P, 512], F32)) for i in range(8)]
        T_BANK, V_BANK, Z_BANK, S_BANK = bank[0], bank[1], bank[2], bank[3]
        QK_BANK, PHI_BANK = bank[4:6], bank[6:8]
        RT_BANK = V_BANK, QK_BANK[0], V_BANK, QK_BANK[1]
        LAST_BANK = PHI_BANK[0]

        x_sb = sb("x_sb", [P, TT, E])
        x2_sb = x_sb
        logit = sb("logit", [P, TT, NX])
        eq_all = sb("eq_all", [P, TT, NH])
        ident = sb("ident", [P, P])
        ident16 = sb("ident16", [P, P], F16)
        wqk_sb, wv_sb, wo_sb = sb("wqk_sb", [P, 2 * E]), sb("wv_sb", [P, E]), sb("wo_sb", [P, E])
        gw_sb, gb_sb = sb("gw_sb", [P, NX]), sb("gb_sb", [P, NX])
        cos_sb, sin_sb = sb("cos_sb", [P, NT, HALF]), sb("sin_sb", [P, NT, 2, E // 2])
        sorf = sb("sorf", [P, NG, HG * M], F16)
        mhalf = sb("mhalf", [P, CH])
        carrier = sb("carrier", [P, 2])
        sm_sb = sb("sm_sb", [P, W])
        qphi = sb("qphi", [P, NG, L])
        had_sb, hadp_sb = sb("had_sb", [HD, HD]), sb("hadp_sb", [HD, P])
        s1_sb, s2_sb, s3_sb = sb("s1_sb", [HD, P]), sb("s2_sb", [HD, NH]), sb("s3_sb", [HD, NH])
        hm_sb = sb("hm_sb", [P, HG])
        early = qphi[:, :, :].rearrange("p g l -> p (g l)")
        scl_sb = early[:, 0:NH * M]
        u3 = early[0:HD, 512:1024].rearrange("p (g s h x) -> p g s h x", g=NG, s=SLOTS, h=2)
        u1, u2 = early[0:HD, 1024:1024 + P], early[0:HD, 1024 + P:1024 + 2 * P]
        t3 = early[:, 1024 + 2 * P:1024 + 3 * P].rearrange("p (g m) -> p g m", g=NG)
        stage = sb("stage", [P, 2, HID])
        bst, mv = sb("bst", [P, 2, CH, 6]), sb("mv", [P, 2, CH, 2])
        vpe, rstd = sb("vpe", [P, 2, CH]), sb("rstd", [P, 2, CH])
        xn = sb("xn", [P, NT, E])
        xT = sb("xT", [P, L])
        rope_sb = sb("rope_sb", [P, 4, 512])
        rc, rs_ = rope_sb[:, 0:2, :], rope_sb[:, 2:4, :]
        rot = sb("rot", [P, 2, 512])
        rot4 = sb("rot4", [P, NT, 2, NG, SLOTS, 2 * GH], F16)
        sq = sb("sq", [P, 2, 512])
        nrm = sb("nrm", [P, NT, 2, NH])
        ek = sb("ek", [P, NT, NH])
        v_sb = sb("v_sb", [P, NT, E])
        vext = sb("vext", [P, NT, NG * W])
        qT, kT = sb("qT", [P, NG, L], F16), sb("kT", [P, NG, L], F16)
        kphi = sb("kphi", [P, NT, NH * M])
        s_sb = sb("s_sb", [P, NG * (NG + 1) * W])
        den = sb("den", [P, 2, 4, 2, NH])
        att = sb("att", [P, NT, E])
        attT = sb("attT", [P, 2, 512])
        zst, zmv = sb("zst", [P, 2, CH, 6]), sb("zmv", [P, 2, CH, 2])
        zvp, zr = sb("zvp", [P, 2, CH]), sb("zr", [P, 2, CH])
        z_sb = sb("z_sb", [P, 2, CH, E])
        yst, ymv = sb("yst", [P, 2, CH, 6]), sb("ymv", [P, 2, CH, 2])
        yvp, yr = sb("yvp", [P, 2, CH]), sb("yr", [P, 2, CH])
        xn2 = sb("xn2", [P, 2, CH, E])
        hl = sb("hl", [P, 2, CH, 2 * E], F16)
        x2T = sb("x2T", [P, 2, 512])
        w1h, w1l = sb("w1h", [P, NX, HID], F16), sb("w1l", [P, NX, HID], F16)
        w2s = sb("w2s", [P, NX, HC, 2, E], F16)
        b1_sb, b1_all = sb("b1_sb", [64, P]), sb("b1_all", [P, P], F16)
        b1_h = sb("b1_h", [64, P], F16)
        b2_sb, b2_all = sb("b2_sb", [64, P]), sb("b2_all", [P, P], F16)
        b2_h = sb("b2_h", [64, P], F16)
        sel1 = rope_sb[:, :, :].rearrange("p a f -> p (a f)").bitcast(F16)\
            .rearrange("p (x c t) -> p x c t", x=NX, c=HC)
        sel2 = kT[:, 0, :].rearrange("p (x t) -> p x t", x=NX)

        rows = kphi[:, :, :].rearrange("p t f -> p (t f)")
        prob, expo, hit, cand, one1, one2, slot3, cum = (
            rows[:, TT * NX * i:TT * NX * (i + 1)] for i in range(8))
        prob2, tot, excl, cmp8 = (rows[:, TT * NX * i:TT * NX * (i + 1)] for i in range(8, 12))
        tokens = lambda a: a.rearrange("p (t e) -> p t e", e=NX)
        experts = lambda a: a.rearrange("p (e t) -> p e t", e=NX)
        red = sb("red", [P, 6, TT])
        gates = sb("gates", [P, 2, TT])
        mask16 = sb("mask16", [P, TT * NX], F16)
        tri16, ones16 = sb("tri16", [P, P], F16), sb("ones16", [P, P], F16)
        tie, steps128, fresh = sb("tie", [P, NX]), sb("steps128", [P, TT]), sb("fresh", [P, NX * TT])
        count, nblk, bend, ones8 = (sb(n, [P, NX]) for n in ("count", "nblk", "bend", "ones8"))
        slots, slot_i = sb("slots", [P, 2, TT]), sb("slot_i", [P, 2, TT], I32)
        blk_i, row_i = sb("blk_i", [P, 2, TT], I32), sb("row_i", [P, 2, TT], I32)
        blk, row = sb("blk", [P, 2 * TT], F16), sb("row", [P, 2 * TT], F16)
        iota_r, iota_b = sb("iota_r", [P, P], F16), sb("iota_b", [P, NB], F16)
        iota_bf = sb("iota_bf", [1, NB])
        part1, jtab = sb("part1", [P, 1]), sb("jtab", [P, 2 * TT], F16)
        spare = sb("spare", [P, -(-NB // UN) * UN])
        hot = rot4[:, :, :, :, :, :].rearrange("p t a g s x -> p (t a g s x)")
        hot_r = hot[:, 0:HB * HOT * P].rearrange("p (q i r) -> p q i r", q=HB, i=HOT)
        hot_a = hot[:, HB * HOT * P:HB * HOT * (P + NB)].rearrange("p (q i b) -> p q i b", q=HB, i=HOT)
        hot_b = hot[:, HB * HOT * (P + NB):HB * HOT * (P + 3 * NB)]\
            .rearrange("p (q i c b) -> p q i c b", q=HB, i=HOT, c=2)
        eb3, ebf, ebp = sb("eb3", [1, NB, NX]), sb("ebf", [1, NB]), sb("ebp", [1, UN * (ROUNDS + 1)])
        words_f, words_i = sb("words_f", [1, 2, ROUNDS + 1]), sb("words_i", [1, ROUNDS + 1], I32)
        next_i = sb("next_i", [1, ROUNDS], I32)
        ix = sb("ix", [P, 6, NB])
        idx = sb("idx", [P, 2, NB], U32)
        gat_i, sca_i = sb("gat_i", [P, UN], U32), sb("sca_i", [P, UN], U32)
        taken = [0]

        def carve(a, b, dt=F32):
            words = a * b * (1 if dt == F32 else 2) // (1 if dt == F32 else 4)
            flat = qphi[:, :, :].rearrange("p g l -> p (g l)")[:, taken[0]:taken[0] + words]
            taken[0] += words
            return (flat if dt == F32 else flat.bitcast(dt)).rearrange("p (a b) -> p a b", a=a)

        xg, xgT = carve(UN, 2 * E, F16), carve(2, 2 * E, F16)
        hid_h, hid_l = carve(2, HID, F16), carve(2, HID, F16)
        y_part, y_sb = carve(2, E), carve(UN, E)
        XG_BANK, H_BANK, Y_BANK = bank[0:2], bank[4:6], bank[6:8]
        IDX_BANK, RANK_BANK, TOTAL_BANK = bank[2], bank[4], bank[5]
        y1 = rows.rearrange("p (t e) -> p t e", e=E)
        y2 = w2s[:, :, :, :, :].rearrange("p x c h e -> p (x c h e)").bitcast(F32)\
            .rearrange("p (t e) -> p t e", e=E)
        zm, zb = sb("zm", [P, 2, CH]), sb("zb", [P, 2, CH])

        s = {k: sem(k) for k in (
            "route_const", "sm_sub", "sm_exp", "masks", "ranked", "hot_ready", "hot_part", "hot_tile",
            "hot_used", "sel_ready", "bias_ready", "eb_ready", "gi_ready", "xg_done", "xg_copied", "h_done",
            "hi_ready", "lo_ready", "y_done", "yp_ready", "y_ready", "u_done", "f_var", "f_rstd", "f_norm",
            "o_ready", *(f"{k}_land{i}" for k in "gs" for i in range(UN)), "y_ld0", "y_ld1", "carried",
            "f_bias", "o_st", "x_first", "x_rest", "ld_set", "ld_proj", "ld_cos", "ld_sin", "ld_gate",
            "ld_w0", "ld_w1", "ld_b", "pool_const", "dve_done", "pool_own", "h_split", "l_split", "b_zero",
            "t2_done", "t3_done", "u_ready", "sorf_ready", "ln1_var", "ln1_rstd", "xn_ready", "xt_done",
            "xt_copied", "qk_done", "v_done", "rope_read", "rh_ready", "rl_ready", "slot_zero", "rot_ready",
            "sq_done", "nrm_ready", "e_ready", "v_copied", "vext_ready", "rt_done", "rt_copied", "pk_done",
            "ek_done", "s_done", "s_ready", "pq_done", "eq_done", "nu_done", "nu_read", "at_done",
            "at_copied", "z_done", "z_read", "z_var", "z_rstd", "x2_ready", "y_var", "y_rstd", "xn2_ready",
            "hl_ready", "xh_ready", "x2t_done", "x2t_copied", "lg_done", "lg_read", "hl_st0", "hl_st1")}
        S = type("Sems", (), s)

        block = ctx.enter_context(nc.Block())

        @block.sync
        def _(sp):
            sp.dma_start(x_sb[:, 0:NT, :], x_d[:, 0:NT, :]).then_inc(S.x_first, 16)
            sp.dma_start(wqk_sb[:, :], wqk).then_inc(S.ld_proj, 16)
            sp.dma_start(wv_sb[:, :], wv).then_inc(S.ld_proj, 16)
            for dst, src in ((had_sb[:, :], had), (hadp_sb[:, :], hadp), (s2_sb[:, :], sgn2),
                             (s3_sb[:, :], sgn3), (s1_sb[:, :], sgn1.to_broadcast([HD, P])),
                             (hm_sb[:, :], hmask), (scl_sb[:, :], scl.to_broadcast([P, NH * M]))):
                sp.dma_start(dst, src).then_inc(S.ld_set, 16)
            sp.dma_start(cos_sb[:, :, :], cost).then_inc(S.ld_cos, 16)
            sp.dma_start(sin_sb[:, :, :, :], sint).then_inc(S.ld_sin, 16)
            sp.dma_start(x_sb[:, NT:, :], x_d[:, NT:, :]).then_inc(S.x_rest, 16)
            for dst, src in ((wo_sb[:, :], wo), (sm_sb[:, :], smask), (gw_sb[:, :], gate_w),
                             (gb_sb[:, :], gate_b.to_broadcast([P, NX]))):
                sp.dma_start(dst, src).then_inc(S.ld_gate, 16)
            for half in range(2):
                sp.dma_start(b1_sb[32 * half:32 * half + NX * HC, :],
                             b1.rearrange("e (c m) -> (e c) m", m=P)).then_inc(S.ld_b, 16)
            sp.wait_ge(S.b_zero, 1)
            for half in range(2):
                sp.dma_start(b2_sb[32 * half:32 * half + NX, :], b2).then_inc(S.ld_b, 16)

            def weights(c, j):
                e, second = SPLITS // 2 * c + j // 2, j % 2
                if j >= 2 or not isinstance(c, int) or c > 0:
                    sp.wait_ge(S.l_split, SPLITS * c + j - 1)
                at = slice(e, e + 1) if isinstance(e, int) else bass.ds(e, 1)
                dst = stage[:, second, :]
                if second:
                    sp.dma_start(dst.rearrange("p (c o) -> p c o", c=HC),
                                 w2[at].rearrange("x (c p) o -> p (x c) o", p=P)).then_inc(S.ld_w1, 16)
                else:
                    sp.dma_start(dst, w1[at].rearrange("x p f -> p (x f)")).then_inc(S.ld_w0, 16)

            def store(c, h):
                sp.wait_ge(S.hl_ready, 2 * c + h + 1)
                sp.dma_start(xn_v[:, bass.ds(NT * c + CH * h, CH), :], hl[:, h, :, :])\
                    .then_inc(S.hl_st1 if h else S.hl_st0, 16)

            def step(c, prev, cur, nxt):
                if cur:
                    for j in range(SPLITS):
                        weights(c, j)
                if prev:
                    store(c - 1, 0)
                    store(c - 1, 1)

            step(0, False, True, True)
            with sp.Fori(1, NC - 1) as c:
                step(c, True, True, True)
            step(NC - 1, True, True, False)
            step(NC, True, False, False)
            for i in range(UN):
                sp.wait_ge(s[f"s_land{i}"], 16 * ((NB - i + UN - 1) // UN))
            def load(k, q):
                for half, dst in enumerate((y1, y2)):
                    sp.dma_start(dst[:, bass.ds(CH * k, CH), :], y_v[:, bass.ds(TT * half + CH * k, CH), :])\
                        .then_inc(S.y_ld1 if q else S.y_ld0, 16)

            load(0, 0)
            load(1, 1)
            with sp.Fori(1, CHUNKS // 2) as pair:
                for q in range(2):
                    sp.wait_ge(S.y_ld1 if q else S.y_ld0, 32 * pair)
                    load(2 * pair + q, q)
            with sp.Fori(0, CHUNKS) as k:
                sp.wait_ge(S.o_ready, k + 1)
                sp.dma_start(out_d[:, bass.ds(CH * k, CH), :], y2[:, bass.ds(CH * k, CH), :]).then_inc(S.o_st, 16)
            sp.wait_ge(S.o_st, 16 * CHUNKS)

        @block.gpsimd
        def _(pool):
            own = [0]

            def settle(ins):
                ins.then_inc(S.pool_own, 1)
                own[0] += 1
                pool.wait_ge(S.pool_own, own[0])

            settle(pool.memset(ident[:, :], 0.0))
            settle(pool.affine_select(out=ident[:, :], in_=ident[:, :], compare_op=ALU.not_equal, fill=1.0,
                                      base=0, pattern=[[-1, P]], channel_multiplier=1))
            settle(pool.memset(mhalf[:, :], -0.5))
            pool.memset(s_sb[:, :], 0.0)
            pool.tensor_copy(ident16[:, :], ident[:, :]).then_inc(S.pool_const, 1)
            pool.memset(rot4[:, :, :, :, SLOTS - 1, :].rearrange("p t a g x -> p (t a g) x"), 0.0)\
                .then_inc(S.slot_zero, 1)

            def route_constants():
                for t in (b1_all, b2_all, ones16, tri16, ones8, fresh):
                    pool.memset(t[:, :], 1.0 if t in (ones16, tri16, ones8, fresh) else 0.0)
                settle(pool.memset(ebp[:, :], 0.0))
                pool.affine_select(out=tri16[:, :], in_=tri16[:, :], compare_op=ALU.is_gt, fill=0.0,
                                   base=0, pattern=[[1, P]], channel_multiplier=-1)
                pool.affine_select(out=fresh[:, :], in_=fresh[:, :], compare_op=ALU.not_equal, fill=0.0,
                                   base=0, pattern=[[0, NX], [1, TT]], channel_multiplier=0)
                for t, pattern, b, m in (
                        (tie, [[-1, NX]], NX, 0), (steps128, [[P, TT]], 0, 0), (iota_r, [[1, P]], 0, 0),
                        (iota_b, [[1, NB]], 0, 0), (iota_bf, [[1, NB]], 0, 0), (part1, [[0, 1]], 1, 1),
                        (jtab, [[1, 2 * TT]], 0, 0), (spare, [[0, -(-NB // UN)], [P, UN]], 2 * N + 1, 1)):
                    ins = pool.iota(t[:, :], pattern, base=b, channel_multiplier=m,
                                    allow_small_or_imprecise_dtypes=True)
                ins.then_inc(S.route_const, 1)

            def selectors():
                pool.memset(sel2[:, :, :], 0.0)
                settle(pool.memset(sel1[:, :, :, :], 0.0))
                for half in range(2):
                    settle(pool.affine_select(out=sel1[:, :, :, :], in_=sel1[:, :, :, :], compare_op=ALU.not_equal,
                                              fill=1.0, base=-32 * half, channel_multiplier=1,
                                              pattern=[[-HC, NX], [-1, HC], [0, P]]))
                    ins = pool.affine_select(out=sel2[:, :, :], in_=sel2[:, :, :], compare_op=ALU.not_equal,
                                             fill=1.0, base=-32 * half, channel_multiplier=1,
                                             pattern=[[-1, NX], [0, P]])
                    settle(ins)
                pool.tensor_copy(carrier[0:1, 1:2], mhalf[0:1, 0:1]).then_inc(S.sel_ready, 1)

            def power(src, dst, h, have, value, done):
                pool.wait_ge(have, value)
                pool.tensor_tensor(dst[:, h, :], src[:, h, :], mhalf[:, :], ALU.pow).then_inc(done, 1)

            def add_rotated(c, p):
                pool.wait_ge(S.rope_read, 4 * c + p + 1)
                if p >= 2 or not (isinstance(c, int) and c == 0):
                    pool.wait_ge(S.rl_ready, 4 * c + p - 1)
                for h in range(2):
                    src = slice(h * E // 2, h * E // 2 + E // 2)
                    ins = pool.tensor_tensor(
                        rot[:, p % 2, :].rearrange("p (a g h x) -> p a g h x", a=4, g=NG, h=2)[:, :, :, h, :],
                        rc[:, p % 2, :].rearrange("p (a f) -> p a f", a=4)[:, :, src]
                        .rearrange("p a (g x) -> p a g x", g=NG),
                        rs_[:, p % 2, :].rearrange("p (a f) -> p a f", a=4)[:, :, src]
                        .rearrange("p a (g x) -> p a g x", g=NG), ALU.add)
                ins.then_inc(S.rot_ready, 1)

            def rot_low(c, p):
                pool.wait_ge(S.rh_ready, 4 * c + p + 1)
                parts = rot4[:, 2 * p:2 * p + 2, :, :, :, :].rearrange("p t a g s x -> p (t a g) s x")
                pool.tensor_tensor(parts[:, :, 1, :], rot[:, p % 2, :].rearrange("p (b x) -> p b x", x=2 * GH),
                                   parts[:, :, 0, :], ALU.subtract).then_inc(S.rl_ready, 1)

            def xn2_low(c, h):
                pool.wait_ge(S.xh_ready, 2 * c + h + 1)
                pool.tensor_tensor(hl[:, h, :, E:2 * E], xn2[:, h, :, :], hl[:, h, :, 0:E], ALU.subtract)\
                    .then_inc(S.hl_ready, 1)

            def add_x(c, h):
                pool.wait_ge(S.z_read, 2 * c + h + 1)
                pool.tensor_tensor(x2_sb[:, bass.ds(NT * c + CH * h, CH), :],
                                   x_sb[:, bass.ds(NT * c + CH * h, CH), :], z_sb[:, h, :, :],
                                   ALU.add).then_inc(S.x2_ready, 1)

            def split_low(c, j):
                e, second = SPLITS // 2 * c + j // 2, j % 2
                at = slice(e, e + 1) if isinstance(e, int) else bass.ds(e, 1)
                pool.wait_ge(S.h_split, SPLITS * c + j + 1)
                src = stage[:, second, :]
                if second:
                    pool.tensor_tensor(w2s[:, at, :, 1, :].rearrange("p x c o -> p (x c) o"),
                                       src.rearrange("p (c o) -> p c o", c=HC),
                                       w2s[:, at, :, 0, :].rearrange("p x c o -> p (x c) o"),
                                       ALU.subtract).then_inc(S.l_split, 1)
                else:
                    pool.tensor_tensor(w1l[:, at, :].rearrange("p x f -> p (x f)"), src,
                                       w1h[:, at, :].rearrange("p x f -> p (x f)"), ALU.subtract)\
                        .then_inc(S.l_split, 1)

            def scale_v(c, h):
                pool.wait_ge(S.e_ready, 2 * c + h + 1)
                pool.wait_ge(S.v_copied, 2 * c + h + 1)
                ts = slice(CH * h, CH * h + CH)
                pool.tensor_tensor(
                    vext[:, ts, :].rearrange("p t (h d) -> p (t h) d", d=D + 1)[:, :, 0:D],
                    v_sb[:, ts, :].rearrange("p t (h d) -> p (t h) d", d=D),
                    bc(ek[:, ts, :].rearrange("p t h -> p (t h)"), 2, D),
                    ALU.mult).then_inc(S.vext_ready, 1)

            def step(c, prev, cur, nxt):
                if prev:
                    power(zvp, zr, 0, S.z_var, 2 * c - 1, S.z_rstd)
                if nxt:
                    for h in range(2):
                        power(vpe, rstd, h, S.ln1_var, 2 * c + 3 + h, S.ln1_rstd)
                if isinstance(c, int) and c == 0:
                    route_constants()
                if prev:
                    add_x(c - 1, 0)
                    power(yvp, yr, 0, S.y_var, 2 * c - 1, S.y_rstd)
                    power(zvp, zr, 1, S.z_var, 2 * c, S.z_rstd)
                if nxt:
                    add_rotated(c + 1, 0)
                if prev:
                    xn2_low(c - 1, 0)
                if nxt:
                    add_rotated(c + 1, 1)
                if prev:
                    add_x(c - 1, 1)
                if nxt:
                    rot_low(c + 1, 0)
                if prev:
                    power(yvp, yr, 1, S.y_var, 2 * c, S.y_rstd)
                if nxt:
                    rot_low(c + 1, 1)
                if nxt:
                    add_rotated(c + 1, 2)
                if cur:
                    split_low(c, 0)
                if nxt:
                    add_rotated(c + 1, 3)
                if prev:
                    xn2_low(c - 1, 1)
                if cur:
                    split_low(c, 1)
                if nxt:
                    rot_low(c + 1, 2)
                    rot_low(c + 1, 3)
                    scale_v(c + 1, 0)
                if cur:
                    split_low(c, 2)
                    split_low(c, 3)
                if nxt:
                    scale_v(c + 1, 1)

            step(-1, False, False, True)
            step(0, False, True, True)
            with pool.Fori(1, NC - 1) as c:
                step(c, True, True, True)
            step(NC - 1, True, True, False)
            for h in range(2):
                power(zvp, zr, h, S.z_var, 2 * NC - 1 + h, S.z_rstd)
            for h in range(2):
                add_x(NC - 1, h)
            for h in range(2):
                power(yvp, yr, h, S.y_var, 2 * NC - 1 + h, S.y_rstd)
            for h in range(2):
                xn2_low(NC - 1, h)
            def hot_tiles(m, q):
                pool.wait_ge(S.hot_ready, m + 1)
                at = slice(HOT * m, HOT * m + HOT) if isinstance(m, int) else bass.ds(HOT * m, HOT)
                pool.tensor_tensor(hot_b[:, q, :, 1, :], hot_a[:, q, :, :], bc(jtab[:, at], 2, NB), ALU.mult)\
                    .then_inc(S.hot_tile, 1)

            selectors()
            hot_groups(pool, hot_tiles)

            for q in (S.hl_st0, S.hl_st1):
                pool.wait_ge(q, 16 * NC)

            def block_step(n, i):
                if i % 2:
                    return
                fixed = isinstance(n, int)
                gathers = [j for j in range(2) if not fixed or n + j < NB]
                scatters = [j for j in range(2) if not fixed or LAG <= n + j < NB + LAG]
                if gathers:
                    pool.wait_ge(S.gi_ready, n + gathers[-1] + 1)
                if scatters:
                    pool.wait_ge(S.y_ready, n + scatters[-1] - LAG + 1)
                if not (fixed and n == 0):
                    pool.wait_ge(S.carried, n)
                pool.tensor_tensor(carrier[0:1, 1:2], mhalf[0:1, 0:1], mhalf[0:1, 0:1], ALU.add)\
                    .then_inc(S.carried, 2)
                for j in gathers:
                    pool.indirect_dma_start(
                        out=xg[:, i + j, :], out_offset=None, in_=xn_d,
                        in_offset=bass.IndirectOffsetOnAxis(ap=gat_i[:, i + j:i + j + 1], axis=0))\
                        .then_inc(s[f"g_land{i + j}"], 16)
                for j in scatters:
                    k = (i + j - LAG) % UN
                    pool.indirect_dma_start(
                        out=y_d, out_offset=bass.IndirectOffsetOnAxis(ap=sca_i[:, k:k + 1], axis=0),
                        in_=y_sb[:, k, :], in_offset=None).then_inc(s[f"s_land{k}"], 16)

            rounds(pool, block_step, NB + LAG, 2 * UN)

            def power_f(k, q):
                pool.wait_ge(S.f_var, k + 1)
                pool.tensor_tensor(zr[:, q, :], zvp[:, q, :], mhalf[:, :], ALU.pow).then_inc(S.f_rstd, 1)
                pool.wait_ge(S.f_rstd, k + 1)
                pool.tensor_tensor(zb[:, q, :], zm[:, q, :], zr[:, q, :], ALU.mult).then_inc(S.f_bias, 1)

            def add_x2(k):
                pool.wait_ge(S.f_norm, k + 1)
                ts = bass.ds(CH * k, CH)
                pool.tensor_tensor(y2[:, ts, :], x2_sb[:, ts, :], y1[:, ts, :], ALU.add).then_inc(S.o_ready, 1)

            power_f(0, 0)
            power_f(1, 1)
            with pool.Fori(0, CHUNKS // 2 - 1) as pair:
                for q in range(2):
                    add_x2(2 * pair + q)
                    power_f(2 * pair + 2 + q, q)
            for q in range(2):
                add_x2(CHUNKS - 2 + q)

        @block.scalar
        def _(act):
            def split_high(c, j):
                e, second = SPLITS // 2 * c + j // 2, j % 2
                at = slice(e, e + 1) if isinstance(e, int) else bass.ds(e, 1)
                act.wait_ge(S.ld_w1 if second else S.ld_w0, 8 * (SPLITS * c + j - second) + 16)
                src = stage[:, second, :]
                if second:
                    act.activation(w2s[:, at, :, 0, :].rearrange("p x c o -> p (x c) o"),
                                   src.rearrange("p (c o) -> p c o", c=HC), ACT.Copy).then_inc(S.h_split, 1)
                else:
                    act.activation(w1h[:, at, :].rearrange("p x f -> p (x f)"), src, ACT.Copy)\
                        .then_inc(S.h_split, 1)

            def copy(src, dst, have, value, done):
                act.wait_ge(have, value)
                act.activation(dst, src, ACT.Copy).then_inc(done, 1)

            def features_k(c, t):
                act.wait_ge(S.pk_done, NT * c + t + 1)
                act.activation(kphi[:, t, :], PHI_BANK[t % 2][:, :], ACT.Exp).then_inc(S.ek_done, 1)

            def features_q(c, j):
                act.wait_ge(S.pq_done, 2 * NG * c + j + 1)
                h, g = j // NG, j % NG
                act.activation(qphi[:, g, 512 * h:512 * h + 512], PHI_BANK[j % 2][:, :],
                               ACT.Exp).then_inc(S.eq_done, 1)

            def square(c, p):
                act.wait_ge(S.rot_ready, 4 * c + p + 1)
                if p >= 2:
                    act.wait_ge(S.nrm_ready, 4 * c + p - 1)
                else:
                    if not (isinstance(c, int) and c == 0):
                        act.wait_ge(S.nrm_ready, 4 * c + p - 1)
                act.activation(sq[:, p % 2, :], rot[:, p % 2, :], ACT.Square).then_inc(S.sq_done, 1)

            def rot_high(c, p):
                act.wait_ge(S.rot_ready, 4 * c + p + 1)
                act.activation(rot4[:, 2 * p:2 * p + 2, :, :, 0:SLOTS:2, :].rearrange("p t a g s x -> p (t a g) s x"),
                               bc(rot[:, p % 2, :].rearrange("p (b x) -> p b x", x=2 * GH), 2, 2), ACT.Copy)\
                    .then_inc(S.rh_ready, 1)

            def factors(c, h):
                act.wait_ge(S.nrm_ready, 4 * c + 2 * h + 2)
                ts = slice(CH * h, CH * h + CH)
                act.activation(eq_all[:, bass.ds(NT * c + CH * h, CH), :], nrm[:, ts, 0, :], ACT.Exp, scale=-0.5)
                act.activation(vext[:, ts, :].rearrange("p t (h d) -> p t h d", d=D + 1)[:, :, :, D],
                               nrm[:, ts, 1, :], ACT.Exp, scale=-0.5)
                act.activation(ek[:, ts, :], nrm[:, ts, 1, :], ACT.Exp, scale=-0.5).then_inc(S.e_ready, 1)

            def copy_rot(c, p, q):
                act.wait_ge(S.rt_done, 8 * c + 4 * q + p + 1)
                act.activation((qT if q else kT)[:, :, 2 * P * p:2 * P * p + 2 * P],
                               RT_BANK[p][:, :].bitcast(F16).rearrange("p (g t) -> p g t", g=NG), ACT.Copy)\
                    .then_inc(S.rt_copied, 1)

            def copy_v(c, h):
                copy(V_BANK[:, :], v_sb[:, CH * h:CH * h + CH, :].rearrange("p t f -> p (t f)"),
                     S.v_done, 2 * c + h + 1, S.v_copied)

            def step(c, prev, cur, nxt):
                if cur:
                    features_k(c, 0)
                    copy_rot(c, 0, 1)
                    features_k(c, 1)
                    copy_rot(c, 1, 1)
                if prev:
                    copy(T_BANK[:, :], attT[:, 1, :], S.at_done, 2 * c, S.at_copied)
                if cur:
                    features_k(c, 2)
                    copy_rot(c, 2, 1)
                    features_k(c, 3)
                    copy_rot(c, 3, 1)
                    features_k(c, 4)
                    features_k(c, 5)
                if nxt:
                    copy(V_BANK[:, :], xT[:, 0:512], S.xt_done, 2 * c + 3, S.xt_copied)
                    copy(T_BANK[:, :], xT[:, 512:1024], S.xt_done, 2 * c + 4, S.xt_copied)
                if cur:
                    features_k(c, 6)
                    features_k(c, 7)
                    features_q(c, 0)
                if nxt:
                    copy_v(c + 1, 0)
                if prev:
                    copy(T_BANK[:, :], x2T[:, 0, :], S.x2t_done, 2 * c - 1, S.x2t_copied)
                if cur:
                    features_q(c, 1)
                    split_high(c, 0)
                    features_q(c, 2)
                    features_q(c, 3)
                if nxt:
                    square(c + 1, 0)
                    rot_high(c + 1, 0)
                if cur:
                    features_q(c, 4)
                if nxt:
                    copy_v(c + 1, 1)
                if cur:
                    features_q(c, 5)
                    split_high(c, 1)
                if cur:
                    features_q(c, 6)
                    features_q(c, 7)
                if nxt:
                    square(c + 1, 1)
                    rot_high(c + 1, 1)
                    square(c + 1, 2)
                    rot_high(c + 1, 2)
                if prev:
                    copy(T_BANK[:, :], x2T[:, 1, :], S.x2t_done, 2 * c, S.x2t_copied)
                if nxt:
                    copy_rot(c + 1, 0, 0)
                    factors(c + 1, 0)
                    square(c + 1, 3)
                    rot_high(c + 1, 3)
                    copy_rot(c + 1, 1, 0)
                if cur:
                    split_high(c, 2)
                if cur:
                    copy(T_BANK[:, :], attT[:, 0, :], S.at_done, 2 * c + 1, S.at_copied)
                if nxt:
                    copy_rot(c + 1, 2, 0)
                    factors(c + 1, 1)
                if cur:
                    split_high(c, 3)
                if nxt:
                    copy_rot(c + 1, 3, 0)

            act.wait_ge(S.slot_zero, 1)
            step(-1, False, False, True)
            step(0, False, True, True)
            with act.Fori(1, NC - 1) as c:
                step(c, True, True, True)
            step(NC - 1, True, True, False)
            step(NC, True, False, False)

            def hot_parts(m, q):
                act.wait_ge(S.hot_ready, m + 1)
                act.activation(hot_b[:, q, :, 0, :], hot_a[:, q, :, :], ACT.Copy, scale=part1[:, 0:1])\
                    .then_inc(S.hot_part, 1)

            act.wait_ge(S.route_const, 1)
            hot_groups(act, hot_parts)

            def block_step(n, i):
                if not (isinstance(n, int) and (n < 1 or n > NB)):
                    act.wait_ge(S.h_done, n)
                    act.activation(hid_h[:, (i - 1) % 2, :], H_BANK[(i - 1) % 2][:, :], ACT.Relu)\
                        .then_inc(S.hi_ready, 1)
                if not (isinstance(n, int) and n < 2):
                    act.wait_ge(S.y_done, n - 1)
                    act.activation(y_part[:, i % 2, :], Y_BANK[i % 2][:, E:2 * E], ACT.Copy)\
                        .then_inc(S.yp_ready, 1)
                if isinstance(n, int) and n == 5:
                    act.wait_ge(S.sm_sub, 1)
                    act.activation(expo, prob, ACT.Exp).then_inc(S.sm_exp, 1)

            rounds(act, block_step, NB + 2, UN)

            def weigh(k, q):
                act.wait_ge(S.y_ld1 if q else S.y_ld0, 16 * (k - q) + 32)
                for t in range(CH):
                    at = bass.ds(CH * k + t, 1)
                    ins = act.activation(tile(y1, at), tile(y1, at), ACT.Copy, scale=gates[:, 0, at])
                ins.then_inc(S.u_done, 1)

            def normalise(k, q):
                act.wait_ge(S.f_bias, k + 1)
                for t in range(CH):
                    at = bass.ds(CH * k + t, 1)
                    ins = act.activation(tile(y1, at), tile(y2, at), ACT.Identity, scale=zr[:, q, t:t + 1],
                                         bias=zb[:, q, t:t + 1])
                ins.then_inc(S.f_norm, 1)

            weigh(0, 0)
            weigh(1, 1)
            with act.Fori(0, CHUNKS // 2 - 1) as pair:
                for q in range(2):
                    weigh(2 * pair + 2 + q, q)
                    normalise(2 * pair + q, q)
            for q in range(2):
                normalise(CHUNKS - 2 + q, q)

        @block.tensor
        def _(pe):
            pe.wait_ge(S.pool_const, 1)

            def transposes(dst, tiles, done):
                for i, src in enumerate(tiles):
                    ins = pe.transpose(dst[:, P * i:P * i + P], src, ident[:, :])
                ins.then_inc(done, 1)

            def x_transposes(c, h):
                pe.wait_ge(S.xn_ready, 2 * c + h + 1)
                transposes(T_BANK if h else V_BANK, [xn[:, CH * h + t, :] for t in range(CH)], S.xt_done)

            def project(c, p):
                pe.wait_ge(S.xt_copied, 2 * c + p // 2 + 1)
                if p >= 2 or not (isinstance(c, int) and c == 0):
                    pe.wait_ge(S.rope_read, 4 * c + p - 1)
                for t in (2 * p, 2 * p + 1):
                    ins = pe.matmul(QK_BANK[p % 2][:, 2 * E * (t % 2):2 * E * (t % 2 + 1)],
                                    xT[:, P * t:P * t + P], wqk_sb[:, :], start=True, stop=True)
                ins.then_inc(S.qk_done, 1)

            def project_v(c, h):
                if h:
                    pe.wait_ge(S.v_copied, 2 * c + 1)
                for t in range(CH):
                    ins = pe.matmul(V_BANK[:, E * t:E * t + E], xT[:, P * (CH * h + t):P * (CH * h + t) + P],
                                    wv_sb[:, :], start=True, stop=True)
                ins.then_inc(S.v_done, 1)

            def rot_transposes(c, p, q):
                dst = RT_BANK[p][:, :].bitcast(F16)
                for g in range(NG):
                    for t in range(2):
                        at = 2 * P * g + P * t
                        ins = pe.transpose(dst[:, at:at + P],
                                           rot4[:, 2 * p + t, 1 - q, g, :, :].rearrange("p s x -> p (s x)"),
                                           ident16[:, :])
                ins.then_inc(S.rt_done, 1)

            def phi_k(c, t):
                for g in range(NG):
                    ins = pe.matmul(PHI_BANK[t % 2][:, P * g:P * g + P], kT[:, g, P * t:P * t + P], sorf[:, g, :],
                                    start=True, stop=True, skip_group_check=True)
                ins.then_inc(S.pk_done, 1)

            def sums(c, t):
                pe.wait_ge(S.ek_done, NT * c + t + 1)
                if t % CH == 0:
                    pe.wait_ge(S.vext_ready, 2 * c + t // CH + 1)
                if t == 0 and not (isinstance(c, int) and c == 0):
                    pe.wait_ge(S.s_ready, c)
                    if not (isinstance(c, int) and c == 1):
                        pe.wait_ge(S.lg_read, 2 * c - 2)
                for g in range(NG):
                    ins = pe.matmul(S_BANK[:, W * g:W * g + W], kphi[:, t, P * g:P * g + P],
                                    vext[:, t, W * g:W * g + W], start=(t == 0 and g == 0), stop=(t == NT - 1),
                                    skip_group_check=True)
                if t == NT - 1:
                    ins.then_inc(S.s_done, 1)

            def phi_q(c, j):
                if j < 2:
                    pe.wait_ge(S.ek_done, NT * c + NT - 1 + j)
                else:
                    pe.wait_ge(S.eq_done, 2 * NG * c + j - 1)
                h, g = j // NG, j % NG
                pe.matmul(PHI_BANK[j % 2][:, :], sorf[:, g, :], qT[:, g, 512 * h:512 * h + 512],
                          start=True, stop=True).then_inc(S.pq_done, 1)

            def outputs(c, n):
                if n < 2:
                    pe.wait_ge(S.eq_done, 2 * NG * c + 2 * NG - 1 + n)
                else:
                    pe.wait_ge(S.nu_read, 4 * c + n - 1)
                if n == 0:
                    pe.wait_ge(S.s_ready, c + 1)
                for i in range(2):
                    t = 2 * n + i
                    for g in range(NG):
                        ins = pe.matmul(PHI_BANK[n % 2][:, NG * W * i:NG * W * i + NG * W],
                                        qphi[:, g, P * t:P * t + P], s_sb[:, NG * W * g:NG * W * g + NG * W],
                                        start=(g == 0), stop=(g == NG - 1))
                ins.then_inc(S.nu_done, 1)

            def att_transposes(c, h):
                pe.wait_ge(S.nu_read, 4 * c + 2 * h + 2)
                transposes(T_BANK, [att[:, CH * h + t, :] for t in range(CH)], S.at_done)

            def out_project(c, h, dst=Z_BANK):
                pe.wait_ge(S.at_copied, 2 * c + h + 1)
                for t in range(CH):
                    ins = pe.matmul(dst[:, E * t:E * t + E], attT[:, h, P * t:P * t + P], wo_sb[:, :],
                                    start=True, stop=True)
                ins.then_inc(S.z_done, 1)

            def second_transform():
                pe.wait_ge(S.u_ready, 1)
                pe.matmul(PHI_BANK[0][0:HD, 0:P], had_sb[:, :], u2[:, :], start=True, stop=True)\
                    .then_inc(S.t2_done, 1)

            def third_transform():
                pe.wait_ge(S.u_ready, 2)
                for g in range(NG):
                    ins = pe.matmul(PHI_BANK[1][:, M * g:M * g + M],
                                    u3[:, g, :, :, :].rearrange("p s h x -> p (s h x)"),
                                    had_sb[:, 0:M], start=True, stop=True, skip_group_check=True)
                ins.then_inc(S.t3_done, 1)

            def x2_transposes(c, h):
                pe.wait_ge(S.xn2_ready, 2 * c + h + 1)
                transposes(T_BANK, [xn2[:, h, t, :] for t in range(CH)], S.x2t_done)

            def logits(c, h):
                pe.wait_ge(S.x2t_copied, 2 * c + h + 1)
                for t in range(CH):
                    ins = pe.matmul((S_BANK if h else Z_BANK)[:, NX * t:NX * t + NX],
                                    x2T[:, h, P * t:P * t + P], gw_sb[:, :], start=True, stop=True)
                ins.then_inc(S.lg_done, 1)

            def step(c, prev, cur, nxt):
                for t in range(NT):
                    if cur:
                        if t % 2 == 0:
                            pe.wait_ge(S.rt_copied, 8 * c + t // 2 + 1)
                        if t >= 2:
                            pe.wait_ge(S.ek_done, NT * c + t - 1)
                        elif prev:
                            pe.wait_ge(S.nu_read, 4 * c - 1 + t)
                        phi_k(c, t)
                        if t >= 2:
                            sums(c, t - 2)
                        if t < NT // 2:
                            if t % 2 == 0:
                                pe.wait_ge(S.rt_copied, 8 * c + (5 if t else 3))
                            elif t == 3:
                                pe.wait_ge(S.rt_copied, 8 * c + 4)
                            rot_transposes(c, t, 1)
                    if prev and t == 1:
                        pe.wait_ge(S.at_copied, 2 * c - 1)
                        att_transposes(c - 1, 1)
                    if prev and t == 4:
                        if cur:
                            pe.wait_ge(S.z_read, 2 * c - 1)
                        out_project(c - 1, 1, Z_BANK if cur else LAST_BANK)
                    if nxt and t == 5:
                        if cur:
                            pe.wait_ge(S.rt_copied, 8 * c + 7)
                        x_transposes(c + 1, 0)
                        x_transposes(c + 1, 1)
                        if not cur:
                            second_transform()
                            pe.wait_ge(S.ld_proj, 32)
                    if nxt and t >= 6:
                        if cur and t == 7:
                            pe.wait_ge(S.rt_copied, 8 * c + 8)
                        project(c + 1, t - 6)
                for j in range(2 * NG):
                    if cur:
                        if j == 0:
                            pe.wait_ge(S.rt_copied, 8 * c + 8)
                        phi_q(c, j)
                        if j < 2:
                            sums(c, NT - 2 + j)
                    if nxt and j == 0:
                        project_v(c + 1, 0)
                    if prev and j == 0:
                        if nxt:
                            pe.wait_ge(S.xt_copied, 2 * c + 4)
                        x2_transposes(c - 1, 0)
                    if nxt and j == 2:
                        project(c + 1, 2)
                    if prev and j == 3:
                        pe.wait_ge(S.z_read, 2 * c if cur else 2 * c - 1)
                        logits(c - 1, 0)
                    if nxt and j == 4:
                        project(c + 1, 3)
                        project_v(c + 1, 1)
                if cur:
                    outputs(c, 0)
                    outputs(c, 1)
                if prev:
                    pe.wait_ge(S.x2t_copied, 2 * c - 1)
                    x2_transposes(c - 1, 1)
                if nxt:
                    pe.wait_ge(S.rl_ready, 4 * c + 5)
                    pe.wait_ge(S.v_copied, 2 * c + 4)
                    rot_transposes(c + 1, 0, 0)
                if cur:
                    outputs(c, 2)
                if nxt:
                    pe.wait_ge(S.rope_read, 4 * c + 7)
                    pe.wait_ge(S.rl_ready, 4 * c + 6)
                    rot_transposes(c + 1, 1, 0)
                    if not cur:
                        third_transform()
                if cur:
                    outputs(c, 3)
                    if prev:
                        pe.wait_ge(S.x2t_copied, 2 * c)
                    att_transposes(c, 0)
                if nxt:
                    pe.wait_ge(S.rt_copied, 8 * c + 9)
                    pe.wait_ge(S.rl_ready, 4 * c + 7)
                    rot_transposes(c + 1, 2, 0)
                if prev:
                    logits(c - 1, 1)
                if cur:
                    if prev:
                        pe.wait_ge(S.lg_read, 2 * c - 1)
                    else:
                        pe.wait_ge(S.ld_gate, 64)
                    out_project(c, 0)
                if nxt:
                    pe.wait_ge(S.rope_read, 4 * c + 8)
                    pe.wait_ge(S.rl_ready, 4 * c + 8)
                    rot_transposes(c + 1, 3, 0)

            step(-1, False, False, True)
            pe.wait_ge(S.sorf_ready, 1)
            step(0, False, True, True)
            with pe.Fori(1, NC - 1) as c:
                step(c, True, True, True)
            step(NC - 1, True, True, False)
            step(NC, True, False, False)

            pe.wait_ge(S.masks, 1)
            pe.wait_ge(S.route_const, 1)
            pe.matmul(RANK_BANK[:, 0:TT * NX], tri16[:, :], mask16[:, :], start=True, stop=True)
            pe.matmul(TOTAL_BANK[:, 0:TT * NX], ones16[:, :], mask16[:, :], start=True, stop=True)\
                .then_inc(S.ranked, 1)

            def place(m, q):
                pe.wait_ge(S.hot_part, m + 1)
                pe.wait_ge(S.hot_tile, m + 1)
                for i in range(HOT):
                    ins = pe.matmul(IDX_BANK[:, 0:2 * NB], hot_r[:, q, i, :],
                                    hot_b[:, q, i, :, :].rearrange("p c b -> p (c b)"),
                                    start=(isinstance(m, int) and m + i == 0), stop=False, skip_group_check=True)
                ins.then_inc(S.hot_used, 1)

            hot_groups(pe, place)

            def gather_transposes(b, i):
                q = i % 2
                pe.wait_ge(s[f"g_land{i}"], landed(b, i))
                dst = XG_BANK[q][:, 0:E].bitcast(F16)
                for k in range(2):
                    ins = pe.transpose(dst[:, E * k:E * k + E], xg[:, i, E * k:E * k + E], ident16[:, :])
                ins.then_inc(S.xg_done, 1)

            def hidden(b, q, e):
                pe.wait_ge(S.xg_copied, b + 1)
                pe.matmul(H_BANK[q][:, :], b1_all[:, :],
                          sel1[:, bass.ds(e, 1), :, :].rearrange("p o c t -> p (o c t)"),
                          start=True, stop=False, skip_group_check=True)
                for c in range(HC):
                    dst = H_BANK[q][:, P * c:P * c + P]
                    high = w1h[:, bass.ds(e, 1), P * c:P * c + P].rearrange("p o f -> p (o f)")
                    low = w1l[:, bass.ds(e, 1), P * c:P * c + P].rearrange("p o f -> p (o f)")
                    pe.matmul(dst, high, xgT[:, q, 0:E], start=False, stop=False, skip_group_check=True)
                    pe.matmul(dst, high, xgT[:, q, E:2 * E], start=False, stop=False, skip_group_check=True)
                    ins = pe.matmul(dst, low, xgT[:, q, 0:E], start=False, stop=True, skip_group_check=True)
                ins.then_inc(S.h_done, 1)

            def output(b, q, e, between):
                pe.wait_ge(S.lo_ready, b + 1)
                dst = Y_BANK[q]
                for c in range(HC):
                    both = w2s[:, bass.ds(e, 1), c, :, :].rearrange("p o h f -> p (o h f)")
                    high = w2s[:, bass.ds(e, 1), c, 0, :].rearrange("p o f -> p (o f)")
                    pe.matmul(dst[:, 0:2 * E], hid_h[:, q, P * c:P * c + P], both,
                              start=(c == 0), stop=False, skip_group_check=True)
                    if c == 0:
                        between()
                    pe.matmul(dst[:, 0:E], hid_l[:, q, P * c:P * c + P], high, start=False, stop=False,
                              skip_group_check=True)
                pe.matmul(dst[:, 0:E], sel2[:, bass.ds(e, 1), :].rearrange("p o t -> p (o t)"), b2_all[:, :],
                          start=False, stop=True, skip_group_check=True).then_inc(S.y_done, 1)

            pe.wait_ge(S.eb_ready, 1)
            pe.wait_ge(S.sel_ready, 1)
            pe.wait_ge(S.bias_ready, 1)
            expert_of, word = {}, []

            def unpack(k):
                if k <= UN:
                    expert_of[k - 2] = pe.snap((word[0] >> (3 * k)) & (NX - 1))

            def block_step(n, i):
                if not (isinstance(n, int) and n >= NB):
                    gather_transposes(n, i)
                if not (isinstance(n, int) and (n < 1 or n > NB)):
                    hidden(n - 1, (i - 1) % 2, expert_of[i - 1])
                if not (isinstance(n, int) and n < 2):
                    output(n - 2, i % 2, expert_of[i - 2], lambda: unpack(i + 2))
                else:
                    unpack(i + 2)

            def expert_round(n, count):
                at = slice(n // UN, n // UN + 1) if isinstance(n, int) else bass.ds(n // UN, 1)
                _, word[:] = nc.values_load_multi_w_load_instructions(
                    words_i[0:1, at], engines=(pe.engine,), min_val=0, max_val=NX ** (UN + 1) - 1)
                for k in range(2):
                    unpack(k)

            rounds(pe, block_step, NB + 2, UN, expert_round)

        @block.vector
        def _(dve):
            done = [0]
            base = [0]

            def mark(ins):
                ins.then_inc(S.dve_done, 1)
                done[0] += 1

            def settle():
                dve.wait_ge(S.dve_done, base[0] + done[0])

            def statistics(tiles, st, m, v, h, ready, minus_mean=None):
                for t, src in enumerate(tiles):
                    ins = dve.bn_stats(st[:, h, t, :], src)
                mark(ins)
                settle()
                if minus_mean is None:
                    dve.tensor_copy(carrier[:, 0:1], mhalf[:, 0:1])
                for t in range(CH):
                    ins = dve.bn_aggr(m[:, h, t, :], st[:, h, t, :])
                mark(ins)
                settle()
                if minus_mean is not None:
                    dve.tensor_scalar(minus_mean[:, h, :], m[:, h, :, 0], -1.0, None, ALU.mult)
                dve.tensor_scalar(v[:, h, :], m[:, h, :, 1], LN_EPS, None, ALU.add).then_inc(ready, 1)

            def normalise(dst, src, m, r, h, finished):
                for t in range(CH):
                    ins = dve.tensor_scalar(dst[t], src[t], m[:, h, t, 0:1], r[:, h, t:t + 1],
                                            ALU.subtract, ALU.mult)
                ins.then_inc(finished, 1)

            def x_tiles(c, h):
                return [x_sb[:, bass.ds(NT * c + CH * h + t, 1), :].rearrange("p o e -> p (o e)")
                        for t in range(CH)]

            def rope(c, p):
                dve.wait_ge(S.qk_done, 4 * c + p + 1)
                if p >= 2:
                    dve.wait_ge(S.rot_ready, 4 * c + p - 1)
                elif not (isinstance(c, int) and c == 0):
                    dve.wait_ge(S.rot_ready, 4 * c + p - 1)
                qk = QK_BANK[p % 2]
                dve.tensor_tensor(rc[:, p % 2, :].rearrange("p (t r i) -> p t r i", t=2, i=HALF),
                                  qk[:, :].rearrange("p (t r i) -> p t r i", t=2, i=HALF),
                                  bc(cos_sb[:, 2 * p:2 * p + 2, :], 2, 2 * E // HALF), ALU.mult)
                for h in range(2):
                    dst, src = (b.rearrange("p (t a h f) -> p t a h f", t=2, a=2, h=2)[:, :, :, k]
                                for b, k in ((rs_[:, p % 2, :], h), (qk[:, :], 1 - h)))
                    ins = dve.tensor_tensor(dst, src, bc(sin_sb[:, 2 * p:2 * p + 2, h, :], 2, 2), ALU.mult)
                ins.then_inc(S.rope_read, 1)

            def squares(c, p):
                dve.wait_ge(S.sq_done, 4 * c + p + 1)
                dve.tensor_reduce(
                    nrm[:, 2 * p:2 * p + 2, :, :].rearrange("p t a (g h) -> p (t a g) h", g=NG),
                    sq[:, p % 2, :].rearrange("p (b s h i) -> p b h s i", s=2, h=HG, i=HALF),
                    AX.XY, ALU.add).then_inc(S.nrm_ready, 1)

            def mask_sums(c):
                dve.wait_ge(S.s_done, c + 1)
                dve.tensor_tensor(s_sb[:, :].rearrange("p (g w) -> p g w", g=NG)[:, :, 0:W],
                                  S_BANK[:, 0:NG * W].rearrange("p (g w) -> p g w", g=NG),
                                  bc(sm_sb[:, :], 1, NG), ALU.mult).then_inc(S.s_ready, 1)

            def divide(c, n):
                dve.wait_ge(S.nu_done, 4 * c + n + 1)
                nu = PHI_BANK[n % 2][:, 0:2 * NG * W].rearrange("p (t h d) -> p t h d", t=2, d=D + 1)
                eqs = eq_all[:, bass.ds(NT * c + 2 * n, 2), :]
                d0, d1, d2, d3 = (den[:, n % 2, k, :, :] for k in range(4))
                mark(dve.scalar_tensor_tensor(out=d0, in0=nu[:, :, :, D], scalar=1.0 / M, in1=eqs,
                                              op0=ALU.mult, op1=ALU.mult))
                settle()
                mark(dve.tensor_scalar(d1, d0, DEN_EPS, None, ALU.max))
                settle()
                mark(dve.reciprocal(d2, d1))
                settle()
                mark(dve.scalar_tensor_tensor(out=d3, in0=d2, scalar=1.0 / M, in1=eqs,
                                              op0=ALU.mult, op1=ALU.mult))
                settle()
                dve.tensor_tensor(
                    att[:, 2 * n:2 * n + 2, :].rearrange("p t (h d) -> p (t h) d", d=D),
                    nu.rearrange("p t h d -> p (t h) d")[:, :, 0:D],
                    bc(d3.rearrange("p t h -> p (t h)"), 2, D), ALU.mult).then_inc(S.nu_read, 1)

            def z_statistics(c, h, src=Z_BANK):
                dve.wait_ge(S.z_done, 2 * c + h + 1)
                statistics([src[:, E * t:E * t + E] for t in range(CH)], zst, zmv, zvp, h, S.z_var)

            def z_normalise(c, h, src=Z_BANK):
                dve.wait_ge(S.z_rstd, 2 * c + h + 1)
                normalise([z_sb[:, h, t, :] for t in range(CH)], [src[:, E * t:E * t + E] for t in range(CH)],
                          zmv, zr, h, S.z_read)

            def x2_tiles(c, h):
                return [x2_sb[:, bass.ds(NT * c + CH * h + t, 1), :].rearrange("p o e -> p (o e)")
                        for t in range(CH)]

            def y_statistics(c, h):
                dve.wait_ge(S.x2_ready, 2 * c + h + 1)
                statistics(x2_tiles(c, h), yst, ymv, yvp, h, S.y_var)

            def y_normalise(c, h):
                dve.wait_ge(S.y_rstd, 2 * c + h + 1)
                normalise([xn2[:, h, t, :] for t in range(CH)], x2_tiles(c, h), ymv, yr, h, S.xn2_ready)
                dve.wait_ge(S.xn2_ready, 2 * c + h + 1)
                if not (isinstance(c, int) and c == 0):
                    dve.wait_ge(S.hl_st1 if h else S.hl_st0, 16 * c)
                dve.tensor_copy(hl[:, h, :, 0:E], xn2[:, h, :, :]).then_inc(S.xh_ready, 1)

            def read_logits(c, h):
                dve.wait_ge(S.lg_done, 2 * c + h + 1)
                dve.tensor_tensor(logit[:, bass.ds(NT * c + CH * h, CH), :],
                                  (S_BANK if h else Z_BANK)[:, 0:NX * CH].rearrange("p (t e) -> p t e", e=NX),
                                  bc(gb_sb[:, :], 1, CH), ALU.add).then_inc(S.lg_read, 1)

            def step(c, prev, cur, nxt):
                if prev:
                    z_statistics(c - 1, 0)
                if nxt:
                    for h in range(2):
                        statistics(x_tiles(c + 1, h), bst, mv, vpe, h, S.ln1_var)
                if prev:
                    z_normalise(c - 1, 0)
                if nxt:
                    for h in range(2):
                        dve.wait_ge(S.ln1_rstd, 2 * c + 3 + h)
                        normalise([xn[:, CH * h + t, :] for t in range(CH)], x_tiles(c + 1, h), mv, rstd, h,
                                  S.xn_ready)
                if prev:
                    y_statistics(c - 1, 0)
                    z_statistics(c - 1, 1, Z_BANK if cur else LAST_BANK)
                if nxt:
                    rope(c + 1, 0)
                if prev:
                    y_normalise(c - 1, 0)
                if nxt:
                    rope(c + 1, 1)
                if prev:
                    z_normalise(c - 1, 1, Z_BANK if cur else LAST_BANK)
                if nxt:
                    squares(c + 1, 0)
                if prev:
                    y_statistics(c - 1, 1)
                if cur:
                    mask_sums(c)
                if nxt:
                    rope(c + 1, 2)
                if prev:
                    read_logits(c - 1, 0)
                    y_normalise(c - 1, 1)
                if nxt:
                    squares(c + 1, 1)
                    rope(c + 1, 3)
                if cur:
                    divide(c, 0)
                    divide(c, 1)
                if nxt:
                    squares(c + 1, 2)
                    squares(c + 1, 3)
                if cur:
                    divide(c, 2)
                    divide(c, 3)
                if prev:
                    read_logits(c - 1, 1)

            dve.memset(b2_sb[:, :], 0.0).then_inc(S.b_zero, 1)
            dve.wait_ge(S.pool_const, 1)
            dve.wait_ge(S.x_first, 16)
            for h in range(2):
                statistics(x_tiles(0, h), bst, mv, vpe, h, S.ln1_var)
            for h in range(2):
                dve.wait_ge(S.ln1_rstd, h + 1)
                normalise([xn[:, CH * h + t, :] for t in range(CH)], x_tiles(0, h), mv, rstd, h, S.xn_ready)
            dve.wait_ge(S.ld_set, 7 * 16)
            mark(dve.tensor_tensor(u1[:, :], hadp_sb[:, :], s1_sb[:, :], ALU.mult))
            settle()

            def by_head(ap):
                return ap.rearrange("k (s h i) -> k s h i", s=2, i=HALF)

            for a in range(2):
                ins = dve.tensor_tensor(by_head(u2[:, :])[:, a], by_head(u1[:, :])[:, a],
                                        bc(s2_sb[:, :], 2, HALF), ALU.mult)
            ins.then_inc(S.u_ready, 1)
            dve.wait_ge(S.ld_cos, 16)
            dve.wait_ge(S.ld_sin, 16)
            rope(0, 0)
            rope(0, 1)
            dve.wait_ge(S.t2_done, 1)
            for a in range(2):
                for slot in range(SLOTS):
                    ins = dve.tensor_tensor(
                        u3[:, :, slot, a, :].rearrange("k g (h i) -> k g h i", i=HALF),
                        PHI_BANK[0][0:HD, P // 2 * a:P // 2 * a + P // 2]
                        .rearrange("k (g h i) -> k g h i", g=NG, i=HALF),
                        bc(s3_sb[:, :].rearrange("k (g h) -> k g h", g=NG), 3, HALF), ALU.mult)
            ins.then_inc(S.u_ready, 1)
            squares(0, 0)
            rope(0, 2)
            squares(0, 1)
            rope(0, 3)
            by_group = lambda ap: ap.rearrange("p (g h m) -> p g h m", g=NG, m=M)
            scaled = by_group(scl_sb[:, :])
            mark(dve.tensor_tensor(scaled, scaled, bc(bc(hm_sb[:, :], 2, M), 1, NG), ALU.mult))
            squares(0, 2)
            dve.wait_ge(S.t3_done, 1)
            mark(dve.tensor_scalar(t3[:, :, :], PHI_BANK[1][:, 0:NG * M].rearrange("p (g m) -> p g m", g=NG),
                                   float(HD) ** -2, None, ALU.mult))
            settle()
            mark(dve.tensor_tensor(scaled, scaled, bc(t3[:, :, :], 2, HG), ALU.mult))
            settle()
            flat = sorf[:, :, :].rearrange("p g f -> p (g f)")
            mark(dve.tensor_copy(flat, scl_sb[:, :]))
            settle()
            dve.tensor_tensor(flat[P // 2:, :], scl_sb[P // 2:, :], flat[P // 2:, :], ALU.subtract)\
                .then_inc(S.sorf_ready, 1)
            squares(0, 3)
            dve.wait_ge(S.ld_gate, 64)
            dve.wait_ge(S.x_rest, 16)
            step(0, False, True, True)
            base[0], done[0] = done[0], 0
            start = base[0]
            with dve.Fori(1, NC - 1) as c:
                base[0] = start + (c - 1) * MARKS
                step(c, True, True, True)
                assert done[0] == MARKS, done[0]
            base[0], done[0] = start + (NC - 2) * MARKS, 0
            step(NC - 1, True, True, False)
            halves = (0, Z_BANK), (1, LAST_BANK)
            for h, src in halves:
                z_statistics(NC - 1, h, src)
            for h, src in halves:
                z_normalise(NC - 1, h, src)
            for h, _ in halves:
                y_statistics(NC - 1, h)
            for h, _ in halves:
                y_normalise(NC - 1, h)
            dve.wait_ge(S.ld_b, 64)
            dve.wait_ge(S.route_const, 1)
            for src, high, dst in ((b1_sb, b1_h, b1_all), (b2_sb, b2_h, b2_all)):
                mark(dve.tensor_copy(high[:, :], src[:, :]))
                settle()
                dve.tensor_copy(dst[0:32, :], src[0:32, :])
                ins = dve.tensor_tensor(dst[32:64, :], src[32:64, :], high[32:64, :], ALU.subtract)
            ins.then_inc(S.bias_ready, 1)
            for h, _ in halves:
                read_logits(NC - 1, h)

            def link(ins):
                mark(ins)
                settle()

            def choose(src, one, k):
                link(dve.tensor_reduce(red[:, k, :], src, AX.X, ALU.max))
                link(dve.tensor_tensor(tokens(hit), src, bc(red[:, k, :], 2, NX), ALU.is_equal))
                link(dve.tensor_tensor(tokens(cand), tokens(hit), bc(tie[:, :], 1, TT), ALU.mult))
                link(dve.tensor_reduce(red[:, 2 + k, :], tokens(cand), AX.X, ALU.max))
                link(dve.tensor_tensor(tokens(one), tokens(cand), bc(red[:, 2 + k, :], 2, NX), ALU.is_equal))

            dve.wait_ge(S.route_const, 1)
            dve.wait_ge(S.lg_read, 2 * NC)
            lg = logit[:, :, :]
            pr, ex = tokens(prob), tokens(expo)
            choose(lg, one1, 0)
            link(dve.scalar_tensor_tensor(out=prob2, in0=one1, scalar=-FAR,
                                          in1=lg.rearrange("p t e -> p (t e)"), op0=ALU.mult, op1=ALU.add))
            choose(tokens(prob2), one2, 1)
            dve.tensor_tensor(mask16[:, :], one1, one2, ALU.add).then_inc(S.masks, 1)
            dve.wait_ge(S.ranked, 1)
            link(dve.tensor_copy(experts(tot), TOTAL_BANK[:, 0:TT * NX].rearrange("p (t e) -> p e t", e=NX)))
            link(dve.tensor_tensor_scan(cum, fresh[:, :], tot, 0.0, ALU.mult, ALU.add))
            dve.tensor_copy(count[:, :], experts(cum)[:, :, TT - 1])
            link(dve.tensor_tensor(excl, cum, tot, ALU.subtract))
            link(dve.tensor_tensor(experts(cmp8), bc(count[:, :], 2, TT), bc(steps128[:, :], 1, NX), ALU.is_gt))
            link(dve.tensor_reduce(nblk[:, :], experts(cmp8), AX.X, ALU.add))
            link(dve.tensor_tensor_scan(bend[:, :], ones8[:, :], nblk[:, :], 0.0, ALU.mult, ALU.add))
            link(dve.tensor_tensor(nblk[:, :], bend[:, :], nblk[:, :], ALU.subtract))
            link(dve.scalar_tensor_tensor(out=experts(cmp8), in0=bc(nblk[:, :], 2, TT), scalar=float(P),
                                          in1=experts(excl), op0=ALU.mult, op1=ALU.add))
            link(dve.tensor_tensor(tokens(slot3), RANK_BANK[:, 0:TT * NX].rearrange("p (t e) -> p t e", e=NX),
                                   cmp8.rearrange("p (e t) -> p t e", e=NX), ALU.add))
            for k, one in enumerate((one1, one2)):
                link(dve.tensor_tensor(hit, one, slot3, ALU.mult))
                link(dve.tensor_reduce(slots[:, k, :], tokens(hit), AX.X, ALU.add))
            link(dve.tensor_copy(slot_i[:, :, :], slots[:, :, :]))
            dve.tensor_scalar(blk_i[:, :, :], slot_i[:, :, :], 7, None, ALU.arith_shift_right)
            link(dve.tensor_scalar(row_i[:, :, :], slot_i[:, :, :], P - 1, None, ALU.bitwise_and))
            dve.tensor_copy(blk[:, :], blk_i[:, :, :].rearrange("p k t -> p (k t)"))
            link(dve.tensor_copy(row[:, :], row_i[:, :, :].rearrange("p k t -> p (k t)")))

            def make_hot(m, q):
                if not (isinstance(m, int) and m < HB):
                    dve.wait_ge(S.hot_used, m - HB + 1)
                at = slice(HOT * m, HOT * m + HOT) if isinstance(m, int) else bass.ds(HOT * m, HOT)
                dve.tensor_tensor(hot_a[:, q, :, :], bc(iota_b[:, :], 1, HOT), bc(blk[:, at], 2, NB), ALU.is_equal)
                ins = dve.tensor_tensor(hot_r[:, q, :, :], bc(iota_r[:, :], 1, HOT), bc(row[:, at], 2, P),
                                        ALU.is_equal)
                ins.then_inc(S.hot_ready, 1)

            hot_groups(dve, make_hot)
            dve.wait_ge(S.hot_used, 2 * TT // HOT)
            v, w, a, b_, c_, d_ = (ix[:, i, :] for i in range(6))
            link(dve.tensor_copy(w, IDX_BANK[:, 0:NB]))
            link(dve.scalar_tensor_tensor(out=v, in0=IDX_BANK[:, NB:2 * NB], scalar=float(P), in1=w,
                                          op0=ALU.mult, op1=ALU.add))
            dve.tensor_scalar(a, v, float(N), float(N), ALU.is_gt, ALU.mult)
            link(dve.scalar_tensor_tensor(out=b_, in0=v, scalar=1.0, in1=spare[:, 0:NB],
                                          op0=ALU.is_lt, op1=ALU.mult))
            dve.tensor_tensor(c_, v, a, ALU.subtract)
            link(dve.tensor_tensor(d_, v, b_, ALU.add))
            dve.tensor_scalar(idx[:, 0, :], c_, -1.0, 0.0, ALU.add, ALU.max)
            link(dve.tensor_scalar(idx[:, 1, :], d_, -1.0, None, ALU.add))

            def block_step(n, i):
                q = i % 2
                if not (isinstance(n, int) and n >= NB):
                    dve.wait_ge(S.xg_done, n + 1)
                    dve.tensor_copy(xgT[:, q, :], XG_BANK[q][:, 0:E].bitcast(F16)).then_inc(S.xg_copied, 1)
                    if not (isinstance(n, int) and n >= NB - UN):
                        next_rows(bass.ds(n + UN, 1), i)
                if not (isinstance(n, int) and (n < 1 or n > NB)):
                    dve.wait_ge(S.hi_ready, n)
                    dve.scalar_tensor_tensor(out=hid_l[:, 1 - q, :], in0=H_BANK[1 - q][:, :], scalar=0.0,
                                             in1=hid_h[:, 1 - q, :], op0=ALU.max, op1=ALU.subtract)\
                        .then_inc(S.lo_ready, 1)
                if not (isinstance(n, int) and n < 2):
                    dve.wait_ge(S.yp_ready, n - 1)
                    k = (i - 2) % UN
                    if not (isinstance(n, int) and n < UN + 2):
                        dve.wait_ge(s[f"s_land{k}"], scattered(n - 2, k))
                    dve.tensor_copy(sca_i[:, k:k + 1], idx[:, 1, bass.ds(n - 2, 1)])
                    dve.tensor_tensor(y_sb[:, k, :], Y_BANK[q][:, 0:E], y_part[:, q, :], ALU.add)\
                        .then_inc(S.y_ready, 1)
                if isinstance(n, int):
                    softmax(n)

            def softmax(n):
                if n == 3:
                    dve.tensor_tensor(pr, lg, bc(red[:, 0, :], 2, NX), ALU.subtract).then_inc(S.sm_sub, 1)
                if n == 6:
                    dve.wait_ge(S.sm_exp, 1)
                    link(dve.tensor_reduce(red[:, 4, :], ex, AX.X, ALU.add))
                    link(dve.reciprocal(red[:, 5, :], red[:, 4, :]))
                if n == 7:
                    mark(dve.tensor_tensor(pr, ex, bc(red[:, 5, :], 2, NX), ALU.mult))
                if n == 8:
                    settle()
                if n in (8, 9):
                    k = n - 8
                    link(dve.tensor_tensor(hit, (one1, one2)[k], prob, ALU.mult))
                    link(dve.tensor_reduce(gates[:, k, :], tokens(hit), AX.X, ALU.add))

            def next_rows(at, i):
                dve.tensor_copy(gat_i[:, i:i + 1], idx[:, 0, at]).then_inc(S.gi_ready, 1)

            for b in range(UN):
                next_rows(slice(b, b + 1), b)
            link(dve.tensor_tensor(eb3[:, :, :], bc(iota_bf[:, :], 2, NX), bc(bend[0:1, :], 1, NB), ALU.is_ge))
            link(dve.tensor_reduce(ebf[:, :], eb3[:, :, :], AX.X, ALU.add))
            link(dve.tensor_scalar(ebp[:, 2:NB + 2], ebf[:, :], float(NX - 1), None, ALU.min))
            of_round = [ebp[:, k:k + UN * ROUNDS + 1:UN] for k in range(UN)]
            words = of_round[UN - 1]
            for k in range(UN - 2, -1, -1):
                part = words_f[:, k % 2, :]
                link(dve.scalar_tensor_tensor(out=part, in0=words, scalar=float(NX), in1=of_round[k],
                                              op0=ALU.mult, op1=ALU.add))
                words = part
            link(dve.tensor_copy(words_i[:, :], words))
            link(dve.tensor_scalar(next_i[:, :], words_i[:, 1:], NX - 1, 3 * UN, ALU.bitwise_and,
                                   ALU.logical_shift_left))
            dve.tensor_tensor(words_i[:, 0:ROUNDS], words_i[:, 0:ROUNDS], next_i[:, :], ALU.bitwise_or)\
                .then_inc(S.eb_ready, 1)
            rounds(dve, block_step, NB + 2, 2 * UN)

            def combine(k, q):
                dve.wait_ge(S.u_done, k + 1)
                for t in range(CH):
                    at = slice(CH * k + t, CH * k + t + 1)
                    ins = dve.scalar_tensor_tensor(out=tile(y2, at), in0=tile(y2, at), scalar=gates[:, 1, at],
                                                   in1=tile(y1, at), op0=ALU.mult, op1=ALU.add)
                mark(ins)
                settle()
                if k >= 2:
                    dve.wait_ge(S.f_bias, k - 1)
                statistics([tile(y2, slice(CH * k + t, CH * k + t + 1)) for t in range(CH)], zst, zmv, zvp, q,
                           S.f_var, zm)

            for k in range(CHUNKS):
                combine(k, k % 2)


MARKS = 28
FAR = 1e30
LAG = 8


def tile(t, at):
    return t[:, at, :].rearrange("p o e -> p (o e)")


def hot_groups(engine, group):
    for m in range(HB):
        group(m, m)
    with engine.Fori(1, 2 * TT // HOT // HB) as k:
        for q in range(HB):
            group(HB * k + q, q)


def rounds(engine, step, end, head, before=None):
    loops = (NB - UN) // UN
    for start in range(0, head, UN):
        if before:
            before(start, UN)
        for i in range(UN):
            step(start + i, i)
    with engine.Fori(head // UN, loops) as k:
        m = UN * k
        if before:
            before(m, UN)
        for i in range(UN):
            step(m + i, i)
    for start in range(UN * loops, end, UN):
        count = min(UN, end - start)
        if before:
            before(start, count)
        for i in range(count):
            step(start + i, i)


def landed(b, i):
    return (b - i) * (16 // UN) + 16


def scattered(b, i):
    return (b - i) * (16 // UN)


def _constants():
    had = np.ones((1, 1), np.float32)
    while had.shape[0] < HD:
        had = np.block([[had, had], [had, -had]]).astype(np.float32)
    rows = np.arange(P)
    half, head, i = rows // (P // 2), rows // HALF % NH, rows % HALF
    hadp = np.ascontiguousarray(had[:, 2 * i + half])
    hmask = ((rows // HALF % HG)[:, None] == np.arange(HG)).astype(np.float32)
    smask = (rows[:, None] // M == np.arange(W) // (D + 1)).astype(np.float32)
    freqs = (np.float32(10000.0) ** (-np.arange(0, D, 2, dtype=np.float32) / np.float32(D))).astype(np.float32)
    ang = np.maximum(np.arange(L, dtype=np.float32) - 1, 0)[:, None] * freqs
    cos, sin = np.cos(ang), np.sin(ang)
    sint = np.stack([np.tile(-sin, (1, NH)), np.tile(sin, (1, NH))], axis=1)

    def tiles(a):
        return np.ascontiguousarray(a.reshape(NT, P, *a.shape[1:]).swapaxes(0, 1).astype(np.float32))

    return dict(had=had, hadp=hadp, hmask=hmask, smask=smask, cost=tiles(cos), sint=tiles(sint))


def kernel(L0_attn_x, L0_attn_w_qkv, L0_attn_w_out, L0_attn_sorf_signs, L0_attn_sorf_scales,
           L0_ffn_gate_w, L0_ffn_gate_b, L0_ffn_w1, L0_ffn_b1, L0_ffn_w2, L0_ffn_b2):
    import concourse.bacc as bacc
    from concourse.bass_utils import run_bass_kernel_spmd

    a = {k: np.asarray(v) for k, v in dict(
        x=L0_attn_x, qkv=L0_attn_w_qkv, wo=L0_attn_w_out, signs=L0_attn_sorf_signs,
        scales=L0_attn_sorf_scales, gate_w=L0_ffn_gate_w, gate_b=L0_ffn_gate_b, w1=L0_ffn_w1,
        b1=L0_ffn_b1, w2=L0_ffn_w2, b2=L0_ffn_b2).items()}
    qk = a["qkv"][:2 * E].reshape(2, NH, HALF, 2, E).transpose(4, 0, 3, 1, 2).reshape(E, 2 * E)
    signs = a["signs"][:, 0]
    arrays = dict(
        x=a["x"].reshape(N, E), wqk=qk, wv=a["qkv"][2 * E:].T, wo=a["wo"].T,
        sgn1=signs[:, 0, :D].reshape(NH, HALF, 2).transpose(2, 0, 1).reshape(1, P),
        sgn2=signs[:, 1].T, sgn3=signs[:, 2].T, scl=a["scales"][:, 0, :M].reshape(1, NH * M),
        gate_w=a["gate_w"].T, gate_b=a["gate_b"].reshape(1, NX), w1=a["w1"],
        b1=a["b1"], w2=a["w2"], b2=a["b2"], **_constants())
    nc = bacc.Bacc("TRN2", target_bir_lowering=False, num_devices=1)
    named = {f"in_{k}": np.ascontiguousarray(v) for k, v in arrays.items()}
    args = [nc.dram_tensor(k, v.shape, mybir.dt.from_np(v.dtype), kind="ExternalInput").ap()
            for k, v in named.items()]
    out = nc.dram_tensor("out", (N, E), F32, kind="ExternalOutput").ap()
    sandwich_kernel(nc, *args, out)
    got = run_bass_kernel_spmd(nc, [named], core_ids=[0])
    return got.results[0]["out"].reshape(NC, L, E)
```
